# Optimizing a Trainium2 kernel written in Bass

```python
import numpy as np
import jax
import jax.numpy as jnp

def _softmax(x, axis=-1):
    return jax.nn.softmax(x, axis=axis)

def _gelu(x):
    return jax.nn.gelu(x, approximate=True)

def _silu(x):
    return jax.nn.silu(x)

def _sigmoid(x):
    return jax.nn.sigmoid(x)

def _layernorm(x, axis=-1, eps=1e-05):
    m = jnp.mean(x, axis=axis, keepdims=True)
    v = jnp.var(x, axis=axis, keepdims=True)
    return (x - m) / jnp.sqrt(v + eps)

def _scatter_add(tgt, idx, src, axis=0):
    return tgt.at[idx].add(src)

def _segment_sum(src, seg, n):
    return jax.ops.segment_sum(src, seg, n)
kernel_name = 'mk_decoder_preln_d1_seqx_r8_d64293'

def setup_inputs(seed: int=0):
    np.random.seed(seed)
    _w = jnp.asarray

    def _rec_inputs():
        import jax
        import jax.numpy as jnp
        _rk = jax.random.key(seed)
        x = -0.0002928 + 1 * jax.random.normal(jax.random.fold_in(_rk, 1), (4, 512, 128), jnp.float32)
        _lenS = 512 - jax.random.randint(jax.random.fold_in(_rk, 7), (4,), 0, max(1, 512 // 4) + 1, jnp.int32)
        _lenS2 = 154 - jax.random.randint(jax.random.fold_in(_rk, 8), (4,), 0, max(1, 154 // 4) + 1, jnp.int32)
        _ctx_1024P = jax.random.normal(jax.random.fold_in(_rk, 11), (4, 16, 128), jnp.float32)
        _ctx_1024c = jax.random.dirichlet(jax.random.fold_in(_rk, 511), 0.3 * jnp.ones((16,), jnp.float32), (4, 154))
        _ctx_1024t = jnp.einsum('bsk,bkd->bsd', _ctx_1024c, _ctx_1024P)
        _ctx_1024t = _ctx_1024t * jax.lax.rsqrt(jnp.mean(jnp.square(_ctx_1024t)) + 1e-12) * 0.953939
        ctx_1024 = -1.39393e-06 + 0.999914 * (_ctx_1024t + 0.3 * jax.random.normal(jax.random.fold_in(_rk, 611), (4, 154, 128), jnp.float32))
        _validS = jnp.arange(512)[None, :] < _lenS[:, None]
        _validS2 = jnp.arange(154)[None, :] < _lenS2[:, None]
        _causal = jnp.tril(jnp.ones((512, 512), dtype=bool))
        mask_1x1xSxS2_if1 = jnp.where(jnp.ones((1, 1, 512, 154), dtype=bool), 1, 0).astype(jnp.int32)
        return (x, ctx_1024, mask_1x1xSxS2_if1)
    x, ctx_1024, mask_1x1xSxS2_if1 = _rec_inputs()

    def _L0_attn_setup():
        import jax, jax.numpy as jnp
        import numpy as np
        DECAY = 0.9
        key = jax.random.key(seed)
        ks = jax.random.split(key, 8)
        B, L, d_model = (4, 256, 128)
        d_state = 16
        d_inner = 2 * d_model
        x = jax.random.normal(ks[0], (B, L, d_model), dtype=jnp.float32)
        Win = jax.random.normal(ks[1], (d_model, d_inner), dtype=jnp.float32) / np.sqrt(d_model)
        bin_ = jnp.zeros((d_inner,), dtype=jnp.float32)
        Bp = jax.random.normal(ks[2], (d_inner, d_state), dtype=jnp.float32) * 0.01
        Cp = jax.random.normal(ks[3], (d_state, d_inner), dtype=jnp.float32) * 0.01
        Dp = jnp.ones((d_inner,), dtype=jnp.float32)
        Wout = jax.random.normal(ks[4], (d_inner, d_model), dtype=jnp.float32) / np.sqrt(d_inner)
        bout = jnp.zeros((d_model,), dtype=jnp.float32)
        return {'x': x, 'Win': Win, 'bin_': bin_, 'Bp': Bp, 'Cp': Cp, 'Dp': Dp, 'Wout': Wout, 'bout': bout}
    _L0_attn_all = _L0_attn_setup()
    _L0_attn_in = {k: v for k, v in _L0_attn_all.items() if k in ('Win', 'bin_', 'Bp', 'Cp', 'Dp', 'Wout', 'bout')}
    del _L0_attn_all

    def _L0_xattn_setup():
        import jax, jax.numpy as jnp
        import numpy as np
        D_MODEL = 128
        H = 16
        D_K = D_MODEL // H
        B, S = (2, 256)
        NEG = -1000000000.0

        def _split_heads(x):
            b, s, _ = x.shape
            return x.reshape(b, s, H, D_K).transpose(0, 2, 1, 3)
        key = jax.random.key(seed)
        ks = jax.random.split(key, 8)
        scale = 1.0 / np.sqrt(D_MODEL)
        return {'q': jax.random.normal(ks[0], (B, S, D_MODEL), jnp.float32), 'k': jax.random.normal(ks[1], (B, S, D_MODEL), jnp.float32), 'v': jax.random.normal(ks[2], (B, S, D_MODEL), jnp.float32), 'mask': jnp.ones((1, 1, S, S), jnp.int32), 'Wq': jax.random.normal(ks[3], (D_MODEL, D_MODEL), jnp.float32) * scale, 'bq': jnp.zeros((D_MODEL,), jnp.float32), 'Wk': jax.random.normal(ks[4], (D_MODEL, D_MODEL), jnp.float32) * scale, 'bk': jnp.zeros((D_MODEL,), jnp.float32), 'Wv': jax.random.normal(ks[5], (D_MODEL, D_MODEL), jnp.float32) * scale, 'bv': jnp.zeros((D_MODEL,), jnp.float32), 'Wo': jax.random.normal(ks[6], (D_MODEL, D_MODEL), jnp.float32) * scale, 'bo': jnp.zeros((D_MODEL,), jnp.float32)}
    _L0_xattn_all = _L0_xattn_setup()
    _L0_xattn_in = {k: v for k, v in _L0_xattn_all.items() if k in ('Wq', 'bq', 'Wk', 'bk', 'Wv', 'bv', 'Wo', 'bo')}
    del _L0_xattn_all

    def _L0_ffn_setup():
        import jax, jax.numpy as jnp
        import numpy as np
        B, T, D, E, FF, K = (4, 128, 128, 8, 256, 2)
        SINKHORN_ITERS = 3

        def _sinkhorn(log_alpha, iters=SINKHORN_ITERS):
            for _ in range(iters):
                log_alpha = log_alpha - jax.nn.logsumexp(log_alpha, axis=-1, keepdims=True)
                log_alpha = log_alpha - jax.nn.logsumexp(log_alpha, axis=-2, keepdims=True)
            gates = jnp.exp(log_alpha)
            return gates / (jnp.sum(gates, axis=-1, keepdims=True) + 1e-08)
        key = jax.random.key(seed)
        ks = jax.random.split(key, 7)
        scale = 0.02
        return {'x': jax.random.normal(ks[0], (B, T, D), dtype=jnp.float32), 'router_w': jax.random.normal(ks[1], (E, D), dtype=jnp.float32) * scale, 'router_b': jnp.zeros((E,), dtype=jnp.float32), 'temperature': jnp.ones((1,), dtype=jnp.float32) * 0.5, 'wg': jax.random.normal(ks[2], (E, D, FF), dtype=jnp.float32) * scale, 'wp': jax.random.normal(ks[3], (E, D, FF), dtype=jnp.float32) * scale, 'wo': jax.random.normal(ks[4], (E, FF, D), dtype=jnp.float32) * scale}
    _L0_ffn_all = _L0_ffn_setup()
    _L0_ffn_in = {k: v for k, v in _L0_ffn_all.items() if k in ('router_w', 'router_b', 'temperature', 'wg', 'wp', 'wo')}
    del _L0_ffn_all
    return {'x': x, 'ctx_1024': ctx_1024, 'mask_1x1xSxS2_if1': mask_1x1xSxS2_if1, 'L0_attn_Win': _L0_attn_in['Win'], 'L0_attn_bin_': _L0_attn_in['bin_'], 'L0_attn_Bp': _L0_attn_in['Bp'], 'L0_attn_Cp': _L0_attn_in['Cp'], 'L0_attn_Dp': _L0_attn_in['Dp'], 'L0_attn_Wout': _L0_attn_in['Wout'], 'L0_attn_bout': _L0_attn_in['bout'], 'L0_xattn_Wq': _L0_xattn_in['Wq'], 'L0_xattn_bq': _L0_xattn_in['bq'], 'L0_xattn_Wk': _L0_xattn_in['Wk'], 'L0_xattn_bk': _L0_xattn_in['bk'], 'L0_xattn_Wv': _L0_xattn_in['Wv'], 'L0_xattn_bv': _L0_xattn_in['bv'], 'L0_xattn_Wo': _L0_xattn_in['Wo'], 'L0_xattn_bo': _L0_xattn_in['bo'], 'L0_ffn_router_w': _L0_ffn_in['router_w'], 'L0_ffn_router_b': _L0_ffn_in['router_b'], 'L0_ffn_temperature': _L0_ffn_in['temperature'], 'L0_ffn_wg': _L0_ffn_in['wg'], 'L0_ffn_wp': _L0_ffn_in['wp'], 'L0_ffn_wo': _L0_ffn_in['wo']}

def reference(x, ctx_1024, mask_1x1xSxS2_if1, L0_attn_Win, L0_attn_bin_, L0_attn_Bp, L0_attn_Cp, L0_attn_Dp, L0_attn_Wout, L0_attn_bout, L0_xattn_Wq, L0_xattn_bq, L0_xattn_Wk, L0_xattn_bk, L0_xattn_Wv, L0_xattn_bv, L0_xattn_Wo, L0_xattn_bo, L0_ffn_router_w, L0_ffn_router_b, L0_ffn_temperature, L0_ffn_wg, L0_ffn_wp, L0_ffn_wo):
    import jax
    import jax.numpy as jnp

    def _L0_attn_ref(x, Win, bin_, Bp, Cp, Dp, Wout, bout):
        import jax, jax.numpy as jnp
        import numpy as np
        DECAY = 0.9
        B, L, _ = x.shape
        d_inner, d_state = Bp.shape
        xi = jax.nn.silu(x @ Win + bin_)
        xt_seq = jnp.swapaxes(xi, 0, 1)

        def step(h, xt):
            h = h * DECAY + xt[:, :, None] * Bp[None, :, :]
            y = jnp.einsum('bij,ji->bi', h, Cp) + Dp * xt
            return (h, y)
        h0 = jnp.zeros((B, d_inner, d_state), dtype=x.dtype)
        _, ys = jax.lax.scan(step, h0, xt_seq)
        y = jnp.swapaxes(ys, 0, 1)
        return y @ Wout + bout

    def _L0_xattn_ref(q, k, v, mask, Wq, bq, Wk, bk, Wv, bv, Wo, bo):
        import jax, jax.numpy as jnp
        import numpy as np
        D_MODEL = 128
        H = 16
        D_K = D_MODEL // H
        B, S = (2, 256)
        NEG = -1000000000.0

        def _split_heads(x):
            b, s, _ = x.shape
            return x.reshape(b, s, H, D_K).transpose(0, 2, 1, 3)
        query = _split_heads(q @ Wq.T + bq)
        key_ = _split_heads(k @ Wk.T + bk)
        value = _split_heads(v @ Wv.T + bv)
        scores = jnp.einsum('bhqd,bhkd->bhqk', query, key_) / jnp.sqrt(jnp.asarray(D_K, query.dtype))
        scores = jnp.where(mask == 0, jnp.asarray(NEG, scores.dtype), scores)
        attn = jax.nn.softmax(scores, axis=-1)
        ctx = jnp.einsum('bhqk,bhkd->bhqd', attn, value)
        ctx = ctx.transpose(0, 2, 1, 3).reshape(q.shape[0], -1, D_MODEL)
        return ctx @ Wo.T + bo

    def _L0_ffn_ref(x, router_w, router_b, temperature, wg, wp, wo):
        import jax, jax.numpy as jnp
        import numpy as np
        B, T, D, E, FF, K = (4, 128, 128, 8, 256, 2)
        SINKHORN_ITERS = 3

        def _sinkhorn(log_alpha, iters=SINKHORN_ITERS):
            for _ in range(iters):
                log_alpha = log_alpha - jax.nn.logsumexp(log_alpha, axis=-1, keepdims=True)
                log_alpha = log_alpha - jax.nn.logsumexp(log_alpha, axis=-2, keepdims=True)
            gates = jnp.exp(log_alpha)
            return gates / (jnp.sum(gates, axis=-1, keepdims=True) + 1e-08)
        temp = jnp.maximum(temperature, 0.1)
        scores = (jnp.einsum('btd,ed->bte', x, router_w) + router_b) / temp
        gates = _sinkhorn(scores)
        topk_vals, topk_idx = jax.lax.top_k(gates, K)
        topk_gates = topk_vals / (jnp.sum(topk_vals, axis=-1, keepdims=True) + 1e-08)
        g = jax.nn.relu(jnp.einsum('btd,edf->btef', x, wg))
        p = jnp.einsum('btd,edf->btef', x, wp)
        all_out = jnp.einsum('btef,efd->bted', g * p, wo)
        gathered = jnp.take_along_axis(all_out, topk_idx[..., None], axis=2)
        expert_out = jnp.sum(gathered * topk_gates[..., None], axis=2)
        return x + expert_out
    x = x + _L0_attn_ref(_layernorm(x, axis=-1), L0_attn_Win, L0_attn_bin_, L0_attn_Bp, L0_attn_Cp, L0_attn_Dp, L0_attn_Wout, L0_attn_bout)
    x = x + _L0_xattn_ref(_layernorm(x, axis=-1), ctx_1024, ctx_1024, mask_1x1xSxS2_if1, L0_xattn_Wq, L0_xattn_bq, L0_xattn_Wk, L0_xattn_bk, L0_xattn_Wv, L0_xattn_bv, L0_xattn_Wo, L0_xattn_bo)
    x = x + _L0_ffn_ref(_layernorm(x, axis=-1), L0_ffn_router_w, L0_ffn_router_b, L0_ffn_temperature, L0_ffn_wg, L0_ffn_wp, L0_ffn_wo)
    return x

_drawn_inputs = setup_inputs


def setup_inputs(seed=0):
    import zlib

    import numpy as np

    out = dict(_drawn_inputs(seed))
    spreads = {'L0_attn_bin_': (0.0, 0.1),
     'L0_attn_Dp': (1.0, 0.2),
     'L0_attn_bout': (0.0, 0.1),
     'L0_xattn_bq': (0.0, 0.41),
     'L0_xattn_bk': (0.0, 0.8),
     'L0_xattn_bv': (0.0, 0.1),
     'L0_xattn_bo': (0.0, 0.1),
     'L0_ffn_router_b': (0.0, 0.8)}
    factors = {'L0_attn_Bp': 8.0,
     'L0_attn_Cp': 8.0,
     'L0_ffn_router_w': 8.0,
     'L0_ffn_wg': 8.0,
     'L0_ffn_wp': 8.0,
     'L0_ffn_wo': 8.0}
    for name, (base, spread) in spreads.items():
        noise = np.random.default_rng([zlib.crc32(name.encode()), seed]).standard_normal(out[name].shape)
        drawn = base * np.exp(spread * noise) if base else spread * noise
        out[name] = jnp.asarray(drawn.astype(out[name].dtype))
    for name, factor in factors.items():
        out[name] = (out[name] * factor).astype(out[name].dtype)
    return out
```

```python
from contextlib import ExitStack

import concourse.bass as bass
from concourse import mybir

P = 128
F32 = mybir.dt.float32
F32R = mybir.dt.float32r
BF16 = mybir.dt.bfloat16
I32 = mybir.dt.int32
ALU = mybir.AluOpType
ACT = mybir.ActivationFunctionType
AX = mybir.AxisListType

LN_EPS = 1e-5
DECAY = 0.9
ROUTE_EPS = 1e-8
TEMP_MIN = 0.1
SINKHORN_ITERS = 3
MASKED = -float(2 ** 100)


def build_decoder(nc, x, ctx_seq, mask, Win, bin_, Bp, Cp, Dp, Wout, bout, Wq, bq, Wk, bk, Wv, bv,
                  Wo, bo, router_w, router_b, temperature, wg, wp, wo, out):
    NB, S, D = x.shape
    KEYS = ctx_seq.shape[1]
    INNER, STATE = Bp.shape
    E, _, FF = wg.shape
    H = 16
    DK = D // H
    T = S // P
    HI = INNER // P
    HF = FF // P
    K0 = P
    K1 = KEYS - K0
    Q = 32
    G = H // 4
    KPAD = K0 + Q
    PARTS = 3
    STACK = PARTS * PARTS * DK
    MROW = 96
    DEEP = MROW + PARTS
    VC = DK + 1
    QSCALE = float(DK) ** -0.5
    assert D == P and S == T * P and K1 <= Q and STACK <= MROW and H * DK == D

    with ExitStack() as ctx:
        def sb(name, shape, dt=F32):
            return ctx.enter_context(nc.sbuf_tensor(name, shape, dt))

        def sem(name):
            return ctx.enter_context(nc.semaphore(name))

        def bank(name):
            return ctx.enter_context(nc.psum_tensor(name, [P, 512], F32))

        ident = sb("ident", [P, P])
        ident_bf = sb("ident_bf", [P, P], BF16)
        decay = sb("decay", [P, S])
        win_raw = sb("win_raw", [P, INNER])
        win = [sb("win_hi", [P, INNER], F32R), sb("win_lo", [P, INNER], F32R)]
        wout_raw = sb("wout_raw", [P, HI, D])
        wscan_f = sb("wscan_f", [P, HI, D])
        wskip_f = sb("wskip_f", [P, HI, D])
        wscan = [sb("wscan_hi", [P, HI, D], F32R), sb("wscan_lo", [P, HI, D], F32R)]
        wskip = [sb("wskip_hi", [P, HI, D], F32R), sb("wskip_lo", [P, HI, D], F32R)]
        bp_sb = sb("bp_sb", [P, HI, STATE])
        cp_sb = sb("cp_sb", [STATE, INNER])
        bcprod = sb("bcprod", [P, HI, STATE])
        bc = sb("bc", [P, HI])
        dp_sb = sb("dp_sb", [P, HI])
        bin_sb = sb("bin_sb", [P, HI])
        nbin = sb("nbin", [P, HI])
        bout_sb = sb("bout_sb", [P, 1])
        proj_raw = sb("proj_raw", [P, 4, D])
        proj = [sb("proj_hi", [P, 4, D], F32R), sb("proj_lo", [P, 4, D], F32R)]
        bq_sb = sb("bq_sb", [P, 1])
        bk_sb = sb("bk_sb", [P, 1])
        bv_row = sb("bv_row", [P, D])
        bo_row = sb("bo_row", [P, D])
        rw_raw = sb("rw_raw", [E, D])
        rwT = sb("rwT", [P, E])
        rb_row = sb("rb_row", [P, E])
        temp_sb = sb("temp_sb", [P, 1])
        temp_c = sb("temp_c", [P, 1])
        rtemp = sb("rtemp", [P, 1])
        wgp_raw = sb("wgp_raw", [P, 2, E, FF])
        wgp = [sb("wgp_hi", [P, 2, E, FF], F32R), sb("wgp_lo", [P, 2, E, FF], F32R)]
        wo_sb = sb("wo_sb", [P, E, HF, D])
        mask_sb = sb("mask_sb", [P, T, KEYS], I32)
        mbias = sb("mbias", [P, T, KEYS], BF16)
        mbias_rem = sb("mbias_rem", [P, T, 4, Q], BF16)
        mbiasT = sb("mbiasT", [P, S], BF16)
        mbiasT_rem = sb("mbiasT_rem", [P, S], BF16)
        neghalf = sb("neghalf", [P, T])
        seg = sb("seg", [P, T * E])

        x_in = sb("x_in", [P, T, D])
        ctx_in = sb("ctx_in", [P, 2, D])
        stats = sb("stats", [P, T, 6])
        mv = sb("mv", [P, T, 2])
        veps = sb("veps", [P, T])
        rstd = sb("rstd", [P, T])
        xn = sb("xn", [P, T, D])
        act_in = [sb("act_hi", [P, S], F32R), sb("act_lo", [P, S], F32R)]
        cT = [sb("cT_hi", [P, KEYS], F32R), sb("cT_lo", [P, KEYS], F32R)]
        cR = [sb("cR_hi", [P, 4, Q], F32R), sb("cR_lo", [P, 4, Q], F32R)]
        k_f = sb("k_f", [P, KEYS])
        k_r = sb("k_r", [P, KEYS])
        k_parts = sb("k_parts", [P, PARTS, KEYS], BF16)
        v_main = sb("v_main", [P, H, VC])
        v_rem = sb("v_rem", [P, G, 4, VC])
        k_stack = sb("k_stack", [DEEP, H, KPAD], BF16)
        q_stack = sb("q_stack", [DEEP, H, S], BF16)
        eneg = sb("eneg", [P, HI, S])
        eplus = sb("eplus", [P, HI, S])
        sig = sb("sig", [P, HI, S])
        xi_f = sb("xi_f", [P, HI, S])
        xi = [sb("xi_hi", [P, HI, S], F32R), sb("xi_lo", [P, HI, S], F32R)]
        scan_s = sb("scan_s", [P, S])
        mixT = sb("mixT", [P, S])
        x1 = sb("x1", [P, T, D])
        x1b = sb("x1b", [P, T, D])
        q_f = sb("q_f", [P, S])
        q_r = sb("q_r", [P, S])
        q_parts = sb("q_parts", [P, PARTS, S], BF16)
        nmax = sb("nmax", [P, T, H])
        m_r = sb("m_r", [P, T, H])
        m_parts = sb("m_parts", [P, T, PARTS, H], BF16)
        mT = sb("mT", [PARTS * H, S], BF16)
        prob = sb("prob", [P, 4, S])
        rz = sb("rz", [P, T, H])
        cn = sb("cn", [P, T, D])
        x2 = sb("x2", [P, T, D])
        x3T = sb("x3T", [P, S])
        route = {n: sb("route_" + n, [P, T, E]) for n in
                 ("logit", "diff", "exp", "log", "gate", "norm", "over", "tie", "rank", "first", "pick", "w")}
        rcol = {n: sb("rcol_" + n, [P, T]) for n in ("max", "sum", "lse", "inv", "left", "kept", "kinv", "top")}
        top8 = sb("top8", [P, T, 8])
        elog = sb("elog", [E, S])
        eexp = sb("eexp", [E, S])
        ecol = {n: sb("ecol_" + n, [E, 1]) for n in ("nmax", "sum", "lse", "shift")}
        res_next = sb("res_next", [P, T, D])

        x3 = [sb("x3_hi", [P, S], F32R), sb("x3_lo", [P, S], F32R)]
        w_gate = sb("w_gate", [P, T, E])
        relu = sb("relu", [P, 2, S])
        hid = sb("hid", [P, 2, S])
        acc = sb("acc", [P, T, D])

        pT, pA, pB, pC0, pC1, pG, pU, pO = (bank(n) for n in ("pT", "pA", "pB", "pC0", "pC1", "pG", "pU", "pO"))
        pAB = [pA, pB]
        pC = [pC0, pC1]
        pT_bf = pT[:, :].bitcast(BF16)

        k_scr = nc.dram_tensor("k_scr", [P, PARTS, KEYS], BF16, kind="Internal").ap()
        q_scr = nc.dram_tensor("q_scr", [P, PARTS, S], BF16, kind="Internal").ap()

        s_ones = sem("ones_ready")
        s_passed = sem("wait_passed")
        (s_wsmall, s_wproj, s_wgp, s_wo, s_mask, s_zero, s_ident, s_identb, s_const,
         s_setupT, s_setup_hi, s_setup, s_bc, s_wsplit, s_xsplit, s_maskb, s_maskT, s_maskTc,
         s_nh) = (sem(n) for n in (
             "w_small_in", "w_proj_in", "w_gp_in", "w_o_in", "mask_in", "zeroed", "ident_ready",
             "ident_bf_ready", "const_ready", "setup_transposed", "setup_hi", "setup_vec", "bc_step",
             "w_split", "expert_split", "mask_bias", "mask_transposed", "mask_copied", "neghalf_ready"))
        (s_x, s_ctx, s_ctxT, s_chi, s_clo, s_kps, s_vps, s_ksplit, s_v, s_kscr, s_kst) = (
            sem(n) for n in ("x_in_ready", "ctx_in_ready", "ctx_transposed", "ctx_hi", "ctx_lo", "k_product",
                             "v_product", "k_split", "v_ready", "k_parts_in_dram", "k_stack_ready"))
        (s_stat, s_mv, s_veps, s_rstd, s_xn, s_tT, s_hi, s_lo) = (
            sem(n) for n in ("ln_stats", "ln_mean_var", "ln_var_eps", "ln_rstd", "ln_done", "act_transposed",
                             "act_hi_ready", "act_lo_ready"))
        (s_win, s_eneg, s_silu, s_xi, s_xihi, s_xilo, s_mix, s_scan, s_mixT, s_mixtr, s_x1, s_x1b) = (
            sem(n) for n in ("win_product", "exp_neg_ready", "silu_step", "xi_ready", "xi_hi", "xi_lo",
                             "mix_product", "scan_done", "mix_ready", "mix_transposed", "x1_ready", "x1_bias"))
        (s_qps, s_qsplit, s_qscr, s_qst, s_sa, s_red, s_msplit, s_mTp, s_mTc, s_mrow, s_sb, s_exp, s_pv,
         s_ctxz, s_rz, s_cn, s_yo, s_x2) = (
            sem(n) for n in ("q_product", "q_split", "q_parts_in_dram", "q_stack_ready", "scores_for_max",
                             "max_taken", "max_split", "max_transposed", "max_copied", "max_rows_ready",
                             "scores", "probs", "prob_used", "weighted_values", "z_inverse", "attn_normed",
                             "out_product", "x2_ready"))
        (s_x3T, s_res, s_rps, s_tm, s_tmexp, s_tmln, s_toE, s_em, s_emexp, s_emln, s_toT, s_gexp, s_route) = (
            sem(n) for n in ("x3T_ready", "residual_ready", "router_product", "expert_norm_step",
                             "expert_norm_exp", "expert_norm_log", "to_expert_rows", "token_norm_step",
                             "token_norm_exp", "token_norm_log", "to_token_rows", "gate_exp", "route_step"))
        (s_x3hi, s_x3lo, s_gw, s_gp, s_relu, s_up, s_hid, s_oute, s_acc, s_out) = (
            sem(n) for n in ("x3_hi", "x3_lo", "gate_weights", "gate_product", "relu_ready", "up_product",
                             "hidden_ready", "expert_out", "acc_step", "stored"))

        def after_first(b):
            return not (isinstance(b, int) and b == 0)

        def stand(eng, signal, value):
            eng.wait_ge(signal, value)
            eng.sem_inc(s_passed, 1)

        def f32(ap):
            return ap.bitcast(F32)

        def three_pass(eng, out_ap, lhs_hi, lhs_lo, rhs_hi, rhs_lo, start=True, stop=True):
            eng.matmul(out_ap, lhs_hi, rhs_hi, start=start, stop=False, skip_group_check=True)
            eng.matmul(out_ap, lhs_hi, rhs_lo, start=False, stop=False, skip_group_check=True)
            return eng.matmul(out_ap, lhs_lo, rhs_hi, start=False, stop=stop, skip_group_check=True)

        SA_UNITS = [(qt, hs) for qt in range(T) for hs in
                    ([0, 1, 2], [3, 4, 5], [6, 7, 8], [9, 10, 11], [12, 13], [14, 15])]
        NSA = len(SA_UNITS)
        SB_UNITS = [(g, j) for g in range(G) for j in (None, 0, 1, 2, 3)]
        NSB = len(SB_UNITS)
        NBUF = 4
        N_SMALL = 12
        TM_STEPS = 4
        EM_STEPS = 3
        ROUTE_STEPS = 14
        TM_PER = SINKHORN_ITERS * TM_STEPS + 1
        EM_PER = SINKHORN_ITERS * EM_STEPS

        block = ctx.enter_context(nc.Block())

        @block.sync
        def _(sp):
            sp.dma_start(cp_sb[:, :], Cp).then_inc(s_wsmall, 16)
            sp.dma_start(bp_sb[:, :, :], Bp.rearrange("(h p) n -> p h n", p=P)).then_inc(s_wsmall, 16)
            sp.dma_start(bin_sb[:, :], bin_.rearrange("(h p) -> p h", p=P),
                         allow_slow_non_contiguous=True).then_inc(s_wsmall, 16)
            sp.dma_start(dp_sb[:, :], Dp.rearrange("(h p) -> p h", p=P),
                         allow_slow_non_contiguous=True).then_inc(s_wsmall, 16)
            sp.dma_start(bout_sb[:, :], bout.rearrange("(p o) -> p o", o=1)).then_inc(s_wsmall, 16)
            sp.dma_start(bq_sb[:, :], bq.rearrange("(p o) -> p o", o=1)).then_inc(s_wsmall, 16)
            sp.dma_start(bk_sb[:, :], bk.rearrange("(p o) -> p o", o=1)).then_inc(s_wsmall, 16)
            sp.dma_start(rw_raw[:, :], router_w).then_inc(s_wsmall, 16)
            sp.dma_start(bv_row[:, :], bv.partition_broadcast(P)).then_inc(s_wsmall, 16)
            sp.dma_start(bo_row[:, :], bo.partition_broadcast(P)).then_inc(s_wsmall, 16)
            sp.dma_start(rb_row[:, :], router_b.partition_broadcast(P)).then_inc(s_wsmall, 16)
            sp.dma_start(temp_sb[:, :], temperature.partition_broadcast(P)).then_inc(s_wsmall, 16)
            sp.dma_start(win_raw[:, :], Win).then_inc(s_wproj, 16)
            sp.dma_start(wout_raw[:, :, :], Wout.rearrange("(h p) d -> p h d", p=P)).then_inc(s_wproj, 16)
            for n, w in enumerate((Wq, Wk, Wv, Wo)):
                sp.dma_start(proj_raw[:, n, :], w).then_inc(s_wproj, 16)
            sp.dma_start(mask_sb[:, :, :], mask.rearrange("a c (t p) k -> p (a c t) k", p=P)).then_inc(s_mask, 16)
            sp.dma_start(wgp_raw[:, 0, :, :], wg.rearrange("e d f -> d e f")).then_inc(s_wgp, 16)
            sp.dma_start(wgp_raw[:, 1, :, :], wp.rearrange("e d f -> d e f")).then_inc(s_wgp, 16)
            sp.dma_start(wo_sb[:, :, :, :], wo.rearrange("e (h p) d -> p e h d", p=P)).then_inc(s_wo, 16)

            def row_loads(b):
                if after_first(b):
                    sp.wait_ge(s_ctxT, b)
                sp.dma_start(ctx_in[:, 0, :], ctx_seq[bass.ds(b, 1), 0:K0, :].rearrange("o k d -> (o k) d")
                             ).then_inc(s_ctx, 16)
                sp.dma_start(ctx_in[0:K1, 1, :], ctx_seq[bass.ds(b, 1), K0:KEYS, :].rearrange("o k d -> (o k) d")
                             ).then_inc(s_ctx, 16)
                if after_first(b):
                    sp.wait_ge(s_x1, b)
                sp.dma_start(x_in[:, :, :], x[bass.ds(b, 1), :, :].rearrange("o (t p) d -> p (o t) d", p=P)
                             ).then_inc(s_x, 16)

            def stack_moves(b):
                if after_first(b):
                    sp.wait_ge(s_kst, 16 * PARTS * b)
                sp.wait_ge(s_ksplit, 5 * b + 5)
                sp.dma_start(k_scr, k_parts[:, :, :]).then_inc(s_kscr, 16)
                stand(sp, s_kscr, 16 * b + 16)
                if after_first(b):
                    sp.wait_ge(s_sb, NSB * b)
                for a in range(PARTS):
                    for p_ in range(PARTS):
                        r0 = (a * PARTS + p_) * DK
                        ins = sp.dma_start(k_stack[r0:r0 + DK, :, 0:KEYS],
                                     k_scr[:, p_, :].rearrange("(h d) n -> d h n", d=DK))
                        ins.then_inc(s_kst, 16)
                if after_first(b):
                    sp.wait_ge(s_qst, 16 * PARTS * PARTS * b)
                sp.wait_ge(s_qsplit, 5 * b + 5)
                sp.dma_start(q_scr, q_parts[:, :, :]).then_inc(s_qscr, 16)
                stand(sp, s_qscr, 16 * b + 16)
                for p_ in range(PARTS):
                    for a in range(PARTS):
                        r0 = (p_ * PARTS + a) * DK
                        sp.dma_start(q_stack[r0:r0 + DK, :, :],
                                     q_scr[:, p_, :].rearrange("(h d) n -> d h n", d=DK)).then_inc(s_qst, 16)
                sp.wait_ge(s_mTc, b + 1)
                for p_ in range(PARTS):
                    sp.dma_start(q_stack[MROW + p_:MROW + p_ + 1, :, :],
                                 mT[p_ * H:(p_ + 1) * H, :]).then_inc(s_mrow, 16)

            def row_store(b):
                sp.wait_ge(s_acc, T * E * (b + 1))
                sp.dma_start(out[bass.ds(b, 1), :, :].rearrange("o (t p) d -> p (o t) d", p=P), acc[:, :, :]
                             ).then_inc(s_out, 16)

            def body(b):
                row_loads(b)
                stack_moves(b)
                row_store(b)

            body(0)
            with sp.Fori(1, NB) as b:
                body(b)
            sp.wait_ge(s_out, 16 * NB)

        @block.gpsimd
        def _(pool):
            pool.memset(ident[:, :], 1.0).then_inc(s_ones, 1)
            pool.wait_ge(s_ones, 1)
            pool.affine_select(out=ident[:, :], in_=ident[:, :], compare_op=ALU.is_equal, fill=0.0, base=0,
                               pattern=[[-1, P]], channel_multiplier=1).then_inc(s_ident, 1)
            pool.memset(neghalf[:, :], -0.5).then_inc(s_nh, 1)
            pool.wait_ge(s_nh, 1)

            def ln_scale(n):
                stand(pool, s_mv, T * n + T)
                pool.tensor_scalar(veps[:, :], mv[:, :, 1], LN_EPS, None, ALU.add).then_inc(s_veps, 1)
                pool.wait_ge(s_veps, n + 1)
                pool.tensor_tensor(rstd[:, :], veps[:, :], neghalf[:, :], ALU.pow).then_inc(s_rstd, 1)

            def body(b):
                ln_scale(3 * b)
                for h in range(HI):
                    pool.wait_ge(s_xihi, HI * b + h + 1)
                    pool.tensor_tensor(xi[1][:, h, :], xi_f[:, h, :], f32(xi[0][:, h, :]), ALU.subtract
                                       ).then_inc(s_xilo, 1)
                ln_scale(3 * b + 1)
                pool.tensor_tensor(x1b[:, :, :], x1[:, :, :], bo_row[:, :].unsqueeze(1).broadcast_to([P, T, D]),
                                   ALU.add).then_inc(s_x1b, 1)
                ln_scale(3 * b + 2)
                pool.wait_ge(s_xn, 3 * T * (b + 1))
                if after_first(b):
                    pool.wait_ge(s_acc, T * E * b)
                pool.tensor_tensor(res_next[:, :, :], x2[:, :, :], xn[:, :, :], ALU.add).then_inc(s_res, 1)

            body(0)
            with pool.Fori(1, NB) as b:
                body(b)

        @block.scalar
        def _(act):
            act.wait_ge(s_ident, 1)
            act.copy(ident_bf[:, :], ident[:, :]).then_inc(s_identb, 1)
            act.wait_ge(s_wsmall, 16 * N_SMALL)
            act.mul(nbin[:, :], bin_sb[:, :], -1.0).then_inc(s_const, 1)
            act.wait_ge(s_setupT, 1)
            act.copy(rwT[:, :], pT[:, HI * STATE:HI * STATE + E]).then_inc(s_setup_hi, 1)
            act.wait_ge(s_setupT, 2)
            act.copy(proj[0][:, :, :], pG[:, :].rearrange("p (n d) -> p n d", n=4)).then_inc(s_setup_hi, 1)
            act.wait_ge(s_wproj, 16 * 6)
            act.copy(win[0][:, :], win_raw[:, :]).then_inc(s_setup_hi, 1)
            act.wait_ge(s_maskT, 1)
            act.copy(mbiasT[:, :], pT_bf[:, 0:S]).then_inc(s_maskTc, 1)
            act.wait_ge(s_maskT, 2)
            act.copy(mbiasT_rem[:, :], pT_bf[:, 0:S]).then_inc(s_maskTc, 1)
            act.wait_ge(s_wgp, 32)
            for n in range(2):
                act.copy(wgp[0][:, n, :, :], wgp_raw[:, n, :, :]).then_inc(s_xsplit, 1)

            def hi_of_transposed(b, k):
                act.wait_ge(s_tT, 3 * b + k + 1)
                act.copy(act_in[0][:, :], pT[:, :]).then_inc(s_hi, 1)

            def body(b):
                act.wait_ge(s_ctxT, b + 1)
                act.copy(cT[0][:, :], pT[:, 0:KEYS])
                act.copy(cR[0][:, :, 0:K1], pT[:, K0:KEYS].unsqueeze(1).broadcast_to([P, 4, K1])).then_inc(s_chi, 1)
                hi_of_transposed(b, 0)
                for h in range(HI):
                    act.wait_ge(s_win, HI * b + h + 1)
                    act.wait_ge(s_const, 1)
                    act.activation(eneg[:, h, :], pAB[h][:, :], ACT.Exp, bias=nbin[:, h:h + 1], scale=-1.0
                                   ).then_inc(s_eneg, 1)
                for h in range(HI):
                    act.wait_ge(s_xi, HI * b + h + 1)
                    act.copy(xi[0][:, h, :], xi_f[:, h, :]).then_inc(s_xihi, 1)
                hi_of_transposed(b, 1)
                act.wait_ge(s_mTp, b + 1)
                act.copy(mT[:, :], pT_bf[0:PARTS * H, 0:S]).then_inc(s_mTc, 1)
                for u in range(NSB):
                    act.wait_ge(s_sb, NSB * b + u + 1)
                    if u >= NBUF or after_first(b):
                        act.wait_ge(s_pv, NSB * b + u + 1 - NBUF)
                    act.activation(prob[:, u % NBUF, :], pAB[u % 2][:, :], ACT.Exp).then_inc(s_exp, 1)
                hi_of_transposed(b, 2)
                act.wait_ge(s_toT, (SINKHORN_ITERS + 1) * b + 1)
                act.copy(x3T[:, :], pT[:, :]).then_inc(s_x3T, 1)
                for it in range(SINKHORN_ITERS):
                    n = SINKHORN_ITERS * b + it
                    act.wait_ge(s_tm, TM_PER * b + TM_STEPS * it + 2 + 1)
                    act.activation(route["exp"][:, :, :], route["diff"][:, :, :], ACT.Exp).then_inc(s_tmexp, 1)
                    act.wait_ge(s_tm, TM_PER * b + TM_STEPS * it + 3 + 1)
                    act.activation(rcol["lse"][:, :], rcol["sum"][:, :], ACT.Ln).then_inc(s_tmln, 1)
                    act.wait_ge(s_em, EM_PER * b + EM_STEPS * it + 1)
                    act.activation(eexp[:, :], pA[0:E, :], ACT.Exp, bias=ecol["nmax"][:, :],
                                   accum_out=ecol["sum"][:, :]).then_inc(s_emexp, 1)
                    act.wait_ge(s_emexp, n + 1)
                    act.activation(ecol["lse"][:, :], ecol["sum"][:, :], ACT.Ln).then_inc(s_emln, 1)
                act.wait_ge(s_toT, (SINKHORN_ITERS + 1) * (b + 1))
                act.activation(route["gate"][:, :, :], pT[:, 0:T * E].rearrange("p (t e) -> p t e", t=T), ACT.Exp
                               ).then_inc(s_gexp, 1)
                act.copy(x3[0][:, :], x3T[:, :]).then_inc(s_x3hi, 1)
                for i in range(E * HF):
                    act.wait_ge(s_gp, E * HF * b + i + 1)
                    if i >= 2 or after_first(b):
                        act.wait_ge(s_hid, E * HF * b + i - 1)
                    act.activation(relu[:, i % 2, :], pG[:, :], ACT.Relu).then_inc(s_relu, 1)

            body(0)
            with act.Fori(1, NB) as b:
                body(b)

        @block.vector
        def _(dve):
            dve.memset(decay[:, :], DECAY)
            dve.memset(seg[:, :], 1.0)
            dve.memset(k_stack[:, :, :], 0.0)
            dve.memset(q_stack[:, :, :], 0.0)
            dve.memset(v_rem[:, :, :, :], 0.0)
            dve.memset(f32(cR[0][:, :, :]), 0.0)
            dve.memset(f32(cR[1][:, :, :]), 0.0)
            dve.memset(mbias_rem[:, :, :, :], 0.0).then_inc(s_zero, 1)
            dve.wait_ge(s_zero, 1)
            dve.memset(seg[:, :].rearrange("p (t e) -> p t e", t=T)[:, :, 0:1], 0.0)
            dve.memset(k_stack[MROW:DEEP, :, 0:KEYS], 1.0)
            dve.memset(v_main[:, :, DK:VC], 1.0)
            for j in range(4):
                last = dve.memset(v_rem[Q * j:Q * j + K1, :, j, DK:VC], 1.0)
            last.then_inc(s_zero, 1)
            dve.wait_ge(s_mask, 16)
            dve.tensor_scalar(mbias[:, :, :], mask_sb[:, :, :], 0.0, MASKED, ALU.is_equal, ALU.mult)
            for j in range(4):
                last = dve.tensor_scalar(mbias_rem[:, :, j, 0:K1], mask_sb[:, :, K0:KEYS], 0.0, MASKED,
                                         ALU.is_equal, ALU.mult)
            last.then_inc(s_maskb, 1)
            dve.wait_ge(s_setupT, 1)
            dve.wait_ge(s_setup_hi, 1)
            dve.wait_ge(s_wsmall, 16 * N_SMALL)
            dve.tensor_tensor(bcprod[:, :, :], bp_sb[:, :, :],
                              pT[:, 0:HI * STATE].rearrange("p (h n) -> p h n", h=HI), ALU.mult).then_inc(s_bc, 1)
            dve.wait_ge(s_bc, 1)
            dve.tensor_reduce(bc[:, :], bcprod[:, :, :], AX.X, ALU.add)
            dve.tensor_scalar(temp_c[:, :], temp_sb[:, :], TEMP_MIN, None, ALU.max).then_inc(s_bc, 1)
            dve.wait_ge(s_bc, 2)
            dve.reciprocal(rtemp[:, :], temp_c[:, :])
            dve.wait_ge(s_wproj, 16 * 6)
            for h in range(HI):
                dve.tensor_scalar(wscan_f[:, h, :], wout_raw[:, h, :], bc[:, h:h + 1], None, ALU.mult)
                dve.tensor_scalar(wskip_f[:, h, :], wout_raw[:, h, :], dp_sb[:, h:h + 1], None,
                                  ALU.mult).then_inc(s_bc, 1)
            dve.wait_ge(s_bc, 4)
            dve.tensor_copy(wscan[0][:, :, :], wscan_f[:, :, :])
            dve.tensor_copy(wskip[0][:, :, :], wskip_f[:, :, :]).then_inc(s_bc, 1)
            dve.wait_ge(s_bc, 5)
            dve.tensor_tensor(wscan[1][:, :, :], wscan_f[:, :, :], f32(wscan[0][:, :, :]), ALU.subtract)
            dve.tensor_tensor(wskip[1][:, :, :], wskip_f[:, :, :], f32(wskip[0][:, :, :]), ALU.subtract)
            dve.wait_ge(s_setup_hi, 3)
            dve.tensor_tensor(proj[1][:, :, :], pG[:, :].rearrange("p (n d) -> p n d", n=4),
                              f32(proj[0][:, :, :]), ALU.subtract)
            dve.tensor_tensor(win[1][:, :], win_raw[:, :], f32(win[0][:, :]), ALU.subtract).then_inc(s_setup, 1)
            for n in range(2):
                dve.wait_ge(s_xsplit, n + 1)
                last = dve.tensor_tensor(wgp[1][:, n, :, :], wgp_raw[:, n, :, :], f32(wgp[0][:, n, :, :]),
                                         ALU.subtract)
            last.then_inc(s_wsplit, 1)

            def layer_norm(n, src):
                for t in range(T):
                    dve.bn_stats(stats[:, t, :], src[:, t, :]).then_inc(s_stat, 1)
                for t in range(T):
                    stand(dve, s_stat, T * n + t + 1)
                    dve.bn_aggr(mv[:, t, :], stats[:, t, :]).then_inc(s_mv, 1)
                dve.wait_ge(s_mv, T * n + T)
                dve.wait_ge(s_rstd, n + 1)
                for t in range(T):
                    dve.tensor_scalar(xn[:, t, :], src[:, t, :], mv[:, t, 0:1], rstd[:, t:t + 1],
                                      ALU.subtract, ALU.mult).then_inc(s_xn, 1)

            def lo_of_transposed(b, k):
                dve.wait_ge(s_hi, 3 * b + k + 1)
                dve.tensor_tensor(act_in[1][:, :], pT[:, :], f32(act_in[0][:, :]), ALU.subtract).then_inc(s_lo, 1)

            def split3(src, rest, parts, done, at):
                dve.wait_ge(done, at)
                dve.tensor_copy(parts(0), src).then_inc(done, 1)
                dve.wait_ge(done, at + 1)
                dve.tensor_tensor(rest, src, parts(0), ALU.subtract).then_inc(done, 1)
                dve.wait_ge(done, at + 2)
                dve.tensor_copy(parts(1), rest).then_inc(done, 1)
                dve.wait_ge(done, at + 3)
                dve.tensor_tensor(parts(2), rest, parts(1), ALU.subtract).then_inc(done, 1)

            def body(b):
                dve.wait_ge(s_chi, b + 1)
                dve.tensor_tensor(cT[1][:, :], pT[:, 0:KEYS], f32(cT[0][:, :]), ALU.subtract)
                dve.tensor_tensor(cR[1][:, :, 0:K1], pT[:, K0:KEYS].unsqueeze(1).broadcast_to([P, 4, K1]),
                                  f32(cR[0][:, :, 0:K1]), ALU.subtract).then_inc(s_clo, 1)
                dve.wait_ge(s_kps, b + 1)
                if after_first(b):
                    dve.wait_ge(s_kscr, 16 * b)
                dve.tensor_scalar(k_f[:, :], pA[:, 0:KEYS], bk_sb[:, 0:1], None, ALU.add).then_inc(s_ksplit, 1)
                split3(k_f[:, :], k_r[:, :], lambda a: k_parts[:, a, :], s_ksplit, 5 * b + 1)
                dve.wait_ge(s_vps, b + 1)
                dve.tensor_tensor(v_main[:, :, 0:DK], pB[:, 0:D].rearrange("p (h d) -> p h d", d=DK),
                                  bv_row[:, :].rearrange("p (h d) -> p h d", d=DK), ALU.add)
                for j in range(4):
                    rows = slice(Q * j, Q * j + K1)
                    last = dve.tensor_tensor(
                        v_rem[rows, :, j, 0:DK],
                        pB[rows, D:2 * D].rearrange("p (g j d) -> p g j d", g=G, j=4)[:, :, j, :],
                        bv_row[rows, :].rearrange("p (g j d) -> p g j d", g=G, j=4)[:, :, j, :], ALU.add)
                last.then_inc(s_v, 1)
                dve.wait_ge(s_x, 16 * b + 16)
                layer_norm(3 * b, x_in)
                lo_of_transposed(b, 0)
                for h in range(HI):
                    n = 2 * (HI * b + h)
                    dve.wait_ge(s_eneg, HI * b + h + 1)
                    dve.tensor_scalar(eplus[:, h, :], eneg[:, h, :], 1.0, None, ALU.add).then_inc(s_silu, 1)
                    dve.wait_ge(s_silu, n + 1)
                    dve.reciprocal(sig[:, h, :], eplus[:, h, :]).then_inc(s_silu, 1)
                    dve.wait_ge(s_silu, n + 2)
                    dve.scalar_tensor_tensor(out=xi_f[:, h, :], in0=pAB[h][:, :], scalar=bin_sb[:, h:h + 1],
                                             in1=sig[:, h, :], op0=ALU.add, op1=ALU.mult).then_inc(s_xi, 1)
                dve.wait_ge(s_mix, 2 * b + 1)
                dve.tensor_tensor_scan(scan_s[:, :], decay[:, :], pA[:, :], 0.0, ALU.mult, ALU.add).then_inc(s_scan, 1)
                dve.wait_ge(s_scan, b + 1)
                dve.wait_ge(s_mix, 2 * b + 2)
                dve.scalar_tensor_tensor(out=mixT[:, :], in0=scan_s[:, :], scalar=bout_sb[:, 0:1], in1=pB[:, :],
                                         op0=ALU.add, op1=ALU.add).then_inc(s_mixT, 1)
                dve.wait_ge(s_mixtr, b + 1)
                dve.tensor_tensor(x1[:, :, :], x_in[:, :, :], pT[:, :].rearrange("p (t d) -> p t d", t=T), ALU.add
                                  ).then_inc(s_x1, 1)
                dve.wait_ge(s_x1, b + 1)
                layer_norm(3 * b + 1, x1)
                lo_of_transposed(b, 1)
                dve.wait_ge(s_qps, b + 1)
                if after_first(b):
                    dve.wait_ge(s_qscr, 16 * b)
                dve.tensor_scalar(q_f[:, :], pA[:, :], bq_sb[:, 0:1], QSCALE, ALU.add, ALU.mult).then_inc(s_qsplit, 1)
                split3(q_f[:, :], q_r[:, :], lambda a: q_parts[:, a, :], s_qsplit, 5 * b + 1)
                for u, (qt, hs) in enumerate(SA_UNITS):
                    dve.wait_ge(s_sa, NSA * b + u + 1)
                    dve.tensor_reduce(nmax[:, qt, hs[0]:hs[-1] + 1],
                                      pAB[u % 2][:, 0:len(hs) * KEYS].rearrange("p (h k) -> p h k", k=KEYS),
                                      AX.X, ALU.max, negate=True).then_inc(s_red, 1)
                dve.wait_ge(s_red, NSA * b + NSA)
                dve.tensor_copy(m_parts[:, :, 0, :], nmax[:, :, :]).then_inc(s_msplit, 1)
                dve.wait_ge(s_msplit, 4 * b + 1)
                dve.tensor_tensor(m_r[:, :, :], nmax[:, :, :], m_parts[:, :, 0, :], ALU.subtract).then_inc(s_msplit, 1)
                dve.wait_ge(s_msplit, 4 * b + 2)
                dve.tensor_copy(m_parts[:, :, 1, :], m_r[:, :, :]).then_inc(s_msplit, 1)
                dve.wait_ge(s_msplit, 4 * b + 3)
                dve.tensor_tensor(m_parts[:, :, 2, :], m_r[:, :, :], m_parts[:, :, 1, :], ALU.subtract
                                  ).then_inc(s_msplit, 1)
                dve.wait_ge(s_ctxz, b + 1)
                for c in range(2):
                    cols = pC[c][:, :].rearrange("p (t c) -> p t c", t=2)[:, :, 0:H * VC].rearrange(
                        "p t (h v) -> p t h v", v=VC)
                    dve.reciprocal(rz[:, 2 * c:2 * c + 2, :], cols[:, :, :, DK]).then_inc(s_rz, 1)
                for t in range(T):
                    cols = pC[t // 2][:, 256 * (t % 2):256 * (t % 2) + H * VC].rearrange("p (h v) -> p h v", v=VC)
                    dve.wait_ge(s_rz, 2 * b + t // 2 + 1)
                    dve.tensor_tensor(cn[:, t, :].rearrange("p (h d) -> p h d", d=DK), cols[:, :, 0:DK],
                                      rz[:, t, :].unsqueeze(2).broadcast_to([P, H, DK]), ALU.mult).then_inc(s_cn, 1)
                lo_of_transposed(b, 2)
                dve.wait_ge(s_yo, b + 1)
                dve.wait_ge(s_x1b, b + 1)
                dve.tensor_tensor(x2[:, :, :], x1b[:, :, :], pA[:, :].rearrange("p (t d) -> p t d", t=T), ALU.add
                                  ).then_inc(s_x2, 1)
                dve.wait_ge(s_x2, b + 1)
                layer_norm(3 * b + 2, x2)
                dve.wait_ge(s_rps, b + 1)
                dve.tensor_tensor(route["logit"][:, :, :], pB[:, 0:T * E].rearrange("p (t e) -> p t e", t=T),
                                  rb_row[:, :].unsqueeze(1).broadcast_to([P, T, E]), ALU.add).then_inc(s_tm, 1)
                dve.wait_ge(s_tm, TM_PER * b + 1)
                for it in range(SINKHORN_ITERS):
                    at = TM_PER * b + TM_STEPS * it + 1
                    if it == 0:
                        src = route["norm"][:, :, :]
                        dve.tensor_scalar(src, route["logit"][:, :, :], rtemp[:, 0:1], None, ALU.mult
                                          ).then_inc(s_route, 1)
                        dve.wait_ge(s_route, ROUTE_STEPS * b + 1)
                    else:
                        src = pT[:, 0:T * E].rearrange("p (t e) -> p t e", t=T)
                        dve.wait_ge(s_toT, (SINKHORN_ITERS + 1) * b + it + 1)
                    dve.tensor_reduce(rcol["max"][:, :], src, AX.X, ALU.max).then_inc(s_tm, 1)
                    dve.wait_ge(s_tm, at + 1)
                    dve.tensor_tensor(route["diff"][:, :, :], src,
                                      rcol["max"][:, :].unsqueeze(2).broadcast_to([P, T, E]), ALU.subtract
                                      ).then_inc(s_tm, 1)
                    dve.wait_ge(s_tmexp, SINKHORN_ITERS * b + it + 1)
                    dve.tensor_reduce(rcol["sum"][:, :], route["exp"][:, :, :], AX.X, ALU.add).then_inc(s_tm, 1)
                    dve.wait_ge(s_tmln, SINKHORN_ITERS * b + it + 1)
                    dve.tensor_tensor(route["log"][:, :, :], route["diff"][:, :, :],
                                      rcol["lse"][:, :].unsqueeze(2).broadcast_to([P, T, E]), ALU.subtract
                                      ).then_inc(s_tm, 1)
                    em = EM_PER * b + EM_STEPS * it
                    dve.wait_ge(s_toE, SINKHORN_ITERS * b + it + 1)
                    dve.tensor_reduce(ecol["nmax"][:, :], pA[0:E, :], AX.X, ALU.max, negate=True).then_inc(s_em, 1)
                    dve.wait_ge(s_em, em + 1)
                    dve.wait_ge(s_emln, SINKHORN_ITERS * b + it + 1)
                    dve.tensor_tensor(ecol["shift"][:, :], ecol["nmax"][:, :], ecol["lse"][:, :], ALU.subtract
                                      ).then_inc(s_em, 1)
                    dve.wait_ge(s_em, em + 2)
                    dve.tensor_scalar(elog[:, :], pA[0:E, :], ecol["shift"][:, 0:1], None, ALU.add).then_inc(s_em, 1)
                r0 = ROUTE_STEPS * b

                def step(n, ins):
                    ins.then_inc(s_route, 1)
                    stand(dve, s_route, r0 + n)

                def wide(col):
                    return col.unsqueeze(2).broadcast_to([P, T, E])

                dve.wait_ge(s_gexp, b + 1)
                step(2, dve.tensor_reduce(rcol["sum"][:, :], route["gate"][:, :, :], AX.X, ALU.add))
                step(3, dve.tensor_scalar(rcol["sum"][:, :], rcol["sum"][:, :], ROUTE_EPS, None, ALU.add))
                step(4, dve.reciprocal(rcol["inv"][:, :], rcol["sum"][:, :]))
                step(5, dve.tensor_tensor(route["norm"][:, :, :], route["gate"][:, :, :], wide(rcol["inv"][:, :]),
                                          ALU.mult))
                for t in range(T):
                    last = dve.max(top8[:, t, :], route["norm"][:, t, :])
                step(6, last)
                dve.tensor_tensor(route["over"][:, :, :], route["norm"][:, :, :],
                                  top8[:, :, 1:2].broadcast_to([P, T, E]), ALU.is_gt)
                dve.tensor_tensor(rcol["kept"][:, :], top8[:, :, 0], top8[:, :, 1], ALU.add)
                step(7, dve.tensor_tensor(route["tie"][:, :, :], route["norm"][:, :, :],
                                          top8[:, :, 1:2].broadcast_to([P, T, E]), ALU.is_equal))
                dve.tensor_reduce(rcol["left"][:, :], route["over"][:, :, :], AX.X, ALU.add)
                dve.tensor_scalar(rcol["top"][:, :], rcol["kept"][:, :], ROUTE_EPS, None, ALU.add)
                step(8, dve.tensor_tensor_scan(route["rank"][:, :, :].rearrange("p t e -> p (t e)"), seg[:, :],
                                               route["tie"][:, :, :].rearrange("p t e -> p (t e)"), 0.0,
                                               ALU.mult, ALU.add))
                dve.reciprocal(rcol["kinv"][:, :], rcol["top"][:, :])
                step(9, dve.tensor_tensor(route["first"][:, :, :], route["rank"][:, :, :], wide(rcol["left"][:, :]),
                                          ALU.add))
                step(10, dve.scalar_tensor_tensor(out=route["pick"][:, :, :].rearrange("p t e -> p (t e)"),
                                                  in0=route["first"][:, :, :].rearrange("p t e -> p (t e)"),
                                                  scalar=2.0,
                                                  in1=route["tie"][:, :, :].rearrange("p t e -> p (t e)"),
                                                  op0=ALU.is_le, op1=ALU.mult))
                step(11, dve.tensor_tensor(route["pick"][:, :, :], route["pick"][:, :, :], route["over"][:, :, :],
                                           ALU.add))
                step(12, dve.tensor_tensor(route["w"][:, :, :], route["pick"][:, :, :], route["norm"][:, :, :],
                                           ALU.mult))
                step(13, dve.tensor_tensor(w_gate[:, :, :], route["w"][:, :, :], wide(rcol["kinv"][:, :]), ALU.mult))
                dve.wait_ge(s_x3hi, b + 1)
                dve.wait_ge(s_x3T, b + 1)
                step(14, dve.tensor_tensor(x3[1][:, :], x3T[:, :], f32(x3[0][:, :]), ALU.subtract))

            def experts(b):
                for i in range(E * HF):
                    e = i // HF
                    n = E * HF * b + i
                    dve.wait_ge(s_relu, n + 1)
                    dve.wait_ge(s_up, n + 1)
                    dve.tensor_tensor(hid[:, i % 2, :], relu[:, i % 2, :], pU[:, :], ALU.mult).then_inc(s_hid, 1)
                    if i % HF == HF - 1:
                        dve.wait_ge(s_oute, E * b + e + 1)
                        if e == 0:
                            dve.wait_ge(s_res, b + 1)
                            if after_first(b):
                                dve.wait_ge(s_out, 16 * b)
                        else:
                            dve.wait_ge(s_acc, T * (E * b + e))
                        base = res_next if e == 0 else acc
                        for t in range(T):
                            dve.scalar_tensor_tensor(out=acc[:, t, :], in0=pO[:, t * D:(t + 1) * D],
                                                     scalar=w_gate[:, t, e:e + 1], in1=base[:, t, :],
                                                     op0=ALU.mult, op1=ALU.add).then_inc(s_acc, 1)

            def row(b):
                body(b)
                experts(b)

            row(0)
            with dve.Fori(1, NB) as b:
                row(b)

        @block.tensor
        def _(pe):
            pe.wait_ge(s_ident, 1)
            pe.wait_ge(s_wsmall, 16 * N_SMALL)
            for h in range(HI):
                pe.transpose(pT[:, h * STATE:(h + 1) * STATE], cp_sb[:, h * P:(h + 1) * P], ident[0:STATE, 0:STATE])
            pe.transpose(pT[:, HI * STATE:HI * STATE + E], rw_raw[:, :], ident[0:E, 0:E]).then_inc(s_setupT, 1)
            pe.wait_ge(s_wproj, 16 * 6)
            for n in range(4):
                last = pe.transpose(pG[:, n * D:(n + 1) * D], proj_raw[:, n, :], ident[:, :])
            last.then_inc(s_setupT, 1)
            pe.wait_ge(s_identb, 1)
            pe.wait_ge(s_maskb, 1)
            pe.wait_ge(s_setup_hi, 1)
            pe.wait_ge(s_bc, 1)
            for t in range(T):
                last = pe.transpose(pT_bf[:, t * P:(t + 1) * P], mbias[:, t, 0:K0], ident_bf[:, :])
            last.then_inc(s_maskT, 1)
            pe.wait_ge(s_maskTc, 1)
            for t in range(T):
                last = pe.transpose(pT_bf[:, t * P:(t + 1) * P],
                                    mbias_rem[:, t, :, :].rearrange("p j k -> p (j k)"), ident_bf[:, :])
            last.then_inc(s_maskT, 1)
            pe.wait_ge(s_maskTc, 2)
            pe.wait_ge(s_setup, 1)
            pe.wait_ge(s_zero, 2)

            def transposes(src):
                for t in range(T):
                    last = pe.transpose(pT[:, t * P:(t + 1) * P], src[:, t, :], ident[:, :])
                return last

            def body(b):
                pe.wait_ge(s_ctx, 32 * b + 32)
                if after_first(b):
                    pe.wait_ge(s_gexp, b)
                pe.transpose(pT[:, 0:K0], ctx_in[:, 0, :], ident[:, :])
                pe.transpose(pT[:, K0:KEYS], ctx_in[0:K1, 1, :], ident[0:K1, 0:K1]).then_inc(s_ctxT, 1)
                pe.wait_ge(s_chi, b + 1)
                pe.wait_ge(s_clo, b + 1)
                if after_first(b):
                    pe.wait_ge(s_em, EM_PER * b)
                three_pass(pe, pA[:, 0:KEYS], proj[0][:, 1, :], proj[1][:, 1, :], cT[0][:, :], cT[1][:, :]
                           ).then_inc(s_kps, 1)
                three_pass(pe, pB[:, 0:D], cT[0][:, 0:K0], cT[1][:, 0:K0], proj[0][:, 2, :], proj[1][:, 2, :])
                flat = [c[:, :, :].rearrange("p j k -> p (j k)") for c in cR]
                three_pass(pe, pB[:, D:2 * D], flat[0], flat[1], proj[0][:, 2, :], proj[1][:, 2, :],
                           start=False).then_inc(s_vps, 1)
                pe.wait_ge(s_xn, T * (3 * b) + T)
                transposes(xn).then_inc(s_tT, 1)
                pe.wait_ge(s_hi, 3 * b + 1)
                pe.wait_ge(s_lo, 3 * b + 1)
                pe.wait_ge(s_ksplit, 5 * b + 1)
                pe.wait_ge(s_v, b + 1)
                for h in range(HI):
                    cols = slice(h * P, (h + 1) * P)
                    three_pass(pe, pAB[h][:, :], win[0][:, cols], win[1][:, cols], act_in[0][:, :], act_in[1][:, :]
                               ).then_inc(s_win, 1)
                for w, dst in ((wscan, pA), (wskip, pB)):
                    for h in range(HI):
                        pe.wait_ge(s_xihi, HI * b + HI)
                        pe.wait_ge(s_xilo, HI * b + h + 1)
                        last = three_pass(pe, dst[:, :], w[0][:, h, :], w[1][:, h, :], xi[0][:, h, :], xi[1][:, h, :],
                                          start=(h == 0), stop=(h == HI - 1))
                    last.then_inc(s_mix, 1)
                pe.wait_ge(s_mixT, b + 1)
                for t in range(T):
                    last = pe.transpose(pT[:, t * P:(t + 1) * P], mixT[:, t * P:(t + 1) * P], ident[:, :])
                last.then_inc(s_mixtr, 1)
                pe.wait_ge(s_xn, T * (3 * b + 1) + T)
                transposes(xn).then_inc(s_tT, 1)
                pe.wait_ge(s_hi, 3 * b + 2)
                pe.wait_ge(s_lo, 3 * b + 2)
                three_pass(pe, pA[:, :], proj[0][:, 0, :], proj[1][:, 0, :], act_in[0][:, :], act_in[1][:, :]
                           ).then_inc(s_qps, 1)
                pe.wait_ge(s_kst, 16 * PARTS * PARTS * (b + 1))
                pe.wait_ge(s_qst, 16 * PARTS * PARTS * (b + 1))
                for u, (qt, hs) in enumerate(SA_UNITS):
                    if u >= 2:
                        pe.wait_ge(s_red, NSA * b + u - 1)
                    elif u == 0:
                        pe.wait_ge(s_qsplit, 5 * b + 1)
                    dst = pAB[u % 2]
                    for n, h in enumerate(hs):
                        pe.matmul(dst[:, n * KEYS:(n + 1) * KEYS], q_stack[0:STACK, h, qt * P:(qt + 1) * P],
                                  k_stack[0:STACK, h, 0:KEYS], start=(n == 0), stop=False, skip_group_check=True)
                    pe.matmul(dst[:, 0:len(hs) * KEYS].rearrange("p (h k) -> p h k", k=KEYS), ident_bf[:, :],
                              mbias[:, qt, :].unsqueeze(1).broadcast_to([P, len(hs), KEYS]),
                              start=False, stop=True, skip_group_check=True).then_inc(s_sa, 1)
                stand(pe, s_msplit, 4 * b + 4)
                for t in range(T):
                    last = pe.transpose(pT_bf[0:PARTS * H, t * P:(t + 1) * P],
                                        m_parts[:, t, :, :].rearrange("p a h -> p (a h)"), ident_bf[:, :])
                last.then_inc(s_mTp, 1)
                pe.wait_ge(s_mrow, 16 * PARTS * (b + 1))

                def scores(u):
                    g, j = SB_UNITS[u]
                    dst = pAB[u % 2]
                    if u >= 2:
                        pe.wait_ge(s_exp, NSB * b + u - 1)
                    else:
                        pe.wait_ge(s_red, NSA * b + NSA)
                    if j is None:
                        for c in range(4):
                            pe.matmul(dst[Q * c:Q * (c + 1), :], k_stack[:, 4 * g + c, K0:KPAD],
                                      q_stack[:, 4 * g + c, :], start=True, stop=False, skip_group_check=True)
                        bias = mbiasT_rem
                    else:
                        pe.matmul(dst[:, :], k_stack[:, 4 * g + j, 0:K0], q_stack[:, 4 * g + j, :],
                                  start=True, stop=False, skip_group_check=True)
                        bias = mbiasT
                    pe.matmul(dst[:, :], ident_bf[:, :], bias[:, :], start=False, stop=True, skip_group_check=True
                              ).then_inc(s_sb, 1)

                def weigh(u):
                    g, j = SB_UNITS[u]
                    pe.wait_ge(s_exp, NSB * b + u + 1)
                    for t in range(T):
                        c0 = 256 * (t % 2)
                        if j is None:
                            cols = slice(c0 + 4 * g * VC, c0 + 4 * (g + 1) * VC)
                            vals = v_rem[:, g, :, :].rearrange("p j v -> p (j v)")
                        else:
                            h = 4 * g + j
                            cols = slice(c0 + h * VC, c0 + (h + 1) * VC)
                            vals = v_main[:, h, :]
                        last = pe.matmul(pC[t // 2][:, cols], prob[:, u % NBUF, t * P:(t + 1) * P], vals,
                                         start=(u == 0 and t % 2 == 0), stop=(u == NSB - 1), skip_group_check=True)
                    last.then_inc(s_pv, 1)
                    return last

                if after_first(b):
                    pe.wait_ge(s_cn, T * b)
                scores(0)
                for u in range(NSB):
                    if u + 1 < NSB:
                        scores(u + 1)
                    weigh(u)
                pe.matmul(pC[1][0:1, 510:512], ident[0:1, 0:1], ident[0:1, 0:2], start=False, stop=True,
                          skip_group_check=True).then_inc(s_ctxz, 1)
                pe.wait_ge(s_cn, T * b + T)
                pe.wait_ge(s_mTc, b + 1)
                transposes(cn).then_inc(s_tT, 1)
                pe.wait_ge(s_hi, 3 * b + 3)
                pe.wait_ge(s_lo, 3 * b + 3)
                pe.wait_ge(s_exp, NSB * b + NSB)
                for t in range(T):
                    toks = slice(t * P, (t + 1) * P)
                    last = three_pass(pe, pA[:, toks], act_in[0][:, toks], act_in[1][:, toks], proj[0][:, 3, :],
                                      proj[1][:, 3, :], start=(t == 0))
                last.then_inc(s_yo, 1)
                pe.wait_ge(s_xn, T * (3 * b + 2) + T)
                transposes(xn).then_inc(s_toT, 1)
                pe.wait_ge(s_x3T, b + 1)
                for t in range(T):
                    last = pe.matmul(pB[:, t * E:(t + 1) * E], x3T[:, t * P:(t + 1) * P], rwT[:, :],
                                     start=(t == 0), stop=True, skip_group_check=True)
                last.then_inc(s_rps, 1)
                for it in range(SINKHORN_ITERS):
                    stand(pe, s_tm, TM_PER * b + TM_STEPS * (it + 1) + 1)
                    for t in range(T):
                        last = pe.transpose(pA[0:E, t * P:(t + 1) * P], route["log"][:, t, :], ident[:, :])
                    last.then_inc(s_toE, 1)
                    stand(pe, s_em, EM_PER * b + EM_STEPS * (it + 1))
                    for t in range(T):
                        last = pe.transpose(pT[:, t * E:(t + 1) * E], elog[:, t * P:(t + 1) * P], ident[0:E, 0:E])
                    last.then_inc(s_toT, 1)
                pe.wait_ge(s_x3hi, b + 1)
                pe.wait_ge(s_route, ROUTE_STEPS * b + ROUTE_STEPS)

            def experts(b):
                N = E * HF

                def up(i):
                    e, hf = divmod(i, HF)
                    cols = slice(hf * P, (hf + 1) * P)
                    if i >= 1:
                        pe.wait_ge(s_relu, N * b + i)
                    three_pass(pe, pG[:, :], wgp[0][:, 0, e, cols], wgp[1][:, 0, e, cols], x3[0][:, :], x3[1][:, :]
                               ).then_inc(s_gp, 1)
                    if i >= 1:
                        pe.wait_ge(s_hid, N * b + i)
                    three_pass(pe, pU[:, :], wgp[0][:, 1, e, cols], wgp[1][:, 1, e, cols], x3[0][:, :], x3[1][:, :]
                               ).then_inc(s_up, 1)

                def down(i):
                    e, hf = divmod(i, HF)
                    pe.wait_ge(s_hid, N * b + i + 1)
                    if hf == 0 and (e > 0 or after_first(b)):
                        pe.wait_ge(s_acc, T * (E * b + e))
                    for t in range(T):
                        last = pe.matmul(pO[:, t * D:(t + 1) * D], hid[:, i % 2, t * P:(t + 1) * P],
                                         wo_sb[:, e, hf, :], start=(hf == 0 and t == 0), stop=(hf == HF - 1),
                                         skip_group_check=True)
                    if hf == HF - 1:
                        last.then_inc(s_oute, 1)

                up(0)
                for i in range(N):
                    if i + 1 < N:
                        up(i + 1)
                    down(i)

            def row(b):
                body(b)
                experts(b)

            body(0)
            pe.wait_ge(s_wsplit, 1)
            pe.wait_ge(s_wo, 16)
            experts(0)
            with pe.Fori(1, NB) as b:
                row(b)


_INS = ["x", "ctx_1024", "mask_1x1xSxS2_if1", "L0_attn_Win", "L0_attn_bin_", "L0_attn_Bp", "L0_attn_Cp", "L0_attn_Dp",
        "L0_attn_Wout", "L0_attn_bout", "L0_xattn_Wq", "L0_xattn_bq", "L0_xattn_Wk", "L0_xattn_bk", "L0_xattn_Wv",
        "L0_xattn_bv", "L0_xattn_Wo", "L0_xattn_bo", "L0_ffn_router_w", "L0_ffn_router_b", "L0_ffn_temperature",
        "L0_ffn_wg", "L0_ffn_wp", "L0_ffn_wo"]
_OUTS = [((4, 512, 128), "float32")]


def kernel(**inputs):
    import numpy as _np
    import concourse.bacc as _bacc
    from concourse import mybir as _mybir
    from concourse.bass_utils import run_bass_kernel_spmd as _run

    nc = _bacc.Bacc("TRN2", target_bir_lowering=False, num_devices=1)
    arrays, args = {}, []
    for name in _INS:
        a = _np.ascontiguousarray(inputs[name])
        arrays[f"in_{name}_dram"] = a
        args.append(nc.dram_tensor(f"in_{name}_dram", a.shape, _mybir.dt.from_np(a.dtype), kind="ExternalInput").ap())
    for i, (shape, dtype) in enumerate(_OUTS):
        dt = _mybir.dt.from_np(_np.dtype(dtype))
        args.append(nc.dram_tensor(f"out_{i}_dram", shape, dt, kind="ExternalOutput").ap())
    build_decoder(nc, *args)
    r = _run(nc, [arrays], core_ids=[0])
    got = tuple(r.results[0][f"out_{i}_dram"] for i in range(len(_OUTS)))
    return got[0]
```

```python
from contextlib import ExitStack

import concourse.bass as bass
from concourse import mybir

P = 128
F32 = mybir.dt.float32
F32R = mybir.dt.float32r
BF16 = mybir.dt.bfloat16
I32 = mybir.dt.int32
ALU = mybir.AluOpType
ACT = mybir.ActivationFunctionType
AX = mybir.AxisListType

LN_EPS = 1e-5
DECAY = 0.9
ROUTE_EPS = 1e-8
TEMP_MIN = 0.1
SINKHORN_ITERS = 3
MASKED = -float(2 ** 100)


def build_decoder(nc, x, ctx_seq, mask, Win, bin_, Bp, Cp, Dp, Wout, bout, Wq, bq, Wk, bk, Wv, bv,
                  Wo, bo, router_w, router_b, temperature, wg, wp, wo, out):
    NB, S, D = x.shape
    KEYS = ctx_seq.shape[1]
    INNER, STATE = Bp.shape
    E, _, FF = wg.shape
    H = 16
    DK = D // H
    T = S // P
    HI = INNER // P
    HF = FF // P
    K0 = P
    K1 = KEYS - K0
    Q = 32
    G = H // 4
    KPAD = K0 + Q
    PARTS = 3
    STACK = PARTS * PARTS * DK
    MROW = 96
    DEEP = MROW + PARTS
    VC = Q
    QSCALE = float(DK) ** -0.5
    assert D == P and S == T * P and K1 <= Q and STACK <= MROW and H * DK == D

    with ExitStack() as ctx:
        def sb(name, shape, dt=F32):
            return ctx.enter_context(nc.sbuf_tensor(name, shape, dt))

        def sem(name):
            return ctx.enter_context(nc.semaphore(name))

        def bank(name):
            return ctx.enter_context(nc.psum_tensor(name, [P, 512], F32))

        ident = sb("ident", [P, P])
        ident_bf = sb("ident_bf", [P, P], BF16)
        decay = sb("decay", [P, S])
        win_raw = sb("win_raw", [P, INNER])
        win = [sb("win_hi", [P, INNER], F32R), sb("win_lo", [P, INNER], F32R)]
        wout_raw = sb("wout_raw", [P, HI, D])
        wscan_f = sb("wscan_f", [P, HI, D])
        wskip_f = sb("wskip_f", [P, HI, D])
        wscan = [sb("wscan_hi", [P, HI, D], F32R), sb("wscan_lo", [P, HI, D], F32R)]
        wskip = [sb("wskip_hi", [P, HI, D], F32R), sb("wskip_lo", [P, HI, D], F32R)]
        bp_sb = sb("bp_sb", [P, HI, STATE])
        cp_sb = sb("cp_sb", [STATE, INNER])
        bcprod = sb("bcprod", [P, HI, STATE])
        bc = sb("bc", [P, HI])
        dp_sb = sb("dp_sb", [P, HI])
        bin_sb = sb("bin_sb", [P, HI])
        nbin = sb("nbin", [P, HI])
        bout_sb = sb("bout_sb", [P, 1])
        proj_raw = sb("proj_raw", [P, 4, D])
        proj = [sb("proj_hi", [P, 4, D], F32R), sb("proj_lo", [P, 4, D], F32R)]
        bq_sb = sb("bq_sb", [P, 1])
        bk_sb = sb("bk_sb", [P, 1])
        bv_row = sb("bv_row", [P, D])
        bo_row = sb("bo_row", [P, D])
        rw_raw = sb("rw_raw", [E, D])
        rwT = [sb("rwT_hi", [P, E], F32R), sb("rwT_lo", [P, E], F32R)]
        rb_row = sb("rb_row", [P, E])
        temp_sb = sb("temp_sb", [P, 1])
        temp_c = sb("temp_c", [P, 1])
        rtemp = sb("rtemp", [P, 1])
        wgp = [sb("wgp_hi", [P, 2, E, FF], F32R), sb("wgp_lo", [P, 2, E, FF], F32R)]
        wo_sb = sb("wo_sb", [P, E, HF, D])
        mask_sb = sb("mask_sb", [P, T, KEYS], I32)
        mbias = sb("mbias", [P, T, KEYS], BF16)
        mbias_rem = sb("mbias_rem", [P, T, 4, Q], BF16)
        mbiasT = sb("mbiasT", [P, S], BF16)
        mbiasT_rem = sb("mbiasT_rem", [P, S], BF16)
        neghalf = sb("neghalf", [P, T])
        seg = sb("seg", [P, T * NB * E])

        x_in = sb("x_in", [P, T, D])
        ctx_in = sb("ctx_in", [P, 2, D])
        stats = sb("stats", [P, T, 6])
        mv = sb("mv", [P, T, 2])
        veps = sb("veps", [P, T])
        rstd = sb("rstd", [P, T])
        xn = sb("xn", [P, T, D])
        act_in = [sb("act_hi", [P, S], F32R), sb("act_lo", [P, S], F32R)]
        cT = [sb("cT_hi", [P, KEYS], F32R), sb("cT_lo", [P, KEYS], F32R)]
        cR = [sb("cR_hi", [P, 4, Q], F32R), sb("cR_lo", [P, 4, Q], F32R)]
        k_f = sb("k_f", [P, KEYS])
        k_r = sb("k_r", [P, KEYS])
        k_parts = sb("k_parts", [P, PARTS, KEYS], BF16)
        v_main = sb("v_main", [P, H, VC])
        v_rem = sb("v_rem", [P, G, 4, VC])
        k_stack = sb("k_stack", [DEEP, H, KPAD], BF16)
        q_stack = sb("q_stack", [DEEP, H, S], BF16)
        sig = sb("sig", [P, HI, S])
        xi_f = sb("xi_f", [P, HI, S])
        xi = [sb("xi_hi", [P, HI, S], F32R), sb("xi_lo", [P, HI, S], F32R)]
        scan_s = sb("scan_s", [P, S])
        mixT = sb("mixT", [P, S])
        x1 = sb("x1", [P, T, D])
        x1b = sb("x1b", [P, T, D])
        q_f = sb("q_f", [P, S])
        q_r = sb("q_r", [P, S])
        q_parts = sb("q_parts", [P, PARTS, S], BF16)
        nmax = sb("nmax", [P, T, H])
        m_r = sb("m_r", [P, T, H])
        m_parts = sb("m_parts", [P, T, PARTS, H], BF16)
        mT = sb("mT", [PARTS * H, S], BF16)
        prob = sb("prob", [P, 10, S])
        wgp_raw = prob[:, 0:2 * E * FF // S, :].rearrange("p u n -> p (u n)").rearrange(
            "p (w e f) -> p w e f", w=2, e=E)
        ctxg = sb("ctxg", [P, 2, S])
        rz = sb("rz", [P, G, T, 4])
        cn = sb("cn", [P, T, D])
        x2 = sb("x2", [P, T, D])
        logit = sb("logit", [P, T, NB, E])
        route = {n: sb("route_" + n, [P, T, NB, E]) for n in
                 ("diff", "exp", "log", "gate", "norm", "over", "tie", "rank", "first", "pick", "w")}
        rcol = {n: sb("rcol_" + n, [P, T, NB]) for n in ("max", "sum", "lse", "inv", "left", "kept", "kinv", "top")}
        top8 = sb("top8", [P, T, NB, 8])
        elog = sb("elog", [NB * E, S])
        eexp = sb("eexp", [NB * E, S])
        ecol = {n: sb("ecol_" + n, [NB * E, 1]) for n in ("nmax", "sum", "lse", "shift")}
        w_gate = sb("w_gate", [P, T, NB, E])

        res = sb("res", [P, NB, T, D])
        x3 = [sb("x3_hi", [P, NB, S], F32R), sb("x3_lo", [P, NB, S], F32R)]
        relu = xi_f
        hid = sig

        pT, pA, pB, pC0, pC1, pG, pU, pO = (bank(n) for n in ("pT", "pA", "pB", "pC0", "pC1", "pG", "pU", "pO"))
        pAB = [pA, pB]
        pC = [pC0, pC1]
        pGU = [pG, pU]
        pT_bf = pT[:, :].bitcast(BF16)

        k_scr = nc.dram_tensor("k_scr", [P, PARTS, KEYS], BF16, kind="Internal").ap()
        q_scr = nc.dram_tensor("q_scr", [P, PARTS, S], BF16, kind="Internal").ap()

        s_ones = sem("ones_ready")
        s_passed = sem("wait_passed")
        (s_wsmall, s_wproj, s_wgp, s_wo, s_mask, s_zero, s_ident, s_identb, s_const,
         s_setupT, s_setup_hi, s_setup, s_bc, s_wsplit, s_xsplit, s_maskb, s_maskT, s_maskTc,
         s_nh) = (sem(n) for n in (
             "w_small_in", "w_proj_in", "w_gp_in", "w_o_in", "mask_in", "zeroed", "ident_ready",
             "ident_bf_ready", "const_ready", "setup_transposed", "setup_hi", "setup_vec", "bc_step",
             "w_split", "expert_split", "mask_bias", "mask_transposed", "mask_copied", "neghalf_ready"))
        (s_x, s_ctx, s_ctxT, s_chi, s_clo, s_kps, s_vps, s_ksplit, s_v, s_kscr, s_kst) = (
            sem(n) for n in ("x_in_ready", "ctx_in_ready", "ctx_transposed", "ctx_hi", "ctx_lo", "k_product",
                             "v_product", "k_split", "v_ready", "k_parts_in_dram", "k_stack_ready"))
        (s_stat, s_mv, s_veps, s_rstd, s_xn, s_tT, s_hi, s_lo) = (
            sem(n) for n in ("ln_stats", "ln_mean_var", "ln_var_eps", "ln_rstd", "ln_done", "act_transposed",
                             "act_hi_ready", "act_lo_ready"))
        (s_win, s_eneg, s_silu, s_xi, s_xihi, s_xilo, s_mix, s_scan, s_mixT, s_mixtr, s_x1, s_x1b) = (
            sem(n) for n in ("win_product", "exp_neg_ready", "silu_step", "xi_ready", "xi_hi", "xi_lo",
                             "mix_product", "scan_done", "mix_ready", "mix_transposed", "x1_ready", "x1_bias"))
        (s_qps, s_qsplit, s_qscr, s_qst, s_sa, s_red, s_msplit, s_mTp, s_mTc, s_mrow, s_sb, s_exp, s_pv,
         s_ctxc, s_ctxtr, s_rz, s_cn, s_yo, s_x2) = (
            sem(n) for n in ("q_product", "q_split", "q_parts_in_dram", "q_stack_ready", "scores_for_max",
                             "max_taken", "max_split", "max_transposed", "max_copied", "max_rows_ready",
                             "scores", "probs", "group_values", "group_copied", "group_transposed", "z_inverse", "attn_normed",
                             "out_product", "x2_ready"))
        (s_x3tr, s_res, s_rps, s_logit, s_tm, s_tmexp, s_tmln, s_toE, s_em, s_emexp, s_emln, s_toT, s_gexp, s_route) = (
            sem(n) for n in ("x3_transposed", "residual_ready", "router_product", "logits_ready", "expert_norm_step",
                             "expert_norm_exp", "expert_norm_log", "to_expert_rows", "token_norm_step",
                             "token_norm_exp", "token_norm_log", "to_token_rows", "gate_exp", "route_step"))
        (s_x3hi, s_x3lo, s_gw, s_gp, s_relu, s_up, s_hid, s_oute, s_acc, s_out) = (
            sem(n) for n in ("x3_hi", "x3_lo", "gate_weights", "gate_product", "relu_ready", "up_product",
                             "hidden_ready", "expert_out", "acc_step", "stored"))

        def after_first(b):
            return not (isinstance(b, int) and b == 0)

        def stand(eng, signal, value):
            eng.wait_ge(signal, value)
            eng.sem_inc(s_passed, 1)

        def at(b):
            return bass.ds(b, 1)

        def tokens_view(ps):
            return ps[:, 0:T * NB * E].rearrange("p (t b e) -> p t b e", t=T, b=NB)

        def f32(ap):
            return ap.bitcast(F32)

        def three_pass(eng, out_ap, lhs_hi, lhs_lo, rhs_hi, rhs_lo, start=True, stop=True):
            eng.matmul(out_ap, lhs_hi, rhs_hi, start=start, stop=False, skip_group_check=True)
            eng.matmul(out_ap, lhs_hi, rhs_lo, start=False, stop=False, skip_group_check=True)
            return eng.matmul(out_ap, lhs_lo, rhs_hi, start=False, stop=stop, skip_group_check=True)

        SA_UNITS = [(qt, hs) for qt in range(T) for hs in
                    ([0, 1, 2], [3, 4, 5], [6, 7, 8], [9, 10, 11], [12, 13], [14, 15])]
        NSA = len(SA_UNITS)
        SB_UNITS = [(g, j) for g in range(G) for j in (None, 0, 1, 2, 3)]
        NSB = len(SB_UNITS)
        NBUF = 10
        N_SMALL = 12
        TM_STEPS = 4
        EM_STEPS = 3
        ROUTE_STEPS = 12

        block = ctx.enter_context(nc.Block())

        @block.sync
        def _(sp):
            sp.dma_start(cp_sb[:, :], Cp).then_inc(s_wsmall, 16)
            sp.dma_start(bp_sb[:, :, :], Bp.rearrange("(h p) n -> p h n", p=P)).then_inc(s_wsmall, 16)
            sp.dma_start(bin_sb[:, :], bin_.rearrange("(h p) -> p h", p=P),
                         allow_slow_non_contiguous=True).then_inc(s_wsmall, 16)
            sp.dma_start(dp_sb[:, :], Dp.rearrange("(h p) -> p h", p=P),
                         allow_slow_non_contiguous=True).then_inc(s_wsmall, 16)
            sp.dma_start(bout_sb[:, :], bout.rearrange("(p o) -> p o", o=1)).then_inc(s_wsmall, 16)
            sp.dma_start(bq_sb[:, :], bq.rearrange("(p o) -> p o", o=1)).then_inc(s_wsmall, 16)
            sp.dma_start(bk_sb[:, :], bk.rearrange("(p o) -> p o", o=1)).then_inc(s_wsmall, 16)
            sp.dma_start(rw_raw[:, :], router_w).then_inc(s_wsmall, 16)
            sp.dma_start(bv_row[:, :], bv.partition_broadcast(P)).then_inc(s_wsmall, 16)
            sp.dma_start(bo_row[:, :], bo.partition_broadcast(P)).then_inc(s_wsmall, 16)
            sp.dma_start(rb_row[:, :], router_b.partition_broadcast(P)).then_inc(s_wsmall, 16)
            sp.dma_start(temp_sb[:, :], temperature.partition_broadcast(P)).then_inc(s_wsmall, 16)
            sp.dma_start(win_raw[:, :], Win).then_inc(s_wproj, 16)
            sp.dma_start(wout_raw[:, :, :], Wout.rearrange("(h p) d -> p h d", p=P)).then_inc(s_wproj, 16)
            for n, w in enumerate((Wq, Wk, Wv, Wo)):
                sp.dma_start(proj_raw[:, n, :], w).then_inc(s_wproj, 16)
            sp.dma_start(mask_sb[:, :, :], mask.rearrange("a c (t p) k -> p (a c t) k", p=P)).then_inc(s_mask, 16)
            sp.dma_start(wgp_raw[:, 0, :, :], wg.rearrange("e d f -> d e f")).then_inc(s_wgp, 16)
            sp.dma_start(wgp_raw[:, 1, :, :], wp.rearrange("e d f -> d e f")).then_inc(s_wgp, 16)
            sp.dma_start(wo_sb[:, :, :, :], wo.rearrange("e (h p) d -> p e h d", p=P)).then_inc(s_wo, 16)

            def row_loads(b):
                if after_first(b):
                    sp.wait_ge(s_ctxT, b)
                sp.dma_start(ctx_in[:, 0, :], ctx_seq[bass.ds(b, 1), 0:K0, :].rearrange("o k d -> (o k) d")
                             ).then_inc(s_ctx, 16)
                sp.dma_start(ctx_in[0:K1, 1, :], ctx_seq[bass.ds(b, 1), K0:KEYS, :].rearrange("o k d -> (o k) d")
                             ).then_inc(s_ctx, 16)
                if after_first(b):
                    sp.wait_ge(s_x1, b)
                sp.dma_start(x_in[:, :, :], x[bass.ds(b, 1), :, :].rearrange("o (t p) d -> p (o t) d", p=P)
                             ).then_inc(s_x, 16)

            def stack_moves(b):
                if after_first(b):
                    sp.wait_ge(s_kst, 16 * PARTS * b)
                sp.wait_ge(s_ksplit, 5 * b + 5)
                sp.dma_start(k_scr, k_parts[:, :, :]).then_inc(s_kscr, 16)
                stand(sp, s_kscr, 16 * b + 16)
                if after_first(b):
                    sp.wait_ge(s_sb, NSB * b)
                for a in range(PARTS):
                    for p_ in range(PARTS):
                        r0 = (a * PARTS + p_) * DK
                        ins = sp.dma_start(k_stack[r0:r0 + DK, :, 0:KEYS],
                                     k_scr[:, p_, :].rearrange("(h d) n -> d h n", d=DK))
                        ins.then_inc(s_kst, 16)
                if after_first(b):
                    sp.wait_ge(s_qst, 16 * PARTS * PARTS * b)
                sp.wait_ge(s_qsplit, 5 * b + 5)
                sp.dma_start(q_scr, q_parts[:, :, :]).then_inc(s_qscr, 16)
                stand(sp, s_qscr, 16 * b + 16)
                for p_ in range(PARTS):
                    for a in range(PARTS):
                        r0 = (p_ * PARTS + a) * DK
                        sp.dma_start(q_stack[r0:r0 + DK, :, :],
                                     q_scr[:, p_, :].rearrange("(h d) n -> d h n", d=DK)).then_inc(s_qst, 16)
                sp.wait_ge(s_mTc, b + 1)
                for p_ in range(PARTS):
                    sp.dma_start(q_stack[MROW + p_:MROW + p_ + 1, :, :],
                                 mT[p_ * H:(p_ + 1) * H, :]).then_inc(s_mrow, 16)

            def body(b):
                row_loads(b)
                stack_moves(b)

            body(0)
            with sp.Fori(1, NB) as b:
                body(b)
            for b in range(NB):
                sp.wait_ge(s_acc, 1 + T * E * (b + 1))
                sp.dma_start(out[b].rearrange("(t p) d -> p t d", p=P), res[:, b, :, :]).then_inc(s_out, 16)
            sp.wait_ge(s_out, 16 * NB)

        @block.gpsimd
        def _(pool):
            pool.memset(ident[:, :], 1.0).then_inc(s_ones, 1)
            pool.wait_ge(s_ones, 1)
            pool.affine_select(out=ident[:, :], in_=ident[:, :], compare_op=ALU.is_equal, fill=0.0, base=0,
                               pattern=[[-1, P]], channel_multiplier=1).then_inc(s_ident, 1)
            pool.memset(neghalf[:, :], -0.5).then_inc(s_nh, 1)
            pool.wait_ge(s_nh, 1)

            def ln_scale(n):
                stand(pool, s_mv, T * n + T)
                pool.tensor_scalar(veps[:, :], mv[:, :, 1], LN_EPS, None, ALU.add).then_inc(s_veps, 1)
                pool.wait_ge(s_veps, n + 1)
                pool.tensor_tensor(rstd[:, :], veps[:, :], neghalf[:, :], ALU.pow).then_inc(s_rstd, 1)

            def body(b):
                ln_scale(3 * b)
                for h in range(HI):
                    pool.wait_ge(s_xihi, HI * b + h + 1)
                    pool.tensor_tensor(xi[1][:, h, :], xi_f[:, h, :], f32(xi[0][:, h, :]), ALU.subtract
                                       ).then_inc(s_xilo, 1)
                ln_scale(3 * b + 1)
                pool.tensor_tensor(x1b[:, :, :], x1[:, :, :], bo_row[:, :].unsqueeze(1).broadcast_to([P, T, D]),
                                   ALU.add).then_inc(s_x1b, 1)
                ln_scale(3 * b + 2)
                pool.wait_ge(s_xn, 3 * T * (b + 1))
                pool.tensor_tensor(res[:, at(b), :, :].rearrange("p o t d -> p (o t) d"), x2[:, :, :], xn[:, :, :], ALU.add).then_inc(s_res, 1)

            body(0)
            with pool.Fori(1, NB) as b:
                body(b)

        @block.scalar
        def _(act):
            act.add_instruction(mybir.InstLoadActFuncSet(name=nc.get_next_instruction_name(), act_func_set_id=6,
                                                         ins=[], outs=[]))
            act.wait_ge(s_ident, 1)
            act.copy(ident_bf[:, :], ident[:, :]).then_inc(s_identb, 1)
            act.wait_ge(s_wsmall, 16 * N_SMALL)
            act.mul(nbin[:, :], bin_sb[:, :], -1.0).then_inc(s_const, 1)
            act.wait_ge(s_setupT, 1)
            act.copy(rwT[0][:, :], pT[:, HI * STATE:HI * STATE + E]).then_inc(s_setup_hi, 1)
            act.wait_ge(s_setupT, 2)
            act.copy(proj[0][:, :, :], pG[:, :].rearrange("p (n d) -> p n d", n=4)).then_inc(s_setup_hi, 1)
            act.wait_ge(s_wproj, 16 * 6)
            act.copy(win[0][:, :], win_raw[:, :]).then_inc(s_setup_hi, 1)
            act.wait_ge(s_maskT, 1)
            act.copy(mbiasT[:, :], pT_bf[:, 0:S]).then_inc(s_maskTc, 1)
            act.wait_ge(s_maskT, 2)
            act.copy(mbiasT_rem[:, :], pT_bf[:, 0:S]).then_inc(s_maskTc, 1)
            act.wait_ge(s_wgp, 32)
            for n in range(2):
                act.copy(wgp[0][:, n, :, :], wgp_raw[:, n, :, :]).then_inc(s_xsplit, 1)

            def hi_of_transposed(b, k):
                act.wait_ge(s_tT, 3 * b + k + 1)
                act.copy(act_in[0][:, :], pT[:, :]).then_inc(s_hi, 1)

            def body(b):
                act.wait_ge(s_ctxT, b + 1)
                act.copy(cT[0][:, :], pT[:, 0:KEYS])
                act.copy(cR[0][:, :, 0:K1], pT[:, K0:KEYS].unsqueeze(1).broadcast_to([P, 4, K1])).then_inc(s_chi, 1)
                hi_of_transposed(b, 0)
                for h in range(HI):
                    act.wait_ge(s_win, HI * b + h + 1)
                    act.wait_ge(s_const, 1)
                    act.activation(sig[:, h, :], pAB[h][:, :], ACT.Exp, bias=nbin[:, h:h + 1], scale=-1.0
                                   ).then_inc(s_eneg, 1)
                for h in range(HI):
                    act.wait_ge(s_xi, HI * b + h + 1)
                    act.copy(xi[0][:, h, :], xi_f[:, h, :]).then_inc(s_xihi, 1)
                hi_of_transposed(b, 1)
                act.wait_ge(s_mTp, b + 1)
                act.copy(mT[:, :], pT_bf[0:PARTS * H, 0:S]).then_inc(s_mTc, 1)
                for g in range(G):
                    for u in range(5 * g, 5 * g + 5):
                        act.wait_ge(s_sb, NSB * b + u + 1)
                        if g >= 2:
                            act.wait_ge(s_pv, G * b + g - 1)
                        elif after_first(b):
                            act.wait_ge(s_pv, G * b)
                        else:
                            act.wait_ge(s_wsplit, 1)
                        act.activation(prob[:, u % NBUF, :], pAB[u % 2][:, :], ACT.Exp).then_inc(s_exp, 1)
                    if g >= 1:
                        copy_group(b, g - 1)
                copy_group(b, G - 1)
                hi_of_transposed(b, 2)
                act.wait_ge(s_x3tr, b + 1)
                act.copy(x3[0][:, at(b), :].rearrange("p o n -> p (o n)"), pT[:, :]).then_inc(s_x3hi, 1)

            def copy_group(b, g):
                act.wait_ge(s_pv, G * b + g + 1)
                if g >= 2:
                    act.wait_ge(s_ctxtr, G * b + g - 1)
                elif after_first(b):
                    act.wait_ge(s_ctxtr, G * b)
                act.copy(ctxg[:, g % 2, :], pC[g % 2][:, :]).then_inc(s_ctxc, 1)

            body(0)
            with act.Fori(1, NB) as b:
                body(b)

            for it in range(SINKHORN_ITERS):
                act.wait_ge(s_tm, TM_STEPS * it + 2 + 1)
                act.activation(route["exp"][:, :, :, :], route["diff"][:, :, :, :], ACT.Exp).then_inc(s_tmexp, 1)
                act.wait_ge(s_tm, TM_STEPS * it + 3 + 1)
                act.activation(rcol["lse"][:, :, :], rcol["sum"][:, :, :], ACT.Ln).then_inc(s_tmln, 1)
                act.wait_ge(s_em, EM_STEPS * it + 1)
                act.activation(eexp[:, :], pA[0:NB * E, :], ACT.Exp, bias=ecol["nmax"][:, :],
                               accum_out=ecol["sum"][:, :]).then_inc(s_emexp, 1)
                act.wait_ge(s_emexp, it + 1)
                act.activation(ecol["lse"][:, :], ecol["sum"][:, :], ACT.Ln).then_inc(s_emln, 1)
            act.wait_ge(s_toT, SINKHORN_ITERS)
            act.activation(route["gate"][:, :, :, :], tokens_view(pT), ACT.Exp).then_inc(s_gexp, 1)

            N = E * HF
            act.sem_inc(s_relu, 1)
            with act.Fori(0, NB) as b:
                for i in range(N):
                    act.wait_ge(s_gp, N * b + i + 1)
                    act.wait_ge(s_hid, 1 + N * b + max(i - 1, 0))
                    act.activation(relu[:, i % 2, :], pG[:, :], ACT.Relu).then_inc(s_relu, 1)

        @block.vector
        def _(dve):
            dve.memset(decay[:, :], DECAY)
            dve.memset(seg[:, :], 1.0)
            dve.memset(k_stack[:, :, :], 0.0)
            dve.memset(q_stack[:, :, :], 0.0)
            dve.memset(v_rem[:, :, :, :], 0.0)
            dve.memset(v_main[:, :, :], 0.0)
            dve.memset(f32(cR[0][:, :, :]), 0.0)
            dve.memset(f32(cR[1][:, :, :]), 0.0)
            dve.memset(mbias_rem[:, :, :, :], 0.0).then_inc(s_zero, 1)
            dve.wait_ge(s_zero, 1)
            dve.memset(seg[:, :].rearrange("p (t e) -> p t e", e=E)[:, :, 0:1], 0.0)
            dve.memset(k_stack[MROW:DEEP, :, 0:KEYS], 1.0)
            dve.memset(v_main[:, :, DK:DK + 1], 1.0)
            for j in range(4):
                last = dve.memset(v_rem[Q * j:Q * j + K1, :, j, DK:DK + 1], 1.0)
            last.then_inc(s_zero, 1)
            dve.wait_ge(s_mask, 16)
            dve.tensor_scalar(mbias[:, :, :], mask_sb[:, :, :], 0.0, MASKED, ALU.is_equal, ALU.mult)
            for j in range(4):
                last = dve.tensor_scalar(mbias_rem[:, :, j, 0:K1], mask_sb[:, :, K0:KEYS], 0.0, MASKED,
                                         ALU.is_equal, ALU.mult)
            last.then_inc(s_maskb, 1)
            dve.wait_ge(s_setupT, 1)
            dve.wait_ge(s_setup_hi, 1)
            dve.wait_ge(s_wsmall, 16 * N_SMALL)
            dve.tensor_tensor(rwT[1][:, :], pT[:, HI * STATE:HI * STATE + E], f32(rwT[0][:, :]), ALU.subtract)
            dve.tensor_tensor(bcprod[:, :, :], bp_sb[:, :, :],
                              pT[:, 0:HI * STATE].rearrange("p (h n) -> p h n", h=HI), ALU.mult).then_inc(s_bc, 1)
            dve.wait_ge(s_bc, 1)
            dve.tensor_reduce(bc[:, :], bcprod[:, :, :], AX.X, ALU.add)
            dve.tensor_scalar(temp_c[:, :], temp_sb[:, :], TEMP_MIN, None, ALU.max).then_inc(s_bc, 1)
            dve.wait_ge(s_bc, 2)
            dve.reciprocal(rtemp[:, :], temp_c[:, :])
            dve.wait_ge(s_wproj, 16 * 6)
            for h in range(HI):
                dve.tensor_scalar(wscan_f[:, h, :], wout_raw[:, h, :], bc[:, h:h + 1], None, ALU.mult)
                dve.tensor_scalar(wskip_f[:, h, :], wout_raw[:, h, :], dp_sb[:, h:h + 1], None,
                                  ALU.mult).then_inc(s_bc, 1)
            dve.wait_ge(s_bc, 4)
            dve.tensor_copy(wscan[0][:, :, :], wscan_f[:, :, :])
            dve.tensor_copy(wskip[0][:, :, :], wskip_f[:, :, :]).then_inc(s_bc, 1)
            dve.wait_ge(s_bc, 5)
            dve.tensor_tensor(wscan[1][:, :, :], wscan_f[:, :, :], f32(wscan[0][:, :, :]), ALU.subtract)
            dve.tensor_tensor(wskip[1][:, :, :], wskip_f[:, :, :], f32(wskip[0][:, :, :]), ALU.subtract)
            dve.wait_ge(s_setup_hi, 3)
            dve.tensor_tensor(proj[1][:, :, :], pG[:, :].rearrange("p (n d) -> p n d", n=4),
                              f32(proj[0][:, :, :]), ALU.subtract)
            dve.tensor_tensor(win[1][:, :], win_raw[:, :], f32(win[0][:, :]), ALU.subtract).then_inc(s_setup, 1)
            for n in range(2):
                dve.wait_ge(s_xsplit, n + 1)
                last = dve.tensor_tensor(wgp[1][:, n, :, :], wgp_raw[:, n, :, :], f32(wgp[0][:, n, :, :]),
                                         ALU.subtract)
            last.then_inc(s_wsplit, 1)

            def layer_norm(n, src):
                for t in range(T):
                    dve.bn_stats(stats[:, t, :], src[:, t, :]).then_inc(s_stat, 1)
                for t in range(T):
                    stand(dve, s_stat, T * n + t + 1)
                    dve.bn_aggr(mv[:, t, :], stats[:, t, :]).then_inc(s_mv, 1)
                dve.wait_ge(s_mv, T * n + T)
                dve.wait_ge(s_rstd, n + 1)
                for t in range(T):
                    dve.tensor_scalar(xn[:, t, :], src[:, t, :], mv[:, t, 0:1], rstd[:, t:t + 1],
                                      ALU.subtract, ALU.mult).then_inc(s_xn, 1)

            def lo_of_transposed(b, k):
                dve.wait_ge(s_hi, 3 * b + k + 1)
                dve.tensor_tensor(act_in[1][:, :], pT[:, :], f32(act_in[0][:, :]), ALU.subtract).then_inc(s_lo, 1)

            def split3(src, rest, parts, done, at):
                dve.wait_ge(done, at)
                dve.tensor_copy(parts(0), src).then_inc(done, 1)
                dve.wait_ge(done, at + 1)
                dve.tensor_tensor(rest, src, parts(0), ALU.subtract).then_inc(done, 1)
                dve.wait_ge(done, at + 2)
                dve.tensor_copy(parts(1), rest).then_inc(done, 1)
                dve.wait_ge(done, at + 3)
                dve.tensor_tensor(parts(2), rest, parts(1), ALU.subtract).then_inc(done, 1)

            def body(b):
                dve.wait_ge(s_chi, b + 1)
                dve.tensor_tensor(cT[1][:, :], pT[:, 0:KEYS], f32(cT[0][:, :]), ALU.subtract)
                dve.tensor_tensor(cR[1][:, :, 0:K1], pT[:, K0:KEYS].unsqueeze(1).broadcast_to([P, 4, K1]),
                                  f32(cR[0][:, :, 0:K1]), ALU.subtract).then_inc(s_clo, 1)
                dve.wait_ge(s_kps, b + 1)
                if after_first(b):
                    dve.wait_ge(s_kscr, 16 * b)
                dve.tensor_scalar(k_f[:, :], pA[:, 0:KEYS], bk_sb[:, 0:1], None, ALU.add).then_inc(s_ksplit, 1)
                split3(k_f[:, :], k_r[:, :], lambda a: k_parts[:, a, :], s_ksplit, 5 * b + 1)
                dve.wait_ge(s_vps, b + 1)
                dve.tensor_tensor(v_main[:, :, 0:DK], pB[:, 0:D].rearrange("p (h d) -> p h d", d=DK),
                                  bv_row[:, :].rearrange("p (h d) -> p h d", d=DK), ALU.add)
                for j in range(4):
                    rows = slice(Q * j, Q * j + K1)
                    last = dve.tensor_tensor(
                        v_rem[rows, :, j, 0:DK],
                        pB[rows, D:2 * D].rearrange("p (g j d) -> p g j d", g=G, j=4)[:, :, j, :],
                        bv_row[rows, :].rearrange("p (g j d) -> p g j d", g=G, j=4)[:, :, j, :], ALU.add)
                last.then_inc(s_v, 1)
                dve.wait_ge(s_x, 16 * b + 16)
                layer_norm(3 * b, x_in)
                lo_of_transposed(b, 0)
                for h in range(HI):
                    n = 2 * (HI * b + h)
                    dve.wait_ge(s_eneg, HI * b + h + 1)
                    dve.tensor_scalar(sig[:, h, :], sig[:, h, :], 1.0, None, ALU.add).then_inc(s_silu, 1)
                    dve.wait_ge(s_silu, n + 1)
                    dve.reciprocal(sig[:, h, :], sig[:, h, :]).then_inc(s_silu, 1)
                    dve.wait_ge(s_silu, n + 2)
                    dve.scalar_tensor_tensor(out=xi_f[:, h, :], in0=pAB[h][:, :], scalar=bin_sb[:, h:h + 1],
                                             in1=sig[:, h, :], op0=ALU.add, op1=ALU.mult).then_inc(s_xi, 1)
                dve.wait_ge(s_mix, 2 * b + 1)
                dve.tensor_tensor_scan(scan_s[:, :], decay[:, :], pA[:, :], 0.0, ALU.mult, ALU.add).then_inc(s_scan, 1)
                dve.wait_ge(s_scan, b + 1)
                dve.wait_ge(s_mix, 2 * b + 2)
                dve.scalar_tensor_tensor(out=mixT[:, :], in0=scan_s[:, :], scalar=bout_sb[:, 0:1], in1=pB[:, :],
                                         op0=ALU.add, op1=ALU.add).then_inc(s_mixT, 1)
                dve.wait_ge(s_mixtr, b + 1)
                dve.tensor_tensor(x1[:, :, :], x_in[:, :, :], pT[:, :].rearrange("p (t d) -> p t d", t=T), ALU.add
                                  ).then_inc(s_x1, 1)
                dve.wait_ge(s_x1, b + 1)
                layer_norm(3 * b + 1, x1)
                lo_of_transposed(b, 1)
                dve.wait_ge(s_qps, b + 1)
                if after_first(b):
                    dve.wait_ge(s_qscr, 16 * b)
                dve.tensor_scalar(q_f[:, :], pA[:, :], bq_sb[:, 0:1], QSCALE, ALU.add, ALU.mult).then_inc(s_qsplit, 1)
                split3(q_f[:, :], q_r[:, :], lambda a: q_parts[:, a, :], s_qsplit, 5 * b + 1)
                for u, (qt, hs) in enumerate(SA_UNITS):
                    dve.wait_ge(s_sa, NSA * b + u + 1)
                    dve.tensor_reduce(nmax[:, qt, hs[0]:hs[-1] + 1],
                                      pAB[u % 2][:, 0:len(hs) * KEYS].rearrange("p (h k) -> p h k", k=KEYS),
                                      AX.X, ALU.max, negate=True).then_inc(s_red, 1)
                dve.wait_ge(s_red, NSA * b + NSA)
                dve.tensor_copy(m_parts[:, :, 0, :], nmax[:, :, :]).then_inc(s_msplit, 1)
                dve.wait_ge(s_msplit, 4 * b + 1)
                dve.tensor_tensor(m_r[:, :, :], nmax[:, :, :], m_parts[:, :, 0, :], ALU.subtract).then_inc(s_msplit, 1)
                dve.wait_ge(s_msplit, 4 * b + 2)
                dve.tensor_copy(m_parts[:, :, 1, :], m_r[:, :, :]).then_inc(s_msplit, 1)
                dve.wait_ge(s_msplit, 4 * b + 3)
                dve.tensor_tensor(m_parts[:, :, 2, :], m_r[:, :, :], m_parts[:, :, 1, :], ALU.subtract
                                  ).then_inc(s_msplit, 1)
                for g in range(G):
                    cols = pGU[g % 2][:, :].rearrange("p (t j v) -> p t j v", t=T, v=VC)
                    dve.wait_ge(s_ctxtr, G * b + g + 1)
                    dve.reciprocal(rz[:, g, :, :], cols[:, :, :, DK]).then_inc(s_rz, 1)
                    dve.wait_ge(s_rz, G * b + g + 1)
                    dve.tensor_tensor(cn[:, :, 4 * g * DK:4 * (g + 1) * DK].rearrange("p t (j d) -> p t j d", d=DK),
                                      cols[:, :, :, 0:DK], rz[:, g, :, :].unsqueeze(3).broadcast_to([P, T, 4, DK]),
                                      ALU.mult).then_inc(s_cn, 1)
                lo_of_transposed(b, 2)
                dve.wait_ge(s_yo, b + 1)
                dve.wait_ge(s_x1b, b + 1)
                dve.tensor_tensor(x2[:, :, :], x1b[:, :, :], pA[:, :].rearrange("p (t d) -> p t d", t=T), ALU.add
                                  ).then_inc(s_x2, 1)
                dve.wait_ge(s_x2, b + 1)
                layer_norm(3 * b + 2, x2)
                dve.wait_ge(s_x3hi, b + 1)
                dve.tensor_tensor(x3[1][:, at(b), :].rearrange("p o n -> p (o n)"), pT[:, :],
                                  f32(x3[0][:, at(b), :].rearrange("p o n -> p (o n)")), ALU.subtract
                                  ).then_inc(s_x3lo, 1)

            body(0)
            with dve.Fori(1, NB) as b:
                body(b)

            def wide(col):
                return col.unsqueeze(3).broadcast_to([P, T, NB, E])

            def steps_of(name):
                return route[name][:, :, :, :]

            for it in range(SINKHORN_ITERS):
                done = TM_STEPS * it + 1
                if it == 0:
                    src = route["norm"][:, :, :, :]
                    dve.wait_ge(s_rps, 1)
                    dve.tensor_tensor(logit[:, :, :, :], tokens_view(pB),
                                      rb_row[:, :].unsqueeze(1).unsqueeze(1).broadcast_to([P, T, NB, E]), ALU.add
                                      ).then_inc(s_logit, 1)
                    dve.wait_ge(s_logit, 1)
                    dve.tensor_scalar(src, logit[:, :, :, :], rtemp[:, 0:1], None, ALU.mult).then_inc(s_tm, 1)
                    dve.wait_ge(s_tm, 1)
                else:
                    src = tokens_view(pT)
                    dve.wait_ge(s_toT, it)
                dve.tensor_reduce(rcol["max"][:, :, :], src, AX.X, ALU.max).then_inc(s_tm, 1)
                dve.wait_ge(s_tm, done + 1)
                dve.tensor_tensor(steps_of("diff"), src, wide(rcol["max"][:, :, :]), ALU.subtract).then_inc(s_tm, 1)
                dve.wait_ge(s_tmexp, it + 1)
                dve.tensor_reduce(rcol["sum"][:, :, :], steps_of("exp"), AX.X, ALU.add).then_inc(s_tm, 1)
                dve.wait_ge(s_tmln, it + 1)
                dve.tensor_tensor(steps_of("log"), steps_of("diff"), wide(rcol["lse"][:, :, :]), ALU.subtract
                                  ).then_inc(s_tm, 1)
                done = EM_STEPS * it
                dve.wait_ge(s_toE, it + 1)
                dve.tensor_reduce(ecol["nmax"][:, :], pA[0:NB * E, :], AX.X, ALU.max, negate=True).then_inc(s_em, 1)
                dve.wait_ge(s_em, done + 1)
                dve.wait_ge(s_emln, it + 1)
                dve.tensor_tensor(ecol["shift"][:, :], ecol["nmax"][:, :], ecol["lse"][:, :], ALU.subtract
                                  ).then_inc(s_em, 1)
                dve.wait_ge(s_em, done + 2)
                dve.tensor_scalar(elog[:, :], pA[0:NB * E, :], ecol["shift"][:, 0:1], None, ALU.add).then_inc(s_em, 1)
            def step(n, ins):
                ins.then_inc(s_route, 1)
                dve.wait_ge(s_route, n)

            dve.wait_ge(s_gexp, 1)
            step(1, dve.tensor_reduce(rcol["sum"][:, :, :], steps_of("gate"), AX.X, ALU.add))
            step(2, dve.tensor_scalar(rcol["inv"][:, :, :], rcol["sum"][:, :, :], ROUTE_EPS, None, ALU.add))
            step(3, dve.reciprocal(rcol["left"][:, :, :], rcol["inv"][:, :, :]))
            step(4, dve.tensor_tensor(steps_of("norm"), steps_of("gate"), wide(rcol["left"][:, :, :]), ALU.mult))
            for t in range(T):
                for b in range(NB):
                    last = dve.max(top8[:, t, b, :], route["norm"][:, t, b, :])
            step(5, last)
            second = top8[:, :, :, 1:2].broadcast_to([P, T, NB, E])
            dve.tensor_tensor(steps_of("over"), steps_of("norm"), second, ALU.is_gt)
            dve.tensor_tensor(rcol["kept"][:, :, :], top8[:, :, :, 0], top8[:, :, :, 1], ALU.add)
            step(6, dve.tensor_tensor(steps_of("tie"), steps_of("norm"), second, ALU.is_equal))
            dve.tensor_reduce(rcol["left"][:, :, :], steps_of("over"), AX.X, ALU.add)
            dve.tensor_scalar(rcol["top"][:, :, :], rcol["kept"][:, :, :], ROUTE_EPS, None, ALU.add)
            step(7, dve.tensor_tensor_scan(steps_of("rank").rearrange("p t b e -> p (t b e)"), seg[:, :],
                                           steps_of("tie").rearrange("p t b e -> p (t b e)"), 0.0,
                                           ALU.mult, ALU.add))
            dve.reciprocal(rcol["kinv"][:, :, :], rcol["top"][:, :, :])
            step(8, dve.tensor_tensor(steps_of("first"), steps_of("rank"), wide(rcol["left"][:, :, :]), ALU.add))
            step(9, dve.scalar_tensor_tensor(out=steps_of("pick").rearrange("p t b e -> p (t b e)"),
                                             in0=steps_of("first").rearrange("p t b e -> p (t b e)"), scalar=2.0,
                                             in1=steps_of("tie").rearrange("p t b e -> p (t b e)"),
                                             op0=ALU.is_le, op1=ALU.mult))
            step(10, dve.tensor_tensor(steps_of("diff"), steps_of("pick"), steps_of("over"), ALU.add))
            step(11, dve.tensor_tensor(steps_of("w"), steps_of("diff"), steps_of("norm"), ALU.mult))
            step(12, dve.tensor_tensor(w_gate[:, :, :, :], steps_of("w"), wide(rcol["kinv"][:, :, :]), ALU.mult))

            dve.wait_ge(s_res, NB)
            N = E * HF
            dve.sem_inc(s_hid, 1)
            dve.sem_inc(s_acc, 1)
            with dve.Fori(0, NB) as b:
                for i in range(N):
                    e = i // HF
                    dve.wait_ge(s_relu, 1 + N * b + i + 1)
                    dve.wait_ge(s_up, N * b + i + 1)
                    dve.tensor_tensor(hid[:, i % 2, :], relu[:, i % 2, :], pU[:, :], ALU.mult).then_inc(s_hid, 1)
                    if i % HF == HF - 1:
                        dve.wait_ge(s_oute, E * b + e + 1)
                        if e > 0:
                            dve.wait_ge(s_acc, 1 + T * (E * b + e))
                        for t in range(T):
                            row = res[:, at(b), t, :].rearrange("p o d -> p (o d)")
                            dve.scalar_tensor_tensor(out=row, in0=pO[:, t * D:(t + 1) * D],
                                                     scalar=w_gate[:, t, at(b), e], in1=row,
                                                     op0=ALU.mult, op1=ALU.add).then_inc(s_acc, 1)

        @block.tensor
        def _(pe):
            pe.wait_ge(s_ident, 1)
            pe.wait_ge(s_wsmall, 16 * N_SMALL)
            for h in range(HI):
                pe.transpose(pT[:, h * STATE:(h + 1) * STATE], cp_sb[:, h * P:(h + 1) * P], ident[0:STATE, 0:STATE])
            pe.transpose(pT[:, HI * STATE:HI * STATE + E], rw_raw[:, :], ident[0:E, 0:E]).then_inc(s_setupT, 1)
            pe.wait_ge(s_wproj, 16 * 6)
            for n in range(4):
                last = pe.transpose(pG[:, n * D:(n + 1) * D], proj_raw[:, n, :], ident[:, :])
            last.then_inc(s_setupT, 1)
            pe.wait_ge(s_identb, 1)
            pe.wait_ge(s_maskb, 1)
            pe.wait_ge(s_setup_hi, 1)
            pe.wait_ge(s_bc, 1)
            for t in range(T):
                last = pe.transpose(pT_bf[:, t * P:(t + 1) * P], mbias[:, t, 0:K0], ident_bf[:, :])
            last.then_inc(s_maskT, 1)
            pe.wait_ge(s_maskTc, 1)
            for t in range(T):
                last = pe.transpose(pT_bf[:, t * P:(t + 1) * P],
                                    mbias_rem[:, t, :, :].rearrange("p j k -> p (j k)"), ident_bf[:, :])
            last.then_inc(s_maskT, 1)
            pe.wait_ge(s_maskTc, 2)
            pe.wait_ge(s_setup, 1)
            pe.wait_ge(s_zero, 2)

            def transposes(src):
                for t in range(T):
                    last = pe.transpose(pT[:, t * P:(t + 1) * P], src[:, t, :], ident[:, :])
                return last

            def body(b):
                pe.wait_ge(s_ctx, 32 * b + 32)
                if after_first(b):
                    pe.wait_ge(s_x3lo, b)
                pe.transpose(pT[:, 0:K0], ctx_in[:, 0, :], ident[:, :])
                pe.transpose(pT[:, K0:KEYS], ctx_in[0:K1, 1, :], ident[0:K1, 0:K1]).then_inc(s_ctxT, 1)
                pe.wait_ge(s_chi, b + 1)
                pe.wait_ge(s_clo, b + 1)
                if after_first(b):
                    pe.wait_ge(s_x2, b)
                three_pass(pe, pA[:, 0:KEYS], proj[0][:, 1, :], proj[1][:, 1, :], cT[0][:, :], cT[1][:, :]
                           ).then_inc(s_kps, 1)
                three_pass(pe, pB[:, 0:D], cT[0][:, 0:K0], cT[1][:, 0:K0], proj[0][:, 2, :], proj[1][:, 2, :])
                flat = [c[:, :, :].rearrange("p j k -> p (j k)") for c in cR]
                three_pass(pe, pB[:, D:2 * D], flat[0], flat[1], proj[0][:, 2, :], proj[1][:, 2, :],
                           start=False).then_inc(s_vps, 1)
                pe.wait_ge(s_xn, T * (3 * b) + T)
                transposes(xn).then_inc(s_tT, 1)
                pe.wait_ge(s_hi, 3 * b + 1)
                pe.wait_ge(s_lo, 3 * b + 1)
                pe.wait_ge(s_ksplit, 5 * b + 1)
                pe.wait_ge(s_v, b + 1)
                for h in range(HI):
                    cols = slice(h * P, (h + 1) * P)
                    three_pass(pe, pAB[h][:, :], win[0][:, cols], win[1][:, cols], act_in[0][:, :], act_in[1][:, :]
                               ).then_inc(s_win, 1)
                for w, dst in ((wscan, pA), (wskip, pB)):
                    for h in range(HI):
                        pe.wait_ge(s_xihi, HI * b + HI)
                        pe.wait_ge(s_xilo, HI * b + h + 1)
                        last = three_pass(pe, dst[:, :], w[0][:, h, :], w[1][:, h, :], xi[0][:, h, :], xi[1][:, h, :],
                                          start=(h == 0), stop=(h == HI - 1))
                    last.then_inc(s_mix, 1)
                pe.wait_ge(s_mixT, b + 1)
                for t in range(T):
                    last = pe.transpose(pT[:, t * P:(t + 1) * P], mixT[:, t * P:(t + 1) * P], ident[:, :])
                last.then_inc(s_mixtr, 1)
                pe.wait_ge(s_xn, T * (3 * b + 1) + T)
                transposes(xn).then_inc(s_tT, 1)
                pe.wait_ge(s_hi, 3 * b + 2)
                pe.wait_ge(s_lo, 3 * b + 2)
                three_pass(pe, pA[:, :], proj[0][:, 0, :], proj[1][:, 0, :], act_in[0][:, :], act_in[1][:, :]
                           ).then_inc(s_qps, 1)
                pe.wait_ge(s_kst, 16 * PARTS * PARTS * (b + 1))
                pe.wait_ge(s_qst, 16 * PARTS * PARTS * (b + 1))
                for u, (qt, hs) in enumerate(SA_UNITS):
                    if u >= 2:
                        pe.wait_ge(s_red, NSA * b + u - 1)
                    elif u == 0:
                        pe.wait_ge(s_qsplit, 5 * b + 1)
                    dst = pAB[u % 2]
                    for n, h in enumerate(hs):
                        pe.matmul(dst[:, n * KEYS:(n + 1) * KEYS], q_stack[0:STACK, h, qt * P:(qt + 1) * P],
                                  k_stack[0:STACK, h, 0:KEYS], start=(n == 0), stop=False, skip_group_check=True)
                    pe.matmul(dst[:, 0:len(hs) * KEYS].rearrange("p (h k) -> p h k", k=KEYS), ident_bf[:, :],
                              mbias[:, qt, :].unsqueeze(1).broadcast_to([P, len(hs), KEYS]),
                              start=False, stop=True, skip_group_check=True).then_inc(s_sa, 1)
                stand(pe, s_msplit, 4 * b + 4)
                for t in range(T):
                    last = pe.transpose(pT_bf[0:PARTS * H, t * P:(t + 1) * P],
                                        m_parts[:, t, :, :].rearrange("p a h -> p (a h)"), ident_bf[:, :])
                last.then_inc(s_mTp, 1)
                pe.wait_ge(s_mrow, 16 * PARTS * (b + 1))

                def scores(u):
                    g, j = SB_UNITS[u]
                    dst = pAB[u % 2]
                    if u >= 2:
                        pe.wait_ge(s_exp, NSB * b + u - 1)
                    else:
                        pe.wait_ge(s_red, NSA * b + NSA)
                    if j is None:
                        for c in range(4):
                            pe.matmul(dst[Q * c:Q * (c + 1), :], k_stack[:, 4 * g + c, K0:KPAD],
                                      q_stack[:, 4 * g + c, :], start=True, stop=False, skip_group_check=True)
                        bias = mbiasT_rem
                    else:
                        pe.matmul(dst[:, :], k_stack[:, 4 * g + j, 0:K0], q_stack[:, 4 * g + j, :],
                                  start=True, stop=False, skip_group_check=True)
                        bias = mbiasT
                    pe.matmul(dst[:, :], ident_bf[:, :], bias[:, :], start=False, stop=True, skip_group_check=True
                              ).then_inc(s_sb, 1)

                def weigh(g):
                    pe.wait_ge(s_exp, NSB * b + 5 * g + 5)
                    if g >= 2:
                        pe.wait_ge(s_ctxc, G * b + g - 1)
                    elif after_first(b):
                        pe.wait_ge(s_ctxc, G * b)
                    dst = pC[g % 2]
                    pe.matmul(dst[:, :], v_rem[:, g, :, :].rearrange("p j v -> p (j v)"),
                              prob[:, (5 * g) % NBUF, :], start=True, stop=False, skip_group_check=True)
                    for j in range(4):
                        last = pe.matmul(dst[Q * j:Q * (j + 1), :], v_main[:, 4 * g + j, :],
                                         prob[:, (5 * g + 1 + j) % NBUF, :], start=False, stop=True,
                                         skip_group_check=True)
                    last.then_inc(s_pv, 1)

                def by_token(g):
                    pe.wait_ge(s_ctxc, G * b + g + 1)
                    if g >= 2:
                        pe.wait_ge(s_cn, G * b + g - 1)
                    elif after_first(b):
                        pe.wait_ge(s_cn, G * b)
                    for t in range(T):
                        last = pe.transpose(pGU[g % 2][:, t * P:(t + 1) * P], ctxg[:, g % 2, t * P:(t + 1) * P],
                                            ident[:, :])
                    last.then_inc(s_ctxtr, 1)

                for g in range(G + 2):
                    if g < G:
                        for u in range(5 * g, 5 * g + 5):
                            scores(u)
                    if 1 <= g <= G:
                        weigh(g - 1)
                    if g >= 2:
                        by_token(g - 2)
                pe.wait_ge(s_cn, G * b + G)
                transposes(cn).then_inc(s_tT, 1)
                pe.wait_ge(s_hi, 3 * b + 3)
                pe.wait_ge(s_lo, 3 * b + 3)
                pe.wait_ge(s_exp, NSB * b + NSB)
                for t in range(T):
                    toks = slice(t * P, (t + 1) * P)
                    last = three_pass(pe, pA[:, toks], act_in[0][:, toks], act_in[1][:, toks], proj[0][:, 3, :],
                                      proj[1][:, 3, :], start=(t == 0))
                last.then_inc(s_yo, 1)
                pe.wait_ge(s_xn, T * (3 * b + 2) + T)
                transposes(xn).then_inc(s_x3tr, 1)

            body(0)
            with pe.Fori(1, NB) as b:
                body(b)

            pe.wait_ge(s_x3hi, NB)
            pe.wait_ge(s_x3lo, NB)
            pe.wait_ge(s_exp, NSB * NB)
            for t in range(T):
                for b in range(NB):
                    toks = [half[:, b, t * P:(t + 1) * P] for half in x3]
                    c0 = (t * NB + b) * E
                    last = three_pass(pe, pB[:, c0:c0 + E], toks[0], toks[1], rwT[0][:, :], rwT[1][:, :],
                                      start=(c0 == 0))
            last.then_inc(s_rps, 1)
            for it in range(SINKHORN_ITERS):
                pe.wait_ge(s_tm, TM_STEPS * (it + 1) + 1)
                for t in range(T):
                    last = pe.transpose(pA[0:NB * E, t * P:(t + 1) * P],
                                        route["log"][:, t, :, :].rearrange("p b e -> p (b e)"), ident[:, :])
                last.then_inc(s_toE, 1)
                pe.wait_ge(s_em, EM_STEPS * (it + 1))
                for t in range(T):
                    last = pe.transpose(pT[:, t * NB * E:(t + 1) * NB * E], elog[:, t * P:(t + 1) * P],
                                        ident[0:NB * E, 0:NB * E])
                last.then_inc(s_toT, 1)

            N = E * HF
            pe.wait_ge(s_wsplit, 1)
            pe.wait_ge(s_wo, 16)
            pe.wait_ge(s_cn, G * NB)
            pe.wait_ge(s_x3lo, NB)
            pe.wait_ge(s_route, ROUTE_STEPS)

            with pe.Fori(0, NB) as b:
                x3_b = [half[:, at(b), :].rearrange("p o n -> p (o n)") for half in x3]

                def up(i):
                    e, hf = divmod(i, HF)
                    cols = slice(hf * P, (hf + 1) * P)
                    pe.wait_ge(s_relu, 1 + N * b + i)
                    three_pass(pe, pG[:, :], wgp[0][:, 0, e, cols], wgp[1][:, 0, e, cols], x3_b[0], x3_b[1]
                               ).then_inc(s_gp, 1)
                    pe.wait_ge(s_hid, 1 + N * b + i)
                    three_pass(pe, pU[:, :], wgp[0][:, 1, e, cols], wgp[1][:, 1, e, cols], x3_b[0], x3_b[1]
                               ).then_inc(s_up, 1)

                def down(i):
                    e, hf = divmod(i, HF)
                    pe.wait_ge(s_hid, 1 + N * b + i + 1)
                    if hf == 0:
                        pe.wait_ge(s_acc, 1 + T * (E * b + e))
                    for t in range(T):
                        last = pe.matmul(pO[:, t * D:(t + 1) * D], hid[:, i % 2, t * P:(t + 1) * P],
                                         wo_sb[:, e, hf, :], start=(hf == 0 and t == 0), stop=(hf == HF - 1),
                                         skip_group_check=True)
                    if hf == HF - 1:
                        last.then_inc(s_oute, 1)

                up(0)
                for i in range(N):
                    if i + 1 < N:
                        up(i + 1)
                    down(i)


_INS = ["x", "ctx_1024", "mask_1x1xSxS2_if1", "L0_attn_Win", "L0_attn_bin_", "L0_attn_Bp", "L0_attn_Cp", "L0_attn_Dp",
        "L0_attn_Wout", "L0_attn_bout", "L0_xattn_Wq", "L0_xattn_bq", "L0_xattn_Wk", "L0_xattn_bk", "L0_xattn_Wv",
        "L0_xattn_bv", "L0_xattn_Wo", "L0_xattn_bo", "L0_ffn_router_w", "L0_ffn_router_b", "L0_ffn_temperature",
        "L0_ffn_wg", "L0_ffn_wp", "L0_ffn_wo"]
_OUTS = [((4, 512, 128), "float32")]


def kernel(**inputs):
    import numpy as _np
    import concourse.bacc as _bacc
    from concourse import mybir as _mybir
    from concourse.bass_utils import run_bass_kernel_spmd as _run

    nc = _bacc.Bacc("TRN2", target_bir_lowering=False, num_devices=1)
    arrays, args = {}, []
    for name in _INS:
        a = _np.ascontiguousarray(inputs[name])
        arrays[f"in_{name}_dram"] = a
        args.append(nc.dram_tensor(f"in_{name}_dram", a.shape, _mybir.dt.from_np(a.dtype), kind="ExternalInput").ap())
    for i, (shape, dtype) in enumerate(_OUTS):
        dt = _mybir.dt.from_np(_np.dtype(dtype))
        args.append(nc.dram_tensor(f"out_{i}_dram", shape, dt, kind="ExternalOutput").ap())
    build_decoder(nc, *args)
    r = _run(nc, [arrays], core_ids=[0])
    got = tuple(r.results[0][f"out_{i}_dram"] for i in range(len(_OUTS)))
    return got[0]
```

```python
from contextlib import ExitStack

import concourse.bass as bass
from concourse import mybir

P = 128
F32 = mybir.dt.float32
F32R = mybir.dt.float32r
BF16 = mybir.dt.bfloat16
I32 = mybir.dt.int32
ALU = mybir.AluOpType
ACT = mybir.ActivationFunctionType
AX = mybir.AxisListType

LN_EPS = 1e-5
DECAY = 0.9
ROUTE_EPS = 1e-8
TEMP_MIN = 0.1
SIGMOID_MAX = float(2 ** 60)
SINKHORN_ITERS = 3
MASKED = -float(2 ** 100)


def build_decoder(nc, x, ctx_seq, mask, Win, bin_, Bp, Cp, Dp, Wout, bout, Wq, bq, Wk, bk, Wv, bv,
                  Wo, bo, router_w, router_b, temperature, wg, wp, wo, out):
    NB, S, D = x.shape
    KEYS = ctx_seq.shape[1]
    INNER, STATE = Bp.shape
    E, _, FF = wg.shape
    H = 16
    DK = D // H
    T = S // P
    HI = INNER // P
    HF = FF // P
    K0 = P
    K1 = KEYS - K0
    Q = 32
    G = H // 4
    KPAD = K0 + Q
    PARTS = 3
    STACK = PARTS * PARTS * DK
    MROW = STACK
    DEEP = MROW + PARTS
    VC = Q
    QSCALE = float(DK) ** -0.5
    NBUF = 8
    LNS = ("mix", "att", "ffn")
    GB = 2
    GROUPS = NB // GB
    assert D == P and S == T * P and K1 <= Q and H * DK == D

    with ExitStack() as ctx:
        def sb(name, shape, dt=F32):
            return ctx.enter_context(nc.sbuf_tensor(name, shape, dt))

        def sem(name):
            return ctx.enter_context(nc.semaphore(name))

        def bank(name):
            return ctx.enter_context(nc.psum_tensor(name, [P, 512], F32))

        ident = sb("ident", [P, P])
        decay = sb("decay", [P, S])
        ident_bf = sb("ident_bf", [P, P], BF16)
        win = [sb("win_hi", [P, INNER], F32R), sb("win_lo", [P, INNER], F32R)]
        wscan = [sb("wscan_hi", [P, HI, D], F32R), sb("wscan_lo", [P, HI, D], F32R)]
        wskip = [sb("wskip_hi", [P, HI, D], F32R), sb("wskip_lo", [P, HI, D], F32R)]
        bp_sb = sb("bp_sb", [P, HI, STATE])
        cp_sb = sb("cp_sb", [STATE, INNER])
        bcprod = sb("bcprod", [P, HI, STATE])
        bc = sb("bc", [P, HI])
        dp_sb = sb("dp_sb", [P, HI])
        bin_sb = sb("bin_sb", [P, HI])
        nbin = sb("nbin", [P, HI])
        bout_sb = sb("bout_sb", [P, 1])
        proj = [sb("proj_hi", [P, 4, D], F32R), sb("proj_lo", [P, 4, D], F32R)]
        bq_sb = sb("bq_sb", [P, 1])
        bk_sb = sb("bk_sb", [P, 1])
        bv_row = sb("bv_row", [P, D])
        bo_row = sb("bo_row", [P, D])
        rw_raw = sb("rw_raw", [E, D])
        rwT = [sb("rwT_hi", [P, E], F32R), sb("rwT_lo", [P, E], F32R)]
        rb_row = sb("rb_row", [P, E])
        temp_sb = sb("temp_sb", [P, 1])
        temp_c = sb("temp_c", [P, 1])
        rtemp = sb("rtemp", [P, 1])
        wgp = [sb("wgp_hi", [P, 2, E, FF], F32R), sb("wgp_lo", [P, 2, E, FF], F32R)]
        mbias = sb("mbias", [P, T, KEYS], BF16)
        mbias_rem = sb("mbias_rem", [P, T, 4, Q], BF16)
        mbiasT = sb("mbiasT", [P, S], BF16)
        mbiasT_rem = sb("mbiasT_rem", [P, S], BF16)
        neghalf = sb("neghalf", [P, T])
        seg = sb("seg", [P, T * GB * E])

        ctx_in = sb("ctx_in", [P, NB, 2, D])
        ln = {k: {"stats": sb(k + "_stats", [P, T, 6]), "mv": sb(k + "_mv", [P, T, 2]), "veps": sb(k + "_veps", [P, T]),
                  "rstd": sb(k + "_rstd", [P, T]), "nmean": sb(k + "_nmean", [P, T]),
                  "shift": sb(k + "_shift", [P, T])} for k in LNS}
        xn = sb("xn", [P, T, D])
        xn_post = sb("xn_post", [P, T, D])
        act_in = [sb("act_hi", [P, S], F32R), sb("act_lo", [P, S], F32R)]
        act_post = [sb("act_post_hi", [P, S], F32R), sb("act_post_lo", [P, S], F32R)]
        cT = [sb("cT_hi", [P, KEYS], F32R), sb("cT_lo", [P, KEYS], F32R)]
        cR = [sb("cR_hi", [P, 4, Q], F32R), sb("cR_lo", [P, 4, Q], F32R)]
        k_f = sb("k_f", [P, KEYS])
        k_parts = sb("k_parts", [P, PARTS, KEYS], BF16)
        v_main = sb("v_main", [P, 2, H, VC])
        v_rem = sb("v_rem", [P, 2, G, 4, VC])
        k_stack = [sb("k_stack%d" % i, [DEEP, H, KPAD], BF16) for i in range(2)]
        sig = sb("sig", [P, HI, S])
        xi_f = sb("xi_f", [P, HI, S])
        xi = [sb("xi_hi", [P, HI, S], F32R), sb("xi_lo", [P, HI, S], F32R)]
        mixT = sb("mixT", [P, S])
        x1 = sb("x1", [P, T, D])
        q_f = sb("q_f", [P, S])
        q_parts = sb("q_parts", [P, PARTS, S], BF16)
        nmax_mask = sb("nmax_mask", [P, T * KEYS])
        nmax = nmax_mask[:, 0:T * H].rearrange("p (t h) -> p t h", t=T)
        m_r = sb("m_r", [P, T, H])
        m_parts = sb("m_parts", [P, T, PARTS, H], BF16)
        mT = sb("mT", [PARTS * H, S], BF16)
        prob = sb("prob", [P, NBUF, S])
        wgp_raw = prob[:, 0:2 * E * FF // S, :].rearrange("p u n -> p (u n)").rearrange(
            "p (w e f) -> p w e f", w=2, e=E)
        wo_sb = prob[:, 0:E * FF // S, :].rearrange("p u n -> p (u n)").rearrange(
            "p (e h d) -> p e h d", e=E, h=HF)
        ctxg = sb("ctxg", [P, 2, S])
        rz = sb("rz", [P, G, T, 4])
        cn = sb("cn", [P, T, D])
        x2 = sb("x2", [P, T, D])
        logit = sb("logit", [P, GROUPS, T, GB, E])
        route = {n: sb("route_" + n, [P, GROUPS, T, GB, E]) for n in
                 ("diff", "exp", "log", "gate", "norm", "over", "tie", "rank", "pick", "w")}
        rcol = {n: sb("rcol_" + n, [P, GROUPS, T, GB]) for n in ("max", "sum", "lse", "inv", "left", "kept", "kinv", "top")}
        top8 = sb("top8", [P, GROUPS, T, GB, 8])
        ecol = {n: sb("ecol_" + n, [GB * E, 1]) for n in ("nmax", "sum", "lse", "shift")}
        w_gate = sb("w_gate", [P, T, NB, E])

        res = sb("res", [P, NB, T, D])
        x3 = [sb("x3_hi", [P, NB, S], F32R), sb("x3_lo", [P, NB, S], F32R)]
        q_stack = [sb("q_stack%d" % i, [DEEP, H, S], BF16) for i in range(2)]

        setup_f = ctxg[:, :, :].rearrange("p h n -> p (h n)")
        win_raw = setup_f[:, 0:INNER]
        wout_raw, wscan_f, wskip_f = (
            setup_f[:, INNER + i * HI * D:INNER + (i + 1) * HI * D].rearrange("p (h d) -> p h d", h=HI)
            for i in range(3))
        proj_raw = x2
        mask_sb = nmax_mask[:, 0:T * KEYS].bitcast(I32).rearrange("p (t k) -> p t k", t=T)
        elog, eexp = mixT[0:GB * E, :], q_f[0:GB * E, :]
        relu = xi_f
        hid = sig

        pT, pA, pB, pS0, pS1, pS2, pC, pG = (bank(n) for n in ("pT", "pA", "pB", "pS0", "pS1", "pS2", "pC", "pG"))
        pAB = [pA, pB]
        pS = [pS0, pS1, pS2]
        KCOL, VCOL, RCOL = slice(0, KEYS), slice(2 * P, 3 * P), slice(3 * P, 4 * P)
        pLogit, pByExpert, pByToken = [pB, pC], [pA, pT], [pB, pG]
        pGate, pUp, pO = [pA, pB], [pS0, pS1], pS2
        pG_bf = pG[:, :].bitcast(BF16)
        pC_bf = pC[:, :].bitcast(BF16)
        pT_bf = pT[:, :].bitcast(BF16)

        k_scr = nc.dram_tensor("k_scr", [P, PARTS, KEYS], BF16, kind="Internal").ap()
        q_scr = nc.dram_tensor("q_scr", [P, PARTS, S], BF16, kind="Internal").ap()

        s_ones = sem("ones_ready")
        (s_wwin, s_wmix, s_wsmall, s_wproj, s_wgp, s_wo, s_wo2, s_mask, s_zero, s_ident, s_identb, s_const,
         s_bc, s_wsplit, s_xsplit, s_maskb, s_maskT, s_maskTc,
         s_nh, s_cpT, s_rwhi, s_projT, s_projhi, s_proj, s_winhi, s_winsplit, s_mixw, s_kones, s_seg) = (sem(n) for n in (
             "w_win_in", "w_mix_in", "w_small_in", "w_proj_in", "w_gp_in", "w_o_in", "w_o_rest_in", "mask_in", "zeroed", "ident_ready",
             "ident_bf_ready", "const_ready", "bc_step",
             "w_split", "expert_split", "mask_bias", "mask_transposed", "mask_copied", "neghalf_ready",
             "small_transposed", "rw_hi", "proj_transposed", "proj_hi", "proj_split", "win_hi", "win_split",
             "mix_weights", "key_rows_of_ones", "segments_ready"))
        s_x = [sem("x_in_ready%d" % b) for b in range(NB)]
        (s_ctx, s_ctxT, s_chi, s_clo, s_vps, s_ksplit, s_v, s_kscr, s_kst) = (
            sem(n) for n in ("ctx_in_ready", "ctx_transposed", "ctx_hi", "ctx_lo",
                             "kv_product", "k_split", "v_ready", "k_parts_in_dram", "k_stack_ready"))
        s_stat, s_mv, s_veps, s_rstd, s_xn, s_tT, s_hi, s_lo = (
            {k: sem(k + "_" + n) for k in LNS}
            for n in ("ln_stats", "ln_mean_var", "ln_var_eps", "ln_rstd", "ln_done", "act_transposed",
                      "act_hi_ready", "act_lo_ready"))
        s_nmean, s_shift = ({k: sem(k + "_" + n) for k in ("mix", "att")} for n in ("neg_mean", "ln_shift"))
        s_cnT, s_cnhi, s_cnlo = (sem(n) for n in ("attn_transposed", "attn_hi_ready", "attn_lo_ready"))
        (s_win, s_eneg, s_eplus, s_lnp, s_sig, s_xi, s_xihi, s_xilo, s_mix, s_scan, s_mixT, s_mixtr, s_x1, s_x1b) = (
            sem(n) for n in ("win_product", "exp_neg_ready", "one_plus_exp", "log_ready", "sigmoid_ready", "xi_ready", "xi_hi", "xi_lo",
                             "mix_product", "scan_done", "mix_ready", "mix_transposed", "x1_ready", "x1_bias"))
        (s_qps, s_qsplit, s_qscr, s_qst, s_sa, s_red, s_msplit, s_mTp, s_mTc, s_mrow, s_sb, s_exp, s_pv,
         s_ctxc, s_ctxtr, s_rz, s_cn, s_yo, s_x2) = (
            sem(n) for n in ("q_product", "q_split", "q_parts_in_dram", "q_stack_ready", "scores_for_max",
                             "max_taken", "max_split", "max_transposed", "max_copied", "max_rows_ready",
                             "scores", "probs", "group_values", "group_copied", "group_transposed", "z_inverse", "attn_normed",
                             "out_product", "x2_ready"))
        (s_res, s_rps, s_logit, s_tm, s_tmexp, s_tmln, s_toE, s_em, s_emexp, s_emln, s_toT, s_gexp, s_route) = (
            sem(n) for n in ("residual_ready", "router_product", "logits_ready", "expert_norm_step",
                             "expert_norm_exp", "expert_norm_log", "to_expert_rows", "token_norm_step",
                             "token_norm_exp", "token_norm_log", "to_token_rows", "gate_exp", "route_step"))
        (s_gp, s_relu, s_up, s_hid, s_down, s_acc, s_out) = (
            sem(n) for n in ("gate_product", "relu_ready", "up_product", "hidden_ready",
                             "down_product", "acc_step", "stored"))

        def at(b):
            return bass.ds(b, 1)

        def q_bank(b):
            return pA if b > 0 else pS2

        def score_bank(b, k):
            return pS[((NSA + NSB) * b + k) % len(pS)]

        def tokens_view(ps):
            return ps[:, 0:T * GB * E].rearrange("p (t b e) -> p t b e", t=T, b=GB)

        def f32(ap):
            return ap.bitcast(F32)

        def three_pass(eng, out_ap, lhs_hi, lhs_lo, rhs_hi, rhs_lo, start=True, stop=True):
            eng.matmul(out_ap, lhs_hi, rhs_hi, start=start, stop=False, skip_group_check=True)
            eng.matmul(out_ap, lhs_hi, rhs_lo, start=False, stop=False, skip_group_check=True)
            return eng.matmul(out_ap, lhs_lo, rhs_hi, start=False, stop=stop, skip_group_check=True)

        SA_UNITS = [(qt, hs) for qt in range(T) for hs in
                    ([0, 1, 2], [3, 4, 5], [6, 7, 8], [9, 10, 11], [12, 13], [14, 15])]
        NSA = len(SA_UNITS)
        SB_UNITS = [(g, j) for g in range(G) for j in (None, 0, 1, 2, 3)]
        NSB = len(SB_UNITS)
        AHEAD = 2
        WO_FIRST = (NSB * (NB - 1) + NSB - 5) % NBUF * S // (HF * D)
        N_SMALL = 5
        EXPERT_STEP = 2
        EXPERT_STEPS = 2 * E // EXPERT_STEP
        EXPERTS_AT = [17, 18, 19, 20, 21, 22, 23, 24]
        LAST_AT = [3, 3, 6, 6]
        QUERIES_AT = [0, 4, 4, 4, 7, 7, 8, 9, 10, 11, 11]
        KV_AT = [15, 15, 17, 25, 26, 26, 27]
        MIX_AT = [0, 0, 5, 9, 9, 9, 13, 13, 13, 13, 14, 14, 15, 15, 16, 15, 15, 16, 16,
                  19, 22, 24, 26, 27, 27, 28, 28]
        POST_AT = [12, 12, 14, 25, 26, 26, 26, 29, 33, 33, 33, 30]
        GROUP_AT = [6, 6, 9, 9]
        LEFT_STEPS = [1, 1, 3, 2, 3, 3, 3] + SINKHORN_ITERS * [2, 2, 2, 2, 2] + [1, 1, 1, 1]
        ROUTER_AT = ([34, 35, 36, 37, 38, 39, 40, 41, 42, 44, 45],
                     [0, 0, 1, 1, 2, 5, 5, 5, 7, 10, 10, 10, 11, 11, 12, 15, 15, 15, 17, 20, 20, 30, 32, 34])
        TM_STEPS = 4
        EM_STEPS = 3
        ROUTE_STEPS = 12
        TM_PER = SINKHORN_ITERS * TM_STEPS + 1
        EM_PER = SINKHORN_ITERS * EM_STEPS

        def mix_in(b):
            return [("norm_stats", b, "mix"), ("norm_scale", b, "mix"), ("norm", b, "mix"), ("norm_T", b, "mix"),
                    ("hi", b, "mix"), ("lo", b, "mix"), ("win", b, 0), ("exp_neg", b, 0), ("exp_neg", b, 1),
                    ("one_plus", b, 0), ("one_plus", b, 1), ("sigmoid", b, 0), ("sigmoid", b, 1), ("xi", b, 0),
                    ("xi", b, 1), ("xi_hi", b, 0), ("xi_lo", b, 0), ("xi_hi", b, 1), ("xi_lo", b, 1)]

        def mix_out(b):
            return [("mix_product", b, 0), ("mix_product", b, 1), ("scan", b, 0), ("mix_T", b, 0), ("x1", b, 0),
                    ("norm_stats", b, "att"), ("norm_scale", b, "att"), ("x1_bias", b, 0)]

        def queries(b):
            return [("norm", b, "att"), ("norm_T", b, "att"), ("hi", b, "att"), ("lo", b, "att"),
                    ("q_product", b, 0)] + [("q_split", b, n) for n in range(5)] + [("q_move", b, 0)]

        def keys_values(b):
            return [("ctx_T", b, 0), ("ctx_hi", b, 0), ("ctx_lo", b, 0), ("kv_product", b, 0), ("k_split", b, 0),
                    ("k_move", b, 0), ("values", b, 0)]

        def last_group(b):
            return [("weigh", b, G - 1), ("copy_group", b, G - 1), ("by_token", b, G - 1), ("attn_norm", b, G - 1)]

        def router(grp):
            steps = [("logits", grp, 0)]
            for it in range(SINKHORN_ITERS):
                steps += [(name, grp, it) for name in
                          ("expert_max", "expert_exp", "expert_sum", "expert_ln", "expert_log", "to_experts",
                           "token_max", "token_exp", "token_log", "to_tokens")]
            return steps + [("gate_exp", grp, 0), ("gates", grp, 0), ("gates", grp, 1), ("gates", grp, 2)]

        def post(b):
            return [("attn_T", b, 0), ("attn_hi", b, 0), ("attn_lo", b, 0), ("out_product", b, 0), ("x2", b, 0),
                    ("norm_stats", b, "ffn"), ("norm_scale", b, "ffn"), ("norm", b, "ffn"), ("norm_T", b, "ffn"),
                    ("hi", b, "ffn"), ("lo", b, "ffn"), ("residual", b, 0)]

        first = mix_in(0)
        WIN = first.index(("win", 0, 0))
        second = mix_in(1)
        WIN1 = WIN + 1
        STEPS = (first[:1] + [("setup_win", 0, 0)] + first[1:2] + [("ones", 0, 0)] + first[2:WIN + 1]
                 + [("setup_proj", 0, 0), ("ctx_T", 0, 0)] + first[WIN + 1:] + [("setup_mix", 0, 0)]
                 + keys_values(0)[1:] + mix_out(0)[:2] + second[:2] + mix_out(0)[2:3] + [("setup_mask", 0, 0)]
                 + mix_out(0)[3:5] + second[2:4] + mix_out(0)[5:] + second[4:WIN1] + queries(0)[:4]
                 + second[WIN1:WIN1 + 2] + queries(0)[4:] + [("load_experts", 0, 0)] + second[WIN1 + 2:] + mix_out(1))
        for b in range(NB):
            slots = [[] for _ in range(NSA + NSB + 3)]
            for u in range(NSA):
                slots[u].append(("scores_max", b, u))
            slots[NSA] += [("max_split", b, 0)]
            slots[NSA + 1] += [("max_T", b, 0)]
            slots[NSA + 2] += [("max_rows", b, 0)]
            B0 = NSA + 3
            for u in range(NSB):
                slots[B0 + u].append(("scores", b, u))

            def place(steps, at_slots):
                for step, slot in zip(steps, at_slots, strict=True):
                    slots[slot].append(step)

            if b > 0:
                place(last_group(b - 1), LAST_AT)
            if b == 0:
                place([("split_experts", 0, n) for n in range(EXPERT_STEPS)], EXPERTS_AT)
            if b + 1 < NB:
                place(queries(b + 1), QUERIES_AT)
            if b > 0:
                place(post(b - 1), POST_AT)
            if b + 1 < NB:
                place(keys_values(b + 1), KV_AT)
            if b + 2 < NB:
                place(mix_in(b + 2) + mix_out(b + 2), MIX_AT)
            if b == NB - 2:
                place(router(0)[:len(ROUTER_AT[0])], ROUTER_AT[0])
            elif b == NB - 1:
                place(router(0)[len(ROUTER_AT[0]):], ROUTER_AT[1])
            for g in range(G - 1):
                place([("weigh", b, g), ("copy_group", b, g), ("by_token", b, g), ("attn_norm", b, g)],
                      [B0 + 5 * g + n for n in GROUP_AT])
            STEPS += [step for slot in slots for step in slot]
        units = [(b, i) for b in range(GB) for i in range(E * HF)]
        rest = iter(last_group(NB - 1)[1:] + post(NB - 1) + router(1))
        left = [[next(rest) for _ in range(n)] for n in LEFT_STEPS]
        STEPS += last_group(NB - 1)[:1] + [("expert_up", *units[0])]
        for k, unit in enumerate(units):
            if k + 1 < len(units):
                STEPS.append(("expert_up", *units[k + 1]))
            STEPS.append(("expert_down", *unit))
            STEPS += left.pop(0) if left else []
        STEPS += [step for steps in left for step in steps]

        block = ctx.enter_context(nc.Block())

        @block.sync
        def _(sp):
            sp.dma_start(res[:, 0, :, :], x[0].rearrange("(t p) d -> p t d", p=P)).then_inc(s_x[0], 16)
            sp.dma_start(win_raw, Win).then_inc(s_wwin, 16)
            sp.dma_start(bin_sb[:, :], bin_.rearrange("(h p) -> p h", p=P),
                         allow_slow_non_contiguous=True).then_inc(s_wwin, 16)
            sp.dma_start(ctx_in[:, :, 0, :], ctx_seq[:, 0:K0, :].rearrange("b k d -> k b d")).then_inc(s_ctx, 16)
            sp.dma_start(ctx_in[0:K1, :, 1, :], ctx_seq[:, K0:KEYS, :].rearrange("b k d -> k b d")).then_inc(s_ctx, 16)
            for n, w in enumerate((Wq, Wk, Wv, Wo)):
                sp.dma_start(proj_raw[:, n, :], w).then_inc(s_wproj, 16)
            sp.dma_start(bk_sb[:, :], bk.rearrange("(p o) -> p o", o=1)).then_inc(s_wproj, 16)
            sp.dma_start(bv_row[:, :], bv.partition_broadcast(P)).then_inc(s_wproj, 16)
            sp.dma_start(wout_raw, Wout.rearrange("(h p) d -> p h d", p=P)).then_inc(s_wmix, 16)
            sp.dma_start(cp_sb[:, :], Cp).then_inc(s_wmix, 16)
            sp.dma_start(bp_sb[:, :, :], Bp.rearrange("(h p) n -> p h n", p=P)).then_inc(s_wmix, 16)
            sp.dma_start(dp_sb[:, :], Dp.rearrange("(h p) -> p h", p=P),
                         allow_slow_non_contiguous=True).then_inc(s_wmix, 16)
            sp.dma_start(rw_raw[:, :], router_w).then_inc(s_wmix, 16)
            sp.dma_start(bout_sb[:, :], bout.rearrange("(p o) -> p o", o=1)).then_inc(s_wsmall, 16)
            sp.dma_start(bq_sb[:, :], bq.rearrange("(p o) -> p o", o=1)).then_inc(s_wsmall, 16)
            sp.dma_start(bo_row[:, :], bo.partition_broadcast(P)).then_inc(s_wsmall, 16)
            sp.dma_start(rb_row[:, :], router_b.partition_broadcast(P)).then_inc(s_wsmall, 16)
            sp.dma_start(temp_sb[:, :], temperature.partition_broadcast(P)).then_inc(s_wsmall, 16)
            sp.dma_start(mask_sb, mask.rearrange("a c (t p) k -> p (a c t) k", p=P)).then_inc(s_mask, 16)
            sp.dma_start(res[:, 1, :, :], x[1].rearrange("(t p) d -> p t d", p=P)).then_inc(s_x[1], 16)

            for step, b, n in STEPS:
                if step == "load_experts":
                    for i in range(2, NB):
                        sp.dma_start(res[:, i, :, :], x[i].rearrange("(t p) d -> p t d", p=P)).then_inc(s_x[i], 16)
                    sp.dma_start(wgp_raw[:, 0, :, :], wg.rearrange("e d f -> d e f")).then_inc(s_wgp, 16)
                    sp.dma_start(wgp_raw[:, 1, :, :], wp.rearrange("e d f -> d e f")).then_inc(s_wgp, 16)
                elif step == "k_move":
                    if b > 0:
                        sp.wait_ge(s_kst, 16 * PARTS * PARTS * b)
                    sp.wait_ge(s_ksplit, 5 * b + 5)
                    sp.dma_start(k_scr, k_parts[:, :, :]).then_inc(s_kscr, 16)
                    sp.wait_ge(s_kscr, 16 * b + 16)
                    if b >= 2:
                        sp.wait_ge(s_sb, NSB * (b - 1))
                    sp.wait_ge(s_kones, 9)
                    for a in range(PARTS):
                        for p_ in range(PARTS):
                            r0 = (a * PARTS + p_) * DK
                            sp.dma_start(k_stack[b % 2][r0:r0 + DK, :, 0:KEYS],
                                         k_scr[:, p_, :].rearrange("(h d) n -> d h n", d=DK)).then_inc(s_kst, 16)
                elif step == "q_move":
                    if b > 0:
                        sp.wait_ge(s_qst, 16 * PARTS * PARTS * b)
                    sp.wait_ge(s_qsplit, 5 * b + 5)
                    sp.dma_start(q_scr, q_parts[:, :, :]).then_inc(s_qscr, 16)
                    sp.wait_ge(s_qscr, 16 * b + 16)
                    if b >= 2:
                        sp.wait_ge(s_sb, NSB * (b - 1))
                    for p_ in range(PARTS):
                        for a in range(PARTS):
                            r0 = (p_ * PARTS + a) * DK
                            sp.dma_start(q_stack[b % 2][r0:r0 + DK, :, :],
                                         q_scr[:, p_, :].rearrange("(h d) n -> d h n", d=DK)).then_inc(s_qst, 16)
            sp.wait_ge(s_pv, G * NB - 1)
            sp.dma_start(wo_sb[:, 0:WO_FIRST, :, :], wo[0:WO_FIRST].rearrange("e (h p) d -> p e h d", p=P)
                         ).then_inc(s_wo, 16)
            sp.wait_ge(s_pv, G * NB)
            sp.dma_start(wo_sb[:, WO_FIRST:E, :, :], wo[WO_FIRST:E].rearrange("e (h p) d -> p e h d", p=P)
                         ).then_inc(s_wo2, 16)
            for b in range(NB):
                sp.wait_ge(s_acc, AHEAD + T * E * (b + 1))
                sp.dma_start(out[b].rearrange("(t p) d -> p t d", p=P), res[:, b, :, :]).then_inc(s_out, 16)
            sp.wait_ge(s_out, 16 * NB)

        @block.gpsimd
        def _(pool):
            pool.memset(ident[:, :], 1.0).then_inc(s_ones, 1)
            pool.wait_ge(s_ones, 1)
            pool.affine_select(out=ident[:, :], in_=ident[:, :], compare_op=ALU.is_equal, fill=0.0, base=0,
                               pattern=[[-1, P]], channel_multiplier=1).then_inc(s_ident, 1)
            pool.memset(neghalf[:, :], -0.5).then_inc(s_nh, 1)
            pool.memset(f32(cR[0][:, :, :]), 0.0)
            pool.memset(f32(cR[1][:, :, :]), 0.0)
            pool.memset(v_rem[:, :, :, :, :], 0.0)
            pool.memset(v_main[:, :, :, :], 0.0).then_inc(s_zero, 1)
            pool.wait_ge(s_zero, 1)
            pool.wait_ge(s_nh, 1)

            for step, b, n in STEPS:
                if step == "ones":
                    ones = ([v_main[:, :, :, DK:DK + 1]]
                            + [v_rem[Q * j:Q * j + K1, :, :, j, DK:DK + 1] for j in range(4)]
                            + [stack[2 * Q:DEEP, :, 0:KEYS] for stack in k_stack])
                    zeros = [stack[:, :, KEYS:KPAD] for stack in k_stack]
                    done = 0
                    for value, places in ((1.0, ones), (0.0, zeros)):
                        for where in places:
                            pool.memset(where, value).then_inc(s_kones, 1)
                            done += 1
                            pool.wait_ge(s_kones, done)
                elif step == "split_experts":
                    pool.wait_ge(s_xsplit, n + 1)
                    w, e = divmod(n * EXPERT_STEP, E)
                    es = slice(e, e + EXPERT_STEP)
                    pool.tensor_tensor(wgp[1][:, w, es, :], wgp_raw[:, w, es, :], f32(wgp[0][:, w, es, :]),
                                       ALU.subtract).then_inc(s_wsplit, 1)
                elif step == "norm_scale":
                    pool.wait_ge(s_mv[n], T * (b + 1))
                    pool.tensor_scalar(ln[n]["veps"][:, :], ln[n]["mv"][:, :, 1], LN_EPS, None, ALU.add
                                       ).then_inc(s_veps[n], 1)
                    pool.wait_ge(s_veps[n], b + 1)
                    pool.tensor_tensor(ln[n]["rstd"][:, :], ln[n]["veps"][:, :], neghalf[:, :], ALU.pow
                                       ).then_inc(s_rstd[n], 1)
                    if n != "ffn":
                        pool.tensor_scalar(ln[n]["nmean"][:, :], ln[n]["mv"][:, :, 0], -1.0, None, ALU.mult
                                           ).then_inc(s_nmean[n], 1)
                        pool.wait_ge(s_rstd[n], b + 1)
                        pool.wait_ge(s_nmean[n], b + 1)
                        pool.tensor_tensor(ln[n]["shift"][:, :], ln[n]["nmean"][:, :], ln[n]["rstd"][:, :], ALU.mult
                                           ).then_inc(s_shift[n], 1)
                elif step == "xi_lo":
                    pool.wait_ge(s_xihi, HI * b + n + 1)
                    pool.tensor_tensor(xi[1][:, n, :], xi_f[:, n, :], f32(xi[0][:, n, :]), ALU.subtract
                                       ).then_inc(s_xilo, 1)
                elif step == "x1_bias":
                    pool.wait_ge(s_x1, b + 1)
                    pool.tensor_tensor(res[:, b, :, :], x1[:, :, :], bo_row[:, :].unsqueeze(1).broadcast_to([P, T, D]),
                                       ALU.add).then_inc(s_x1b, 1)
                elif step == "residual":
                    pool.wait_ge(s_xn["ffn"], T * (b + 1))
                    pool.tensor_tensor(res[:, b, :, :], x2[:, :, :], xn_post[:, :, :], ALU.add).then_inc(s_res, 1)

        @block.scalar
        def _(act):
            act.add_instruction(mybir.InstLoadActFuncSet(name=nc.get_next_instruction_name(), act_func_set_id=6,
                                                         ins=[], outs=[]))
            act.wait_ge(s_ident, 1)
            act.copy(ident_bf[:, :], ident[:, :]).then_inc(s_identb, 1)
            act.sem_inc(s_relu, AHEAD)

            def relu_of(b, i):
                N = E * HF
                act.wait_ge(s_gp, N * b + i + 1)
                act.wait_ge(s_hid, AHEAD + N * b + i - 1)
                act.activation(relu[:, i % 2, :], pGate[i % 2][:, :], ACT.Relu).then_inc(s_relu, 1)

            for step, b, n in STEPS:
                if step == "setup_win":
                    act.wait_ge(s_wwin, 32)
                    act.copy(win[0][:, :], win_raw).then_inc(s_winhi, 1)
                    act.mul(nbin[:, :], bin_sb[:, :], -1.0).then_inc(s_const, 1)
                elif step == "setup_proj":
                    act.wait_ge(s_projT, 1)
                    act.copy(proj[0][:, :, :], pG[:, :].rearrange("p (n d) -> p n d", n=4)).then_inc(s_projhi, 1)
                elif step == "setup_mix":
                    act.wait_ge(s_cpT, 1)
                    act.copy(rwT[0][:, :], pC[:, HI * STATE:HI * STATE + E]).then_inc(s_rwhi, 1)
                elif step == "setup_mask":
                    for n, dst in enumerate((mbiasT, mbiasT_rem)):
                        act.wait_ge(s_maskT, n + 1)
                        act.copy(dst[:, :], (pG_bf, pC_bf)[n][:, 0:S]).then_inc(s_maskTc, 1)
                elif step == "split_experts":
                    act.wait_ge(s_wgp, 32)
                    w, e = divmod(n * EXPERT_STEP, E)
                    es = slice(e, e + EXPERT_STEP)
                    act.copy(wgp[0][:, w, es, :], wgp_raw[:, w, es, :]).then_inc(s_xsplit, 1)
                elif step == "ctx_hi":
                    act.wait_ge(s_zero, 1)
                    act.wait_ge(s_ctxT, b + 1)
                    act.copy(cT[0][:, :], pT[:, 0:KEYS])
                    act.copy(cR[0][:, :, 0:K1], pT[:, K0:KEYS].unsqueeze(1).broadcast_to([P, 4, K1])
                             ).then_inc(s_chi, 1)
                elif step == "norm" and n != "ffn":
                    act.wait_ge(s_shift[n], b + 1)
                    if n == "att":
                        act.wait_ge(s_tT["mix"], b + 1 if b > 0 else 2)
                    elif b == 1:
                        act.wait_ge(s_tT["mix"], 1)
                    elif b > 1:
                        act.wait_ge(s_tT["att"], b)
                    src = x1[:, :, :] if n == "att" else res[:, b, :, :]
                    for t in range(T):
                        act.activation(xn[:, t, :], src[:, t, :], ACT.Identity, scale=ln[n]["rstd"][:, t:t + 1],
                                       bias=ln[n]["shift"][:, t:t + 1]).then_inc(s_xn[n], 1)
                elif step == "hi":
                    act.wait_ge(s_tT[n], b + 1)
                    if n == "ffn":
                        act.copy(x3[0][:, b, :], pG[:, :]).then_inc(s_hi[n], 1)
                    else:
                        act.copy(act_in[0][:, :], pT[:, :]).then_inc(s_hi[n], 1)
                elif step == "exp_neg":
                    act.wait_ge(s_win, HI * b + n + 1)
                    act.wait_ge(s_const, 1)
                    act.activation(sig[:, n, :], pAB[n][:, :], ACT.Exp, bias=nbin[:, n:n + 1], scale=-1.0
                                   ).then_inc(s_eneg, 1)
                elif step == "sigmoid":
                    act.wait_ge(s_eplus, HI * b + n + 1)
                    act.activation(sig[:, n, :], sig[:, n, :], ACT.Ln).then_inc(s_lnp, 1)
                    act.wait_ge(s_lnp, HI * b + n + 1)
                    act.activation(sig[:, n, :], sig[:, n, :], ACT.Exp, scale=-1.0).then_inc(s_sig, 1)
                elif step == "xi_hi":
                    act.wait_ge(s_xi, HI * b + n + 1)
                    act.copy(xi[0][:, n, :], xi_f[:, n, :]).then_inc(s_xihi, 1)
                elif step == "max_rows":
                    act.wait_ge(s_mTp, b + 1)
                    if b > 0:
                        act.wait_ge(s_mrow, 16 * PARTS * b)
                    act.copy(mT[:, :], pT_bf[0:PARTS * H, 0:S]).then_inc(s_mTc, 1)
                    act.wait_ge(s_mTc, b + 1)
                    for p_ in range(PARTS):
                        act.dma_start(q_stack[b % 2][MROW + p_:MROW + p_ + 1, :, :],
                                      mT[p_ * H:(p_ + 1) * H, :]).then_inc(s_mrow, 16)
                elif step == "scores":
                    act.wait_ge(s_sb, NSB * b + n + 1)
                    before = NSB * b + n - NBUF
                    if before >= 0:
                        act.wait_ge(s_pv, before // 5 + 1)
                    else:
                        act.wait_ge(s_wsplit, EXPERT_STEPS)
                    act.activation(prob[:, (NSB * b + n) % NBUF, :], score_bank(b, NSA + n)[:, :], ACT.Exp
                                   ).then_inc(s_exp, 1)
                elif step == "copy_group":
                    act.wait_ge(s_pv, G * b + n + 1)
                    if G * b + n >= 2:
                        act.wait_ge(s_ctxtr, G * b + n - 1)
                    act.copy(ctxg[:, n % 2, :], pC[:, :]).then_inc(s_ctxc, 1)
                elif step == "attn_hi":
                    act.wait_ge(s_cnT, b + 1)
                    act.copy(act_post[0][:, :], pG[:, :]).then_inc(s_cnhi, 1)

                elif step == "expert_up":
                    relu_of(b, n)
                elif step == "expert_exp":
                    act.wait_ge(s_tm, TM_PER * b + TM_STEPS * n + 2 + 1)
                    act.activation(route["exp"][:, b, :, :, :], route["diff"][:, b, :, :, :], ACT.Exp
                                   ).then_inc(s_tmexp, 1)
                elif step == "expert_ln":
                    act.wait_ge(s_tm, TM_PER * b + TM_STEPS * n + 3 + 1)
                    act.activation(rcol["lse"][:, b, :, :], rcol["sum"][:, b, :, :], ACT.Ln).then_inc(s_tmln, 1)
                elif step == "token_exp":
                    done = SINKHORN_ITERS * b + n
                    act.wait_ge(s_em, EM_PER * b + EM_STEPS * n + 1)
                    act.activation(eexp, pByExpert[b][0:GB * E, :], ACT.Exp, bias=ecol["nmax"][:, :],
                                   accum_out=ecol["sum"][:, :]).then_inc(s_emexp, 1)
                    act.wait_ge(s_emexp, done + 1)
                    act.activation(ecol["lse"][:, :], ecol["sum"][:, :], ACT.Ln).then_inc(s_emln, 1)
                elif step == "gate_exp":
                    act.wait_ge(s_toT, SINKHORN_ITERS * (b + 1))
                    act.activation(route["gate"][:, b, :, :, :], tokens_view(pByToken[b]), ACT.Exp
                                   ).then_inc(s_gexp, 1)

            N = E * HF
            with act.Fori(GB, NB) as b:
                for i in range(N):
                    relu_of(b, i)

        @block.vector
        def _(dve):
            dve.memset(decay[:, :], DECAY)
            dve.memset(seg[:, :], 1.0)
            dve.memset(mbias_rem[:, :, :, :], 0.0).then_inc(s_seg, 1)
            dve.wait_ge(s_seg, 1)
            dve.memset(seg[:, :].rearrange("p (t e) -> p t e", e=E)[:, :, 0:1], 0.0)

            def split3(src, parts, done, at, steps=range(4)):
                for n in steps:
                    dve.wait_ge(done, at + n)
                    if n in (0, 2):
                        last = dve.tensor_copy(parts(n // 2), src)
                    elif n == 1:
                        last = dve.tensor_tensor(src, src, parts(0), ALU.subtract)
                    else:
                        last = dve.tensor_tensor(parts(2), src, parts(1), ALU.subtract)
                    last.then_inc(done, 1)

            def normed(b, kind):
                return {"mix": res[:, b, :, :], "att": x1[:, :, :], "ffn": x2[:, :, :]}[kind]

            dve.sem_inc(s_hid, AHEAD)
            dve.sem_inc(s_acc, AHEAD)

            def hidden(b, i):
                done = E * HF * b + i
                dve.wait_ge(s_relu, AHEAD + done + 1)
                dve.wait_ge(s_up, done + 1)
                dve.wait_ge(s_down, AHEAD + done - 1)
                dve.tensor_tensor(hid[:, i % 2, :], relu[:, i % 2, :], pUp[i % 2][:, :], ALU.mult).then_inc(s_hid, 1)

            def gated_sum(b, e):
                if isinstance(b, int) and e == 0:
                    dve.wait_ge(s_res, b + 1)
                dve.wait_ge(s_down, AHEAD + E * HF * b + HF * (e + 1))
                if e > 0:
                    dve.wait_ge(s_acc, AHEAD + T * (E * b + e))
                for t in range(T):
                    row = res[:, at(b), t, :].rearrange("p o d -> p (o d)")
                    dve.scalar_tensor_tensor(out=row, in0=pO[:, t * D:(t + 1) * D], scalar=w_gate[:, t, at(b), e],
                                             in1=row, op0=ALU.mult, op1=ALU.add).then_inc(s_acc, 1)

            def wide(col):
                return col.unsqueeze(3).broadcast_to([P, T, GB, E])

            def gates(grp, part):
                def of(name):
                    return route[name][:, grp, :, :, :]

                def flat(name):
                    return of(name).rearrange("p t b e -> p (t b e)")

                def col(name):
                    return rcol[name][:, grp, :, :]

                def step(n, ins):
                    ins.then_inc(s_route, 1)
                    dve.wait_ge(s_route, ROUTE_STEPS * grp + n)

                if part == 0:
                    dve.wait_ge(s_gexp, grp + 1)
                    step(1, dve.tensor_reduce(col("sum"), of("gate"), AX.X, ALU.add))
                    step(2, dve.tensor_scalar(col("inv"), col("sum"), ROUTE_EPS, None, ALU.add))
                    step(3, dve.reciprocal(col("left"), col("inv")))
                    step(4, dve.tensor_tensor(of("norm"), of("gate"), wide(col("left")), ALU.mult))
                    for t in range(T):
                        for i in range(GB):
                            last = dve.max(top8[:, grp, t, i, :], route["norm"][:, grp, t, i, :])
                    step(5, last)
                elif part == 1:
                    second = top8[:, grp, :, :, 1:2].broadcast_to([P, T, GB, E])
                    dve.tensor_tensor(of("over"), of("norm"), second, ALU.is_gt)
                    dve.tensor_tensor(col("kept"), top8[:, grp, :, :, 0], top8[:, grp, :, :, 1], ALU.add)
                    step(6, dve.tensor_tensor(of("tie"), of("norm"), second, ALU.is_equal))
                    dve.tensor_reduce(col("left"), of("over"), AX.X, ALU.add)
                    dve.tensor_scalar(col("top"), col("kept"), ROUTE_EPS, None, ALU.add)
                    step(7, dve.tensor_tensor_scan(flat("rank"), seg[:, :], flat("tie"), 0.0, ALU.mult, ALU.add))
                    dve.reciprocal(col("kinv"), col("top"))
                    step(8, dve.tensor_tensor(of("log"), of("rank"), wide(col("left")), ALU.add))
                else:
                    step(9, dve.scalar_tensor_tensor(out=flat("pick"), in0=flat("log"), scalar=2.0,
                                                     in1=flat("tie"), op0=ALU.is_le, op1=ALU.mult))
                    step(10, dve.tensor_tensor(of("diff"), of("pick"), of("over"), ALU.add))
                    step(11, dve.tensor_tensor(of("w"), of("diff"), of("norm"), ALU.mult))
                    step(12, dve.tensor_tensor(w_gate[:, :, grp * GB:(grp + 1) * GB, :], of("w"), wide(col("kinv")),
                                               ALU.mult))

            for step, b, n in STEPS:
                if step == "setup_win":
                    dve.wait_ge(s_winhi, 1)
                    dve.tensor_tensor(win[1][:, :], win_raw, f32(win[0][:, :]), ALU.subtract).then_inc(s_winsplit, 1)
                elif step == "setup_proj":
                    dve.wait_ge(s_projhi, 1)
                    dve.tensor_tensor(proj[1][:, :, :], pG[:, :].rearrange("p (n d) -> p n d", n=4),
                                      f32(proj[0][:, :, :]), ALU.subtract).then_inc(s_proj, 1)
                elif step == "setup_mix":
                    dve.wait_ge(s_rwhi, 1)
                    dve.wait_ge(s_wmix, 16 * 5)
                    dve.tensor_tensor(rwT[1][:, :], pC[:, HI * STATE:HI * STATE + E], f32(rwT[0][:, :]),
                                      ALU.subtract)
                    dve.tensor_tensor(bcprod[:, :, :], bp_sb[:, :, :],
                                      pC[:, 0:HI * STATE].rearrange("p (h n) -> p h n", h=HI), ALU.mult
                                      ).then_inc(s_bc, 1)
                    dve.wait_ge(s_bc, 1)
                    dve.tensor_reduce(bc[:, :], bcprod[:, :, :], AX.X, ALU.add).then_inc(s_bc, 1)
                    for h in range(HI):
                        dve.tensor_scalar(wskip_f[:, h, :], wout_raw[:, h, :], dp_sb[:, h:h + 1], None, ALU.mult)
                    dve.wait_ge(s_bc, 2)
                    for h in range(HI):
                        last = dve.tensor_scalar(wscan_f[:, h, :], wout_raw[:, h, :], bc[:, h:h + 1], None, ALU.mult)
                    last.then_inc(s_bc, 1)
                    dve.wait_ge(s_bc, 3)
                    dve.tensor_copy(wskip[0][:, :, :], wskip_f)
                    dve.tensor_copy(wscan[0][:, :, :], wscan_f).then_inc(s_bc, 1)
                    dve.wait_ge(s_bc, 4)
                    dve.tensor_tensor(wskip[1][:, :, :], wskip_f, f32(wskip[0][:, :, :]), ALU.subtract)
                    dve.tensor_tensor(wscan[1][:, :, :], wscan_f, f32(wscan[0][:, :, :]), ALU.subtract
                                      ).then_inc(s_mixw, 1)
                elif step == "setup_mask":
                    dve.wait_ge(s_mask, 16)
                    dve.tensor_scalar(mbias[:, :, :], mask_sb, 0.0, MASKED, ALU.is_equal, ALU.mult)
                    for j in range(4):
                        last = dve.tensor_scalar(mbias_rem[:, :, j, 0:K1], mask_sb[:, :, K0:KEYS], 0.0, MASKED,
                                                 ALU.is_equal, ALU.mult)
                    last.then_inc(s_maskb, 1)
                    dve.wait_ge(s_wsmall, 16 * N_SMALL)
                    dve.tensor_scalar(temp_c[:, :], temp_sb[:, :], TEMP_MIN, None, ALU.max).then_inc(s_bc, 1)
                    dve.wait_ge(s_bc, 5)
                    dve.reciprocal(rtemp[:, :], temp_c[:, :])
                elif step == "ctx_lo":
                    dve.wait_ge(s_chi, b + 1)
                    dve.tensor_tensor(cT[1][:, :], pT[:, 0:KEYS], f32(cT[0][:, :]), ALU.subtract)
                    dve.tensor_tensor(cR[1][:, :, 0:K1], pT[:, K0:KEYS].unsqueeze(1).broadcast_to([P, 4, K1]),
                                      f32(cR[0][:, :, 0:K1]), ALU.subtract).then_inc(s_clo, 1)
                elif step == "k_split":
                    dve.wait_ge(s_vps, b + 1)
                    dve.wait_ge(s_wproj, 16 * 6)
                    if b > 0:
                        dve.wait_ge(s_kscr, 16 * b)
                    dve.tensor_scalar(k_f[:, :], pG[:, KCOL], bk_sb[:, 0:1], None, ALU.add).then_inc(s_ksplit, 1)
                    split3(k_f[:, :], lambda a: k_parts[:, a, :], s_ksplit, 5 * b + 1)
                elif step == "values":
                    dve.wait_ge(s_vps, b + 1)
                    dve.wait_ge(s_kones, 9)
                    if b >= 2:
                        dve.wait_ge(s_pv, G * (b - 1))
                    dve.tensor_tensor(v_main[:, b % 2, :, 0:DK], pG[:, VCOL].rearrange("p (h d) -> p h d", d=DK),
                                      bv_row[:, :].rearrange("p (h d) -> p h d", d=DK), ALU.add)
                    for j in range(4):
                        rows = slice(Q * j, Q * j + K1)
                        last = dve.tensor_tensor(
                            v_rem[rows, b % 2, :, j, 0:DK],
                            pG[rows, RCOL].rearrange("p (g j d) -> p g j d", g=G, j=4)[:, :, j, :],
                            bv_row[rows, :].rearrange("p (g j d) -> p g j d", g=G, j=4)[:, :, j, :], ALU.add)
                    last.then_inc(s_v, 1)
                elif step == "norm_stats":
                    if n == "mix":
                        dve.wait_ge(s_x[b], 16)
                    else:
                        dve.wait_ge(s_x1 if n == "att" else s_x2, b + 1)
                    for t in range(T):
                        dve.bn_stats(ln[n]["stats"][:, t, :], normed(b, n)[:, t, :]).then_inc(s_stat[n], 1)
                    for t in range(T):
                        dve.wait_ge(s_stat[n], T * b + t + 1)
                        dve.bn_aggr(ln[n]["mv"][:, t, :], ln[n]["stats"][:, t, :]).then_inc(s_mv[n], 1)
                elif step == "norm" and n == "ffn":
                    dve.wait_ge(s_rstd[n], b + 1)
                    for t in range(T):
                        dve.tensor_scalar(xn_post[:, t, :], x2[:, t, :], ln[n]["mv"][:, t, 0:1],
                                          ln[n]["rstd"][:, t:t + 1], ALU.subtract, ALU.mult).then_inc(s_xn[n], 1)
                elif step == "lo":
                    dve.wait_ge(s_hi[n], b + 1)
                    if n == "ffn":
                        dve.tensor_tensor(x3[1][:, b, :], pG[:, :], f32(x3[0][:, b, :]), ALU.subtract
                                          ).then_inc(s_lo[n], 1)
                    else:
                        dve.tensor_tensor(act_in[1][:, :], pT[:, :], f32(act_in[0][:, :]), ALU.subtract
                                          ).then_inc(s_lo[n], 1)
                elif step == "one_plus":
                    dve.wait_ge(s_eneg, HI * b + n + 1)
                    dve.tensor_scalar(sig[:, n, :], sig[:, n, :], 1.0, SIGMOID_MAX, ALU.add, ALU.min
                                      ).then_inc(s_eplus, 1)
                elif step == "xi":
                    dve.wait_ge(s_sig, HI * b + n + 1)
                    if b > 0:
                        dve.wait_ge(s_xilo, HI * b)
                    dve.scalar_tensor_tensor(out=xi_f[:, n, :], in0=pAB[n][:, :], scalar=bin_sb[:, n:n + 1],
                                             in1=sig[:, n, :], op0=ALU.add, op1=ALU.mult).then_inc(s_xi, 1)
                elif step == "scan":
                    dve.wait_ge(s_mix, 2 * b + 1)
                    dve.tensor_tensor_scan(mixT[:, :], decay[:, :], pA[:, :], 0.0, ALU.mult, ALU.add
                                           ).then_inc(s_scan, 1)
                    dve.wait_ge(s_scan, b + 1)
                    dve.wait_ge(s_mix, 2 * b + 2)
                    dve.wait_ge(s_wsmall, 16 * N_SMALL)
                    dve.scalar_tensor_tensor(out=mixT[:, :], in0=mixT[:, :], scalar=bout_sb[:, 0:1], in1=pB[:, :],
                                             op0=ALU.add, op1=ALU.add).then_inc(s_mixT, 1)
                elif step == "x1":
                    dve.wait_ge(s_mixtr, b + 1)
                    if b > 0:
                        dve.wait_ge(s_x1b, b)
                        dve.wait_ge(s_xn["att"], T * b)
                    dve.tensor_tensor(x1[:, :, :], res[:, b, :, :], pT[:, :].rearrange("p (t d) -> p t d", t=T),
                                      ALU.add).then_inc(s_x1, 1)
                elif step == "q_split":
                    if n == 0:
                        dve.wait_ge(s_qps, b + 1)
                        if b > 0:
                            dve.wait_ge(s_qscr, 16 * b)
                        dve.tensor_scalar(q_f[:, :], q_bank(b)[:, :], bq_sb[:, 0:1], QSCALE, ALU.add, ALU.mult
                                          ).then_inc(s_qsplit, 1)
                    else:
                        split3(q_f[:, :], lambda a: q_parts[:, a, :], s_qsplit, 5 * b + 1, steps=(n - 1,))
                elif step == "scores_max":
                    qt, hs = SA_UNITS[n]
                    dve.wait_ge(s_sa, NSA * b + n + 1)
                    dve.tensor_reduce(nmax[:, qt, hs[0]:hs[-1] + 1],
                                      score_bank(b, n)[:, 0:len(hs) * KEYS].rearrange("p (h k) -> p h k", k=KEYS),
                                      AX.X, ALU.max, negate=True).then_inc(s_red, 1)
                elif step == "max_split":
                    dve.wait_ge(s_red, NSA * (b + 1))
                    if b > 0:
                        dve.wait_ge(s_mTp, b)
                    dve.tensor_copy(m_parts[:, :, 0, :], nmax).then_inc(s_msplit, 1)
                    dve.wait_ge(s_msplit, 4 * b + 1)
                    dve.tensor_tensor(m_r[:, :, :], nmax, m_parts[:, :, 0, :], ALU.subtract
                                      ).then_inc(s_msplit, 1)
                    dve.wait_ge(s_msplit, 4 * b + 2)
                    dve.tensor_copy(m_parts[:, :, 1, :], m_r[:, :, :]).then_inc(s_msplit, 1)
                    dve.wait_ge(s_msplit, 4 * b + 3)
                    dve.tensor_tensor(m_parts[:, :, 2, :], m_r[:, :, :], m_parts[:, :, 1, :], ALU.subtract
                                      ).then_inc(s_msplit, 1)
                elif step == "attn_norm":
                    cols = pG[:, :].rearrange("p (t j v) -> p t j v", t=T, v=VC)
                    dve.wait_ge(s_ctxtr, G * b + n + 1)
                    dve.reciprocal(rz[:, n, :, :], cols[:, :, :, DK]).then_inc(s_rz, 1)
                    dve.wait_ge(s_rz, G * b + n + 1)
                    if b > 0:
                        dve.wait_ge(s_cnT, b)
                    dve.tensor_tensor(cn[:, :, 4 * n * DK:4 * (n + 1) * DK].rearrange("p t (j d) -> p t j d", d=DK),
                                      cols[:, :, :, 0:DK], rz[:, n, :, :].unsqueeze(3).broadcast_to([P, T, 4, DK]),
                                      ALU.mult).then_inc(s_cn, 1)
                elif step == "attn_lo":
                    dve.wait_ge(s_cnhi, b + 1)
                    dve.tensor_tensor(act_post[1][:, :], pG[:, :], f32(act_post[0][:, :]), ALU.subtract
                                      ).then_inc(s_cnlo, 1)
                elif step == "x2":
                    dve.wait_ge(s_yo, b + 1)
                    dve.wait_ge(s_x1b, b + 1)
                    if b > 0:
                        dve.wait_ge(s_res, b)
                    dve.tensor_tensor(x2[:, :, :], res[:, b, :, :], pC[:, :].rearrange("p (t d) -> p t d", t=T),
                                      ALU.add).then_inc(s_x2, 1)

                elif step == "expert_down":
                    hidden(b, n)
                    if n >= HF and n % HF == 0:
                        gated_sum(b, n // HF - 1)
                    elif n == E * HF - 1:
                        gated_sum(b, E - 1)
                elif step == "logits":
                    dve.wait_ge(s_rps, b + 1)
                    dve.tensor_tensor(logit[:, b, :, :, :], tokens_view(pLogit[b]),
                                      rb_row[:, :].unsqueeze(1).unsqueeze(1).broadcast_to([P, T, GB, E]), ALU.add
                                      ).then_inc(s_logit, 1)
                    dve.wait_ge(s_logit, b + 1)
                    dve.tensor_scalar(route["norm"][:, b, :, :, :], logit[:, b, :, :, :], rtemp[:, 0:1], None,
                                      ALU.mult).then_inc(s_tm, 1)
                elif step == "expert_max":
                    done = TM_PER * b + TM_STEPS * n + 1
                    if n == 0:
                        src = route["norm"][:, b, :, :, :]
                        dve.wait_ge(s_tm, done)
                    else:
                        src = tokens_view(pByToken[b])
                        dve.wait_ge(s_toT, SINKHORN_ITERS * b + n)
                    dve.tensor_reduce(rcol["max"][:, b, :, :], src, AX.X, ALU.max).then_inc(s_tm, 1)
                    dve.wait_ge(s_tm, done + 1)
                    dve.tensor_tensor(route["diff"][:, b, :, :, :], src, wide(rcol["max"][:, b, :, :]), ALU.subtract
                                      ).then_inc(s_tm, 1)
                elif step == "expert_sum":
                    dve.wait_ge(s_tmexp, SINKHORN_ITERS * b + n + 1)
                    dve.tensor_reduce(rcol["sum"][:, b, :, :], route["exp"][:, b, :, :, :], AX.X, ALU.add
                                      ).then_inc(s_tm, 1)
                elif step == "expert_log":
                    dve.wait_ge(s_tmln, SINKHORN_ITERS * b + n + 1)
                    dve.tensor_tensor(route["log"][:, b, :, :, :], route["diff"][:, b, :, :, :],
                                      wide(rcol["lse"][:, b, :, :]), ALU.subtract).then_inc(s_tm, 1)
                elif step == "token_max":
                    dve.wait_ge(s_toE, SINKHORN_ITERS * b + n + 1)
                    dve.tensor_reduce(ecol["nmax"][:, :], pByExpert[b][0:GB * E, :], AX.X, ALU.max, negate=True
                                      ).then_inc(s_em, 1)
                elif step == "token_log":
                    done = EM_PER * b + EM_STEPS * n
                    dve.wait_ge(s_em, done + 1)
                    dve.wait_ge(s_emln, SINKHORN_ITERS * b + n + 1)
                    dve.tensor_tensor(ecol["shift"][:, :], ecol["nmax"][:, :], ecol["lse"][:, :], ALU.subtract
                                      ).then_inc(s_em, 1)
                    dve.wait_ge(s_em, done + 2)
                    dve.tensor_scalar(elog, pByExpert[b][0:GB * E, :], ecol["shift"][:, 0:1], None, ALU.add
                                      ).then_inc(s_em, 1)
                elif step == "gates":
                    gates(b, n)

            dve.wait_ge(s_res, NB)
            with dve.Fori(GB, NB) as b:
                for i in range(E * HF):
                    hidden(b, i)
                    if i >= HF and i % HF == 0:
                        gated_sum(b, i // HF - 1)
                gated_sum(b, E - 1)

        @block.tensor
        def _(pe):
            pe.wait_ge(s_ident, 1)

            def transposes(dst, src):
                for t in range(T):
                    last = pe.transpose(dst[:, t * P:(t + 1) * P], src(t), ident[:, :])
                return last

            def bank_free(b, k):
                before = (NSA + NSB) * b + k - len(pS)
                if before >= 0:
                    row, k = divmod(before, NSA + NSB)
                    if k < NSA:
                        pe.wait_ge(s_red, NSA * row + k + 1)
                    else:
                        pe.wait_ge(s_exp, NSB * row + k - NSA + 1)

            pe.sem_inc(s_down, AHEAD)

            def up(b, i):
                N = E * HF
                e, hf = divmod(i, HF)
                cols = slice(hf * P, (hf + 1) * P)
                x3_b = [half[:, at(b), :].rearrange("p o n -> p (o n)") for half in x3]
                pe.wait_ge(s_relu, AHEAD + N * b + i - 1)
                three_pass(pe, pGate[i % 2][:, :], wgp[0][:, 0, e, cols], wgp[1][:, 0, e, cols], x3_b[0], x3_b[1]
                           ).then_inc(s_gp, 1)
                pe.wait_ge(s_hid, AHEAD + N * b + i - 1)
                three_pass(pe, pUp[i % 2][:, :], wgp[0][:, 1, e, cols], wgp[1][:, 1, e, cols], x3_b[0], x3_b[1]
                           ).then_inc(s_up, 1)

            def down(b, i):
                N = E * HF
                e, hf = divmod(i, HF)
                pe.wait_ge(s_hid, AHEAD + N * b + i + 1)
                if hf == 0:
                    pe.wait_ge(s_acc, AHEAD + T * (E * b + e))
                for t in range(T):
                    toks = slice(t * P, (t + 1) * P)
                    last = pe.matmul(pO[:, toks], hid[:, i % 2, toks], wo_sb[:, e, hf, :],
                                     start=(hf == 0 and t == 0), stop=(hf == HF - 1), skip_group_check=True)
                last.then_inc(s_down, 1)

            for step, b, n in STEPS:
                if step == "setup_proj":
                    pe.wait_ge(s_wproj, 16 * 6)
                    for n in range(4):
                        last = pe.transpose(pG[:, n * D:(n + 1) * D], proj_raw[:, n, :], ident[:, :])
                    last.then_inc(s_projT, 1)
                elif step == "setup_mix":
                    pe.wait_ge(s_wmix, 16 * 5)
                    for h in range(HI):
                        pe.transpose(pC[:, h * STATE:(h + 1) * STATE], cp_sb[:, h * P:(h + 1) * P],
                                     ident[0:STATE, 0:STATE])
                    pe.transpose(pC[:, HI * STATE:HI * STATE + E], rw_raw[:, :], ident[0:E, 0:E]).then_inc(s_cpT, 1)
                elif step == "setup_mask":
                    pe.wait_ge(s_identb, 1)
                    pe.wait_ge(s_maskb, 1)
                    pe.wait_ge(s_v, 1)
                    pe.wait_ge(s_bc, 1)
                    for t in range(T):
                        last = pe.transpose(pG_bf[:, t * P:(t + 1) * P], mbias[:, t, 0:K0], ident_bf[:, :])
                    last.then_inc(s_maskT, 1)
                    for t in range(T):
                        last = pe.transpose(pC_bf[:, t * P:(t + 1) * P],
                                            mbias_rem[:, t, :, :].rearrange("p j k -> p (j k)"), ident_bf[:, :])
                    last.then_inc(s_maskT, 1)
                elif step == "ctx_T":
                    pe.wait_ge(s_ctx, 32)
                    if b == 0:
                        pe.wait_ge(s_lo["mix"], 1)
                    elif b + 1 < NB:
                        pe.wait_ge(s_lo["mix"], b + 2)
                    else:
                        pe.wait_ge(s_lo["att"], b + 1)
                    pe.transpose(pT[:, 0:K0], ctx_in[:, b, 0, :], ident[:, :])
                    pe.transpose(pT[:, K0:KEYS], ctx_in[0:K1, b, 1, :], ident[0:K1, 0:K1]).then_inc(s_ctxT, 1)
                elif step == "kv_product":
                    pe.wait_ge(s_chi, b + 1)
                    pe.wait_ge(s_clo, b + 1)
                    if b == 0:
                        pe.wait_ge(s_proj, 1)
                    elif b == 1:
                        pe.wait_ge(s_maskTc, 2)
                    else:
                        pe.wait_ge(s_cnlo, b - 1)
                    three_pass(pe, pG[:, KCOL], proj[0][:, 1, :], proj[1][:, 1, :], cT[0][:, :], cT[1][:, :])
                    three_pass(pe, pG[:, VCOL], cT[0][:, 0:K0], cT[1][:, 0:K0], proj[0][:, 2, :], proj[1][:, 2, :],
                               start=False)
                    flat = [c[:, :, :].rearrange("p j k -> p (j k)") for c in cR]
                    three_pass(pe, pG[:, RCOL], flat[0], flat[1], proj[0][:, 2, :], proj[1][:, 2, :],
                               start=False).then_inc(s_vps, 1)
                elif step == "norm_T":
                    pe.wait_ge(s_xn[n], T * (b + 1))
                    if n == "ffn":
                        pe.wait_ge(s_cnlo, b + 1)
                        if b + 2 < NB:
                            pe.wait_ge(s_v, b + 3)
                        transposes(pG, lambda t: xn_post[:, t, :]).then_inc(s_tT[n], 1)
                    else:
                        if n == "mix" and b == 1:
                            pe.wait_ge(s_x1, 1)
                        elif n == "mix" and b > 1:
                            pe.wait_ge(s_lo["att"], b)
                        elif n == "att":
                            pe.wait_ge(s_x1, b + 1)
                            pe.wait_ge(s_lo["mix"], b + 1 if b > 0 else 2)
                        transposes(pT, lambda t: xn[:, t, :]).then_inc(s_tT[n], 1)
                elif step == "win":
                    pe.wait_ge(s_hi["mix"], b + 1)
                    pe.wait_ge(s_lo["mix"], b + 1)
                    pe.wait_ge(s_winsplit, 1)
                    if b > 0:
                        pe.wait_ge(s_mixT, b)
                    if b > 1:
                        pe.wait_ge(s_qsplit, 5 * b - 4)
                    for h in range(HI):
                        cols = slice(h * P, (h + 1) * P)
                        three_pass(pe, pAB[h][:, :], win[0][:, cols], win[1][:, cols], act_in[0][:, :],
                                   act_in[1][:, :]).then_inc(s_win, 1)
                elif step == "mix_product":
                    pe.wait_ge(s_mixw, 1)
                    w, dst = ((wscan, pA), (wskip, pB))[n]
                    for h in range(HI):
                        pe.wait_ge(s_xihi, HI * b + HI)
                        pe.wait_ge(s_xilo, HI * b + h + 1)
                        last = three_pass(pe, dst[:, :], w[0][:, h, :], w[1][:, h, :], xi[0][:, h, :],
                                          xi[1][:, h, :], start=(h == 0), stop=(h == HI - 1))
                    last.then_inc(s_mix, 1)
                elif step == "mix_T":
                    pe.wait_ge(s_mixT, b + 1)
                    pe.wait_ge(s_clo, max(b, 1))
                    if b >= 2:
                        pe.wait_ge(s_mTc, b - 1)
                    transposes(pT, lambda t: mixT[:, t * P:(t + 1) * P]).then_inc(s_mixtr, 1)
                elif step == "q_product":
                    pe.wait_ge(s_hi["att"], b + 1)
                    pe.wait_ge(s_lo["att"], b + 1)
                    three_pass(pe, q_bank(b)[:, :], proj[0][:, 0, :], proj[1][:, 0, :], act_in[0][:, :],
                               act_in[1][:, :]).then_inc(s_qps, 1)
                elif step == "scores_max":
                    qt, hs = SA_UNITS[n]
                    if n == 0:
                        pe.wait_ge(s_maskTc, 2)
                        pe.wait_ge(s_kst, 16 * PARTS * PARTS * (b + 1))
                        pe.wait_ge(s_qst, 16 * PARTS * PARTS * (b + 1))
                    bank_free(b, n)
                    dst = score_bank(b, n)
                    for i, h in enumerate(hs):
                        pe.matmul(dst[:, i * KEYS:(i + 1) * KEYS], q_stack[b % 2][0:STACK, h, qt * P:(qt + 1) * P],
                                  k_stack[b % 2][0:STACK, h, 0:KEYS], start=(i == 0), stop=False,
                                  skip_group_check=True)
                    pe.matmul(dst[:, 0:len(hs) * KEYS].rearrange("p (h k) -> p h k", k=KEYS), ident_bf[:, :],
                              mbias[:, qt, :].unsqueeze(1).broadcast_to([P, len(hs), KEYS]),
                              start=False, stop=True, skip_group_check=True).then_inc(s_sa, 1)
                elif step == "max_T":
                    pe.wait_ge(s_msplit, 4 * b + 4)
                    pe.wait_ge(s_clo, min(b + 2, NB))
                    for t in range(T):
                        last = pe.transpose(pT_bf[0:PARTS * H, t * P:(t + 1) * P],
                                            m_parts[:, t, :, :].rearrange("p a h -> p (a h)"), ident_bf[:, :])
                    last.then_inc(s_mTp, 1)
                elif step == "scores":
                    g, j = SB_UNITS[n]
                    if n == 0:
                        pe.wait_ge(s_mrow, 16 * PARTS * (b + 1))
                    bank_free(b, NSA + n)
                    dst = score_bank(b, NSA + n)
                    if j is None:
                        for c in range(4):
                            pe.matmul(dst[Q * c:Q * (c + 1), :], k_stack[b % 2][:, 4 * g + c, K0:KPAD],
                                      q_stack[b % 2][:, 4 * g + c, :], start=True, stop=False, skip_group_check=True)
                        bias = mbiasT_rem
                    else:
                        pe.matmul(dst[:, :], k_stack[b % 2][:, 4 * g + j, 0:K0], q_stack[b % 2][:, 4 * g + j, :],
                                  start=True, stop=False, skip_group_check=True)
                        bias = mbiasT
                    pe.matmul(dst[:, :], ident_bf[:, :], bias[:, :], start=False, stop=True, skip_group_check=True
                              ).then_inc(s_sb, 1)
                elif step == "weigh":
                    pe.wait_ge(s_exp, NSB * b + 5 * n + 5)
                    pe.wait_ge(s_v, b + 1)
                    if n > 0:
                        pe.wait_ge(s_ctxc, G * b + n)
                    elif b > 0:
                        pe.wait_ge(s_x2, b)
                    u0 = NSB * b + 5 * n
                    pe.matmul(pC[:, :], v_rem[:, b % 2, n, :, :].rearrange("p j v -> p (j v)"),
                              prob[:, u0 % NBUF, :], start=True, stop=False, skip_group_check=True)
                    for j in range(4):
                        last = pe.matmul(pC[Q * j:Q * (j + 1), :], v_main[:, b % 2, 4 * n + j, :],
                                         prob[:, (u0 + 1 + j) % NBUF, :], start=False, stop=True,
                                         skip_group_check=True)
                    last.then_inc(s_pv, 1)
                elif step == "by_token":
                    pe.wait_ge(s_ctxc, G * b + n + 1)
                    if n > 0:
                        pe.wait_ge(s_cn, G * b + n)
                    elif b > 0:
                        pe.wait_ge(s_lo["ffn"], b)
                    else:
                        pe.wait_ge(s_v, 2)
                    transposes(pG, lambda t: ctxg[:, n % 2, t * P:(t + 1) * P]).then_inc(s_ctxtr, 1)
                elif step == "attn_T":
                    pe.wait_ge(s_cn, G * (b + 1))
                    transposes(pG, lambda t: cn[:, t, :]).then_inc(s_cnT, 1)
                elif step == "out_product":
                    pe.wait_ge(s_cnhi, b + 1)
                    pe.wait_ge(s_cnlo, b + 1)
                    pe.wait_ge(s_ctxc, G * (b + 1))
                    for t in range(T):
                        toks = slice(t * P, (t + 1) * P)
                        last = three_pass(pe, pC[:, toks], act_post[0][:, toks], act_post[1][:, toks],
                                          proj[0][:, 3, :], proj[1][:, 3, :], start=(t == 0))
                    last.then_inc(s_yo, 1)

                elif step == "logits":
                    pe.wait_ge(s_hi["ffn"], GB * (b + 1))
                    pe.wait_ge(s_lo["ffn"], GB * (b + 1))
                    if b == 0:
                        pe.wait_ge(s_ksplit, 5 * NB)
                        pe.wait_ge(s_v, NB)
                        pe.wait_ge(s_clo, NB)
                    for t in range(T):
                        for i in range(GB):
                            toks = [half[:, GB * b + i, t * P:(t + 1) * P] for half in x3]
                            c0 = (t * GB + i) * E
                            last = three_pass(pe, pLogit[b][:, c0:c0 + E], toks[0], toks[1], rwT[0][:, :],
                                              rwT[1][:, :], start=(c0 == 0))
                    last.then_inc(s_rps, 1)
                elif step == "to_experts":
                    pe.wait_ge(s_tm, TM_PER * b + TM_STEPS * (n + 1) + 1)
                    for t in range(T):
                        last = pe.transpose(pByExpert[b][0:GB * E, t * P:(t + 1) * P],
                                            route["log"][:, b, t, :, :].rearrange("p b e -> p (b e)"), ident[:, :])
                    last.then_inc(s_toE, 1)
                elif step == "to_tokens":
                    pe.wait_ge(s_em, EM_PER * b + EM_STEPS * (n + 1))
                    for t in range(T):
                        last = pe.transpose(pByToken[b][:, t * GB * E:(t + 1) * GB * E], elog[:, t * P:(t + 1) * P],
                                            ident[0:GB * E, 0:GB * E])
                    last.then_inc(s_toT, 1)
                elif step == "expert_up":
                    if (b, n) == (0, 0):
                        pe.wait_ge(s_wsplit, EXPERT_STEPS)
                        pe.wait_ge(s_exp, NSB * NB)
                        pe.wait_ge(s_toT, SINKHORN_ITERS)
                    up(b, n)
                elif step == "expert_down":
                    if (b, n) == (0, 0):
                        pe.wait_ge(s_wo, 16)
                        pe.wait_ge(s_wo2, 16)
                    down(b, n)

            pe.wait_ge(s_route, ROUTE_STEPS * GROUPS)
            N = E * HF
            with pe.Fori(GB, NB) as b:
                up(b, 0)
                for i in range(N):
                    if i + 1 < N:
                        up(b, i + 1)
                    down(b, i)


_INS = ["x", "ctx_1024", "mask_1x1xSxS2_if1", "L0_attn_Win", "L0_attn_bin_", "L0_attn_Bp", "L0_attn_Cp", "L0_attn_Dp",
        "L0_attn_Wout", "L0_attn_bout", "L0_xattn_Wq", "L0_xattn_bq", "L0_xattn_Wk", "L0_xattn_bk", "L0_xattn_Wv",
        "L0_xattn_bv", "L0_xattn_Wo", "L0_xattn_bo", "L0_ffn_router_w", "L0_ffn_router_b", "L0_ffn_temperature",
        "L0_ffn_wg", "L0_ffn_wp", "L0_ffn_wo"]
_OUTS = [((4, 512, 128), "float32")]


def kernel(**inputs):
    import numpy as _np
    import concourse.bacc as _bacc
    from concourse import mybir as _mybir
    from concourse.bass_utils import run_bass_kernel_spmd as _run

    nc = _bacc.Bacc("TRN2", target_bir_lowering=False, num_devices=1)
    arrays, args = {}, []
    for name in _INS:
        a = _np.ascontiguousarray(inputs[name])
        arrays[f"in_{name}_dram"] = a
        args.append(nc.dram_tensor(f"in_{name}_dram", a.shape, _mybir.dt.from_np(a.dtype), kind="ExternalInput").ap())
    for i, (shape, dtype) in enumerate(_OUTS):
        dt = _mybir.dt.from_np(_np.dtype(dtype))
        args.append(nc.dram_tensor(f"out_{i}_dram", shape, dt, kind="ExternalOutput").ap())
    build_decoder(nc, *args)
    r = _run(nc, [arrays], core_ids=[0])
    got = tuple(r.results[0][f"out_{i}_dram"] for i in range(len(_OUTS)))
    return got[0]
```
